# Optimizing a Trainium2 kernel written in Bass

```python
import numpy as np
import jax
import jax.numpy as jnp

def _softmax(x, axis=-1):
    return jax.nn.softmax(x, axis=axis)

def _gelu(x):
    return jax.nn.gelu(x, approximate=True)

def _silu(x):
    return jax.nn.silu(x)

def _sigmoid(x):
    return jax.nn.sigmoid(x)

def _layernorm(x, axis=-1, eps=1e-05):
    m = jnp.mean(x, axis=axis, keepdims=True)
    v = jnp.var(x, axis=axis, keepdims=True)
    return (x - m) / jnp.sqrt(v + eps)

def _scatter_add(tgt, idx, src, axis=0):
    return tgt.at[idx].add(src)

def _segment_sum(src, seg, n):
    return jax.ops.segment_sum(src, seg, n)
kernel_name = 'mk_flamingo_gated_d2_seqx_r8_d053f9'

def setup_inputs(seed: int=0):
    np.random.seed(seed)
    _w = jnp.asarray

    def _rec_inputs():
        import jax
        import jax.numpy as jnp
        _rk = jax.random.key(seed)
        x = 0.001912 + 0.9994 * jax.random.normal(jax.random.fold_in(_rk, 1), (2, 512, 128), jnp.float32)
        _lenS = 512 - jax.random.randint(jax.random.fold_in(_rk, 7), (2,), 0, max(1, 512 // 4) + 1, jnp.int32)
        _lenS2 = 77 - jax.random.randint(jax.random.fold_in(_rk, 8), (2,), 0, max(1, 77 // 4) + 1, jnp.int32)
        _ctx_1024P = jax.random.normal(jax.random.fold_in(_rk, 11), (2, 16, 128), jnp.float32)
        _ctx_1024c = jax.random.dirichlet(jax.random.fold_in(_rk, 511), 0.3 * jnp.ones((16,), jnp.float32), (2, 77))
        _ctx_1024t = jnp.einsum('bsk,bkd->bsd', _ctx_1024c, _ctx_1024P)
        _ctx_1024t = _ctx_1024t * jax.lax.rsqrt(jnp.mean(jnp.square(_ctx_1024t)) + 1e-12) * 0.953939
        ctx_1024 = -0.000125008 + 0.999885 * (_ctx_1024t + 0.3 * jax.random.normal(jax.random.fold_in(_rk, 611), (2, 77, 128), jnp.float32))
        _g = jax.random.normal(jax.random.fold_in(_rk, 9001), (2, 2), jnp.float32)
        _g = jnp.sign(_g) * jnp.maximum(jnp.abs(_g), 1.0) + (_g == 0) * 1.0
        g_xattn = _g[0]
        g_ffn = _g[1]
        return (x, ctx_1024, g_xattn, g_ffn)
    x, ctx_1024, g_xattn, g_ffn = _rec_inputs()

    def _L0_xattn_setup():
        import jax, jax.numpy as jnp
        import numpy as np
        D_MODEL = 128
        D_HEAD = 64
        NHEADS = 8
        IN_DIM = D_HEAD * NHEADS
        EPS = 1e-05

        def layernorm(x, g, b):
            mu = jnp.mean(x, axis=-1, keepdims=True)
            var = jnp.var(x, axis=-1, keepdims=True)
            return (x - mu) * jax.lax.rsqrt(var + EPS) * g + b
        key = jax.random.key(seed)
        ks = jax.random.split(key, 8)
        B, M, L = (4, 1024, 64)
        x = jax.random.normal(ks[0], (B, M, D_MODEL), dtype=jnp.float32)
        latents = jax.random.normal(ks[1], (B, L, D_MODEL), dtype=jnp.float32)
        s = 1.0 / np.sqrt(D_MODEL)
        Wq = jax.random.normal(ks[2], (D_MODEL, IN_DIM), dtype=jnp.float32) * s
        Wkv = jax.random.normal(ks[3], (D_MODEL, 2 * IN_DIM), dtype=jnp.float32) * s
        Wout = jax.random.normal(ks[4], (IN_DIM, D_MODEL), dtype=jnp.float32) * (1.0 / np.sqrt(IN_DIM))
        gm = jnp.ones((D_MODEL,), jnp.float32)
        bm = jnp.zeros((D_MODEL,), jnp.float32)
        gl = jnp.ones((D_MODEL,), jnp.float32)
        bl = jnp.zeros((D_MODEL,), jnp.float32)
        return {'x': x, 'latents': latents, 'Wq': Wq, 'Wkv': Wkv, 'Wout': Wout, 'gm': gm, 'bm': bm, 'gl': gl, 'bl': bl}
    _L0_xattn_all = _L0_xattn_setup()
    _L0_xattn_in = {k: v for k, v in _L0_xattn_all.items() if k in ('Wq', 'Wkv', 'Wout', 'gm', 'bm', 'gl', 'bl')}
    del _L0_xattn_all

    def _L0_ffn_setup():
        import jax, jax.numpy as jnp
        import numpy as np
        B, S, D_MODEL, D_HIDDEN = (4, 256, 128, 512)

        def act_quant(x):
            scale = 127.0 / jnp.clip(jnp.max(jnp.abs(x), axis=-1, keepdims=True), 1e-05)
            return jnp.clip(jnp.round(x * scale), -128, 127) / scale

        def weight_quant(w):
            scale = 1.0 / jnp.clip(jnp.mean(jnp.abs(w)), 1e-05)
            return jnp.clip(jnp.round(w * scale), -1, 1) / scale

        def bit_linear(x, w):
            xq = x + jax.lax.stop_gradient(act_quant(x) - x)
            wq = w + jax.lax.stop_gradient(weight_quant(w) - w)
            return jnp.einsum('bsd,hd->bsh', xq, wq)

        def depthwise_conv1d(x_bcl, w, b):
            y = jax.lax.conv_general_dilated(x_bcl, w, window_strides=(1,), padding=[(1, 1)], dimension_numbers=('NCH', 'OIH', 'NCH'), feature_group_count=x_bcl.shape[1])
            return y + b[None, :, None]
        key = jax.random.key(seed)
        ks = jax.random.split(key, 5)
        lim1 = 1.0 / np.sqrt(D_MODEL)
        lim2 = 1.0 / np.sqrt(D_HIDDEN)
        limc = 1.0 / np.sqrt(3.0)
        return {'x': jax.random.normal(ks[0], (B, S, D_MODEL), dtype=jnp.float32), 'w1': jax.random.uniform(ks[1], (D_HIDDEN, D_MODEL), jnp.float32, -lim1, lim1), 'conv_w': jax.random.uniform(ks[2], (D_HIDDEN, 1, 3), jnp.float32, -limc, limc), 'conv_b': jax.random.uniform(ks[3], (D_HIDDEN,), jnp.float32, -limc, limc), 'w2': jax.random.uniform(ks[4], (D_MODEL, D_HIDDEN), jnp.float32, -lim2, lim2)}
    _L0_ffn_all = _L0_ffn_setup()
    _L0_ffn_in = {k: v for k, v in _L0_ffn_all.items() if k in ('w1', 'conv_w', 'conv_b', 'w2')}
    del _L0_ffn_all

    def _L1_xattn_setup():
        import jax, jax.numpy as jnp
        import numpy as np
        DIM = 128
        N_HEADS = 16
        HEAD_DIM = DIM // N_HEADS
        GAMMA = 10.0

        def larope_cos_sin(seq_len, gamma, head_dim):
            inv_freq = 1.0 / 10000.0 ** (jnp.arange(0, head_dim, 2, dtype=jnp.float32) / head_dim)
            t = jnp.arange(seq_len, dtype=jnp.float32)
            freqs = jnp.outer(gamma * (t / seq_len), inv_freq)
            emb = jnp.concatenate([freqs, freqs], axis=-1)
            return (jnp.cos(emb), jnp.sin(emb))

        def apply_rope(x, cos, sin):
            d = x.shape[-1] // 2
            x1, x2 = (x[..., :d], x[..., d:])
            c = cos[None, None, :, :d]
            s = sin[None, None, :, :d]
            return jnp.concatenate([x1 * c - x2 * s, x1 * s + x2 * c], axis=-1)
        key = jax.random.key(seed)
        ks = jax.random.split(key, 11)
        B, Lq, Lk = (4, 256, 128)
        std = 1.0 / np.sqrt(DIM)
        inp = {'query': jax.random.normal(ks[0], (B, Lq, DIM), dtype=jnp.float32), 'key': jax.random.normal(ks[1], (B, Lk, DIM), dtype=jnp.float32), 'value': jax.random.normal(ks[2], (B, Lk, DIM), dtype=jnp.float32), 'Wq': jax.random.normal(ks[3], (DIM, DIM), dtype=jnp.float32) * std, 'bq': jnp.zeros((DIM,), dtype=jnp.float32), 'Wk': jax.random.normal(ks[4], (DIM, DIM), dtype=jnp.float32) * std, 'bk': jnp.zeros((DIM,), dtype=jnp.float32), 'Wv': jax.random.normal(ks[5], (DIM, DIM), dtype=jnp.float32) * std, 'bv': jnp.zeros((DIM,), dtype=jnp.float32), 'Wo': jax.random.normal(ks[6], (DIM, DIM), dtype=jnp.float32) * std, 'bo': jnp.zeros((DIM,), dtype=jnp.float32)}
        return inp
    _L1_xattn_all = _L1_xattn_setup()
    _L1_xattn_in = {k: v for k, v in _L1_xattn_all.items() if k in ('Wq', 'bq', 'Wk', 'bk', 'Wv', 'bv', 'Wo', 'bo')}
    del _L1_xattn_all

    def _L1_ffn_setup():
        import jax, jax.numpy as jnp
        import numpy as np
        DIM = 128
        INTER = 64
        E = 8
        TOP_K = 2
        ROUTE_SCALE = 1.0
        key = jax.random.key(seed)
        ks = jax.random.split(key, 8)
        s_d = 1.0 / np.sqrt(DIM)
        s_f = 1.0 / np.sqrt(INTER)
        x = jax.random.normal(ks[0], (2, 256, DIM), dtype=jnp.float32)
        gate_w = jax.random.uniform(ks[1], (E, DIM), jnp.float32, -s_d, s_d)
        wg = jax.random.uniform(ks[2], (E, INTER, DIM), jnp.float32, -s_d, s_d)
        wu = jax.random.uniform(ks[3], (E, INTER, DIM), jnp.float32, -s_d, s_d)
        wd = jax.random.uniform(ks[4], (E, DIM, INTER), jnp.float32, -s_f, s_f)
        sg = jax.random.uniform(ks[5], (INTER, DIM), jnp.float32, -s_d, s_d)
        su = jax.random.uniform(ks[6], (INTER, DIM), jnp.float32, -s_d, s_d)
        sd = jax.random.uniform(ks[7], (DIM, INTER), jnp.float32, -s_f, s_f)
        return {'x': x, 'gate_w': gate_w, 'wg': wg, 'wu': wu, 'wd': wd, 'sg': sg, 'su': su, 'sd': sd}
    _L1_ffn_all = _L1_ffn_setup()
    _L1_ffn_in = {k: v for k, v in _L1_ffn_all.items() if k in ('gate_w', 'wg', 'wu', 'wd', 'sg', 'su', 'sd')}
    del _L1_ffn_all
    return {'x': x, 'ctx_1024': ctx_1024, 'g_xattn': g_xattn, 'g_ffn': g_ffn, 'L0_xattn_Wq': _L0_xattn_in['Wq'], 'L0_xattn_Wkv': _L0_xattn_in['Wkv'], 'L0_xattn_Wout': _L0_xattn_in['Wout'], 'L0_xattn_gm': _L0_xattn_in['gm'], 'L0_xattn_bm': _L0_xattn_in['bm'], 'L0_xattn_gl': _L0_xattn_in['gl'], 'L0_xattn_bl': _L0_xattn_in['bl'], 'L0_ffn_w1': _L0_ffn_in['w1'], 'L0_ffn_conv_w': _L0_ffn_in['conv_w'], 'L0_ffn_conv_b': _L0_ffn_in['conv_b'], 'L0_ffn_w2': _L0_ffn_in['w2'], 'L1_xattn_Wq': _L1_xattn_in['Wq'], 'L1_xattn_bq': _L1_xattn_in['bq'], 'L1_xattn_Wk': _L1_xattn_in['Wk'], 'L1_xattn_bk': _L1_xattn_in['bk'], 'L1_xattn_Wv': _L1_xattn_in['Wv'], 'L1_xattn_bv': _L1_xattn_in['bv'], 'L1_xattn_Wo': _L1_xattn_in['Wo'], 'L1_xattn_bo': _L1_xattn_in['bo'], 'L1_ffn_gate_w': _L1_ffn_in['gate_w'], 'L1_ffn_wg': _L1_ffn_in['wg'], 'L1_ffn_wu': _L1_ffn_in['wu'], 'L1_ffn_wd': _L1_ffn_in['wd'], 'L1_ffn_sg': _L1_ffn_in['sg'], 'L1_ffn_su': _L1_ffn_in['su'], 'L1_ffn_sd': _L1_ffn_in['sd']}

def reference(x, ctx_1024, g_xattn, g_ffn, L0_xattn_Wq, L0_xattn_Wkv, L0_xattn_Wout, L0_xattn_gm, L0_xattn_bm, L0_xattn_gl, L0_xattn_bl, L0_ffn_w1, L0_ffn_conv_w, L0_ffn_conv_b, L0_ffn_w2, L1_xattn_Wq, L1_xattn_bq, L1_xattn_Wk, L1_xattn_bk, L1_xattn_Wv, L1_xattn_bv, L1_xattn_Wo, L1_xattn_bo, L1_ffn_gate_w, L1_ffn_wg, L1_ffn_wu, L1_ffn_wd, L1_ffn_sg, L1_ffn_su, L1_ffn_sd):
    import jax
    import jax.numpy as jnp

    def _L0_xattn_ref(x, latents, Wq, Wkv, Wout, gm, bm, gl, bl):
        import jax, jax.numpy as jnp
        import numpy as np
        D_MODEL = 128
        D_HEAD = 64
        NHEADS = 8
        IN_DIM = D_HEAD * NHEADS
        EPS = 1e-05

        def layernorm(x, g, b):
            mu = jnp.mean(x, axis=-1, keepdims=True)
            var = jnp.var(x, axis=-1, keepdims=True)
            return (x - mu) * jax.lax.rsqrt(var + EPS) * g + b
        scale = D_HEAD ** (-0.5)
        xn = layernorm(x, gm, bm)
        ln = layernorm(latents, gl, bl)
        q = ln @ Wq
        kv_input = jnp.concatenate([xn, ln], axis=-2)
        kv = kv_input @ Wkv
        k, v = jnp.split(kv, 2, axis=-1)

        def heads(t):
            B, S, _ = t.shape
            return t.reshape(B, S, NHEADS, D_HEAD).transpose(0, 2, 1, 3)
        q, k, v = (heads(q), heads(k), heads(v))
        q = q / scale
        sim = jnp.einsum('bhid,bhjd->bhij', q, k)
        sim = sim - jax.lax.stop_gradient(jnp.max(sim, axis=-1, keepdims=True))
        attn = jax.nn.softmax(sim, axis=-1)
        out = jnp.einsum('bhij,bhjd->bhid', attn, v)
        B, H, L, dh = out.shape
        out = out.transpose(0, 2, 1, 3).reshape(B, L, H * dh)
        return out @ Wout

    def _L0_ffn_ref(x, w1, conv_w, conv_b, w2):
        import jax, jax.numpy as jnp
        import numpy as np
        B, S, D_MODEL, D_HIDDEN = (4, 256, 128, 512)

        def act_quant(x):
            scale = 127.0 / jnp.clip(jnp.max(jnp.abs(x), axis=-1, keepdims=True), 1e-05)
            return jnp.clip(jnp.round(x * scale), -128, 127) / scale

        def weight_quant(w):
            scale = 1.0 / jnp.clip(jnp.mean(jnp.abs(w)), 1e-05)
            return jnp.clip(jnp.round(w * scale), -1, 1) / scale

        def bit_linear(x, w):
            xq = x + jax.lax.stop_gradient(act_quant(x) - x)
            wq = w + jax.lax.stop_gradient(weight_quant(w) - w)
            return jnp.einsum('bsd,hd->bsh', xq, wq)

        def depthwise_conv1d(x_bcl, w, b):
            y = jax.lax.conv_general_dilated(x_bcl, w, window_strides=(1,), padding=[(1, 1)], dimension_numbers=('NCH', 'OIH', 'NCH'), feature_group_count=x_bcl.shape[1])
            return y + b[None, :, None]
        h = bit_linear(x, w1)
        h = depthwise_conv1d(h.transpose(0, 2, 1), conv_w, conv_b)
        h = h.transpose(0, 2, 1)
        h = jax.nn.silu(h)
        return bit_linear(h, w2)

    def _L1_xattn_ref(query, key, value, Wq, bq, Wk, bk, Wv, bv, Wo, bo):
        import jax, jax.numpy as jnp
        import numpy as np
        DIM = 128
        N_HEADS = 16
        HEAD_DIM = DIM // N_HEADS
        GAMMA = 10.0

        def larope_cos_sin(seq_len, gamma, head_dim):
            inv_freq = 1.0 / 10000.0 ** (jnp.arange(0, head_dim, 2, dtype=jnp.float32) / head_dim)
            t = jnp.arange(seq_len, dtype=jnp.float32)
            freqs = jnp.outer(gamma * (t / seq_len), inv_freq)
            emb = jnp.concatenate([freqs, freqs], axis=-1)
            return (jnp.cos(emb), jnp.sin(emb))

        def apply_rope(x, cos, sin):
            d = x.shape[-1] // 2
            x1, x2 = (x[..., :d], x[..., d:])
            c = cos[None, None, :, :d]
            s = sin[None, None, :, :d]
            return jnp.concatenate([x1 * c - x2 * s, x1 * s + x2 * c], axis=-1)
        B, Lq, _ = query.shape
        Lk = key.shape[1]
        scale = HEAD_DIM ** (-0.5)

        def proj(x, W, b, L):
            y = x @ W.T + b
            return y.reshape(B, L, N_HEADS, HEAD_DIM).transpose(0, 2, 1, 3)
        q = proj(query, Wq, bq, Lq)
        k = proj(key, Wk, bk, Lk)
        v = proj(value, Wv, bv, Lk)
        q_cos, q_sin = larope_cos_sin(Lq, GAMMA, HEAD_DIM)
        k_cos, k_sin = larope_cos_sin(Lk, GAMMA, HEAD_DIM)
        q = apply_rope(q, q_cos, q_sin)
        k = apply_rope(k, k_cos, k_sin)
        scores = jnp.einsum('bhqd,bhkd->bhqk', q, k) * scale
        attn = jax.nn.softmax(scores, axis=-1)
        out = jnp.einsum('bhqk,bhkd->bhqd', attn, v)
        out = out.transpose(0, 2, 1, 3).reshape(B, Lq, DIM)
        return out @ Wo.T + bo

    def _L1_ffn_ref(x, gate_w, wg, wu, wd, sg, su, sd):
        import jax, jax.numpy as jnp
        import numpy as np
        DIM = 128
        INTER = 64
        E = 8
        TOP_K = 2
        ROUTE_SCALE = 1.0
        B, S, D = x.shape
        xf = x.reshape(-1, D)
        N = xf.shape[0]
        scores = jax.nn.softmax(xf @ gate_w.T, axis=-1)
        _, idx = jax.lax.top_k(scores, TOP_K)
        weights = jnp.take_along_axis(scores, idx, axis=-1) * ROUTE_SCALE
        cw = jnp.zeros((N, E), dtype=xf.dtype)
        cw = cw.at[jnp.arange(N)[:, None], idx].add(weights)
        g = jnp.einsum('nd,efd->nef', xf, wg)
        u = jnp.einsum('nd,efd->nef', xf, wu)
        h = jax.nn.silu(g) * u
        y = jnp.einsum('nef,edf->ned', h, wd)
        routed = jnp.einsum('ned,ne->nd', y, cw)
        shared = jax.nn.silu(xf @ sg.T) * (xf @ su.T) @ sd.T
        return (routed + shared).reshape(B, S, D)
    x = x + jnp.tanh(g_xattn[0]) * _L0_xattn_ref(ctx_1024, _layernorm(x, axis=-1), L0_xattn_Wq, L0_xattn_Wkv, L0_xattn_Wout, L0_xattn_gm, L0_xattn_bm, L0_xattn_gl, L0_xattn_bl)
    x = x + jnp.tanh(g_ffn[0]) * _L0_ffn_ref(_layernorm(x, axis=-1), L0_ffn_w1, L0_ffn_conv_w, L0_ffn_conv_b, L0_ffn_w2)
    x = x + jnp.tanh(g_xattn[1]) * _L1_xattn_ref(_layernorm(x, axis=-1), ctx_1024, ctx_1024, L1_xattn_Wq, L1_xattn_bq, L1_xattn_Wk, L1_xattn_bk, L1_xattn_Wv, L1_xattn_bv, L1_xattn_Wo, L1_xattn_bo)
    x = x + jnp.tanh(g_ffn[1]) * _L1_ffn_ref(_layernorm(x, axis=-1), L1_ffn_gate_w, L1_ffn_wg, L1_ffn_wu, L1_ffn_wd, L1_ffn_sg, L1_ffn_su, L1_ffn_sd)
    return x

_drawn_inputs = setup_inputs


def setup_inputs(seed=0):
    import zlib

    import numpy as np

    out = dict(_drawn_inputs(seed))
    spreads = {'g_ffn': (-1.0, 0.6),
     'L0_xattn_gm': (1.0, 0.2),
     'L0_xattn_bm': (0.0, 0.1),
     'L0_xattn_gl': (1.0, 0.2),
     'L0_xattn_bl': (0.0, 0.1),
     'L1_xattn_bq': (0.0, 0.457),
     'L1_xattn_bk': (0.0, 0.8),
     'L1_xattn_bv': (0.0, 0.1),
     'L1_xattn_bo': (0.0, 0.1)}
    factors = {'L1_ffn_gate_w': 3.161, 'L1_ffn_wg': 2.772, 'L1_ffn_wu': 2.732, 'L1_ffn_wd': 2.732}
    for name, (base, spread) in spreads.items():
        noise = np.random.default_rng([zlib.crc32(name.encode()), seed]).standard_normal(out[name].shape)
        drawn = base * np.exp(spread * noise) if base else spread * noise
        out[name] = jnp.asarray(drawn.astype(out[name].dtype))
    for name, factor in factors.items():
        out[name] = (out[name] * factor).astype(out[name].dtype)
    return out
```

```python
from contextlib import ExitStack

import numpy as np

import concourse.bass as bass
from concourse import mybir

F32 = mybir.dt.float32
BF16 = mybir.dt.bfloat16
U32 = mybir.dt.uint32
ALU = mybir.AluOpType
ACT = mybir.ActivationFunctionType
AX = mybir.AxisListType

P = 128
D = 128
B = 2
S = 512
C = 77
QT = S // P
NT = B * QT
H0, DH0 = 8, 64
HP = H0 // 2
IN0 = H0 * DH0
KEYS0 = S + C
KP = 5 * P
HID = 512
HC = HID // P
H1, DH1 = 16, 8
HH = H1 // 2
E1, F1 = 8, 64
MH = E1 * F1
MT = MH + F1
EPS = 1e-5
MAGIC = float(1.5 * 2 ** 23)
SLOTS = 3

COLS = ["gl", "bl", "gm", "bm", "bq", "bqs", "bk", "bks", "bv", "gx0", "gx1", "gf0", "gf1"]
CONV_W = len(COLS)
CONV_B = CONV_W + 3 * HC
NCOL = CONV_B + HC + 1
K_ID, K_ONE, K_IOTA, K_MASK = 0, P, 2 * P, 2 * P + E1
K_CQ = K_MASK + H1
K_SQ = K_CQ + S
K_CK = K_SQ + S
K_SK = K_CK + C
NCONST = K_SK + C


def steps():
    def attention(b):
        out = []
        for hp in range(HP):
            units = [("u", b, hp, qt, hh) for qt in range(QT) for hh in range(2)]
            out += units[:4]
            if hp + 1 < HP:
                out += [("q", b, hp + 1), ("k", b, hp + 1)]
            if b == 0 and hp == 1:
                out += [("s", b)]
            out += units[4:]
        return out

    def begin(b):
        return [("x0", b)] + [("v", b, j) for j in range(3)] + [("q", b, 0), ("k", b, 0)]

    def rest(b):
        out = [("w", b, t) for t in range(QT)] + [("-",), ("f1", b)] + [("f2", b, c) for c in range(HC)]
        out += [("f3", b, t) for t in range(QT)] + [("f4", b, t) for t in range(QT)]
        out += [("a3", b), ("a1", b), ("a2", b)]
        out += [("a4", b, t, h) for t in range(QT) for h in range(2)] + [("-",), ("-",)]
        out += [("a6", b), ("-",), ("m1", b), ("m3", b)]
        out += [("m2", b, t) for t in range(QT)] + [("m4", b, t) for t in range(QT)]
        return out

    return begin(0) + attention(0) + begin(1) + attention(1) + [("-",), ("-",)] + rest(0) + rest(1)


STEPS = steps()
AT = {item: n for n, item in enumerate(STEPS) if item != ("-",)}
REAL = [item for item in STEPS if item != ("-",)]
NTH = {item: n for n, item in enumerate(REAL)}
EAGER = ("q", "k", "v", "u", "a4")


def upto(item):
    return sum(x[0] == item[0] for x in REAL[:NTH[item] + 1])


def mega_kernel(nc, x, ctx, ctxT, cols, wq, wkv, wout, w1T, w2T, l1w, bo, wgu, wdT, const, out):
    stack = ExitStack()
    with stack:
        def sb(name, shape, dt=F32):
            return stack.enter_context(nc.sbuf_tensor(name, shape, dt))

        def sem(name):
            return stack.enter_context(nc.semaphore(name))

        slots = [stack.enter_context(nc.psum_tensor(f"slot{i}", [P, 2 * 512], F32)) for i in range(SLOTS)]
        accs = [stack.enter_context(nc.psum_tensor(f"acc{i}", [P, 512], F32)) for i in range(2)]

        X = sb("X", [P, NT, D])
        CT = sb("CT", [C, B, D])
        CTT = sb("CTT", [P, B, C])
        COL = sb("COL", [P, NCOL])
        WQ = sb("WQ", [P, IN0])
        WKV = sb("WKV", [P, 2 * IN0])
        WOUT = sb("WOUT", [P, HC, D])
        W1 = sb("W1", [P, HID])
        W2 = sb("W2", [P, HC, D])
        L1W = sb("L1W", [P, 6, D])
        BO = sb("BO", [1, D])
        WGU = sb("WGU", [P, 2 * MT + E1])
        WD = sb("WD", [P, 5, D])
        K = sb("K", [P, NCONST])
        ident, ones = K[:, K_ID:K_ID + P], K[:, K_ONE:K_ONE + P]
        identb = sb("identb", [P, P], BF16)

        bnx = sb("bnx", [P, 4, NT, 6])
        mvx = sb("mvx", [P, 4, NT, 2])
        vex = sb("vex", [P, 4, NT])
        bnc = sb("bnc", [C, B, 6])
        mvc = sb("mvc", [C, B, 2])
        vec = sb("vec", [C, B])
        mhalf = sb("mhalf", [P, NT])
        tg = sb("tg", [P, 4])
        ws = sb("ws", [P, 2, 4])
        cw = sb("cw", [P, 3 * HC])
        g2 = sb("g2", [P, 1])
        aq = sb("aq", [P, NT, 4])
        aq2 = sb("aq2", [P, NT, 4])
        nm0 = sb("nm0", [P, 3])
        sum0 = sb("sum0", [P, B, HP, 8])
        rec0 = sb("rec0", [P, B, HP, 8])
        mx1 = sb("mx1", [P, 4, HH])
        rec1 = sb("rec1", [P, NT, H1])
        lg = sb("lg", [P, NT, E1])
        top = sb("top", [P, NT, 8])
        idx = sb("idx", [P, NT, 8], U32)
        idf = sb("idf", [P, NT, 8])
        rt = sb("rt", [P, NT, 4])
        hot = sb("hot", [P, NT, 2, E1])
        cwt = sb("cwt", [P, NT, E1])

        XN = sb("XN", [P, 4, NT, D])
        CN = sb("CN", [C, B, D])
        LT = sb("LT", [P, B, KEYS0])
        XQT = X2T = X3T = LT[:, :, 0:S]
        QS = sb("QS", [P, 2, S])
        KS = sb("KS", [P, 2, KEYS0])
        V = sb("V", [P, B, 5, IN0])
        PR = sb("PR", [P, SLOTS, KP])
        PT = sb("PT", [P, SLOTS, KP])
        ON = sb("ON", [P, NT, IN0])
        OT = sb("OT", [P, 2, KP])
        X1 = sb("X1", [P, NT, D])
        W1Q = sb("W1Q", [P, HID])
        W2Q = sb("W2Q", [P, HC * D], BF16)
        YC = ON[:, :, :].rearrange("p (b c) s -> p b c s", b=B)
        TH = sb("TH", [P, 2, S])
        QM = sb("QM", [P, 2, HID])
        QB = sb("QB", [P, 4, HID], BF16)
        QBT = sb("QBT", [P, 2, HID], BF16)
        X2 = sb("X2", [P, NT, D])
        RC = sb("RC", [P, 2, S])
        Q1 = sb("Q1", [P, B, S])
        K1 = sb("K1", [P, B, C])
        KBD = sb("KBD", [P, B, H1, C])
        V1 = sb("V1", [C, B, H1, DH1 + 1])
        S1 = sb("S1", [P, 4, HH * C])
        PT1 = sb("PT1", [C, 3, HH * P])
        A1 = sb("A1", [P, NT, D])
        A1T = sb("A1T", [P, B, S])
        X3 = sb("X3", [P, NT, D])
        HB = TH
        SHT = sb("SHT", [P, B, QT, F1])
        HMV = V[:, :, :, :].rearrange("p b c n -> p b (c n)")[:, :, 0:QT * MT].rearrange("p b (t n) -> p b t n", t=QT)
        HT = OT
        Y = X1

        names = ["x0", "x1", "ctx", "cols", "wq", "wkv", "const", "wout", "ffn", "l1", "moe"]
        ld = {n: sem(f"ld_{n}") for n in names}
        stored = sem("stored")
        dve_step = sem("dve_step")
        act_step = sem("act_step")
        pool_const = sem("pool_const")
        front_done = sem("front_done")
        var_ready = [sem(f"var_ready{i}") for i in range(4)]
        rstd_ready = [sem(f"rstd_ready{i}") for i in range(4)]
        varc_ready = sem("varc_ready")
        rstdc_ready = sem("rstdc_ready")
        xn_ready = [sem(f"xn_ready{i}") for i in range(4)]
        cn_ready = sem("cn_ready")
        lt_ready = sem("lt_ready")
        v_ready = sem("v_ready")
        q_ready = sem("q_ready")
        k_ready = sem("k_ready")
        max_ready = sem("max_ready")
        prob_ready = sem("prob_ready")
        prob_turned = sem("prob_turned")
        pt_by_act = sem("pt_by_act")
        pt_by_dve = sem("pt_by_dve")
        pv_done = sem("pv_done")
        o_ready = sem("o_ready")
        ot_ready = sem("ot_ready")
        y_done = sem("y_done")
        x1_ready = sem("x1_ready")
        pad_ready = sem("pad_ready")
        identb_ready = sem("identb_ready")
        gates_ready = sem("gates_ready")
        wsum_ready = sem("wsum_ready")
        wmean_ready = sem("wmean_ready")
        w1q_ready = sem("w1q_ready")
        w2q_ready = sem("w2q_ready")
        conv_scaled = sem("conv_scaled")
        xqt_ready = sem("xqt_ready")
        conv_mid = sem("conv_mid")
        conv_done = sem("conv_done")
        tanh_done = sem("tanh_done")
        silu_ready = sem("silu_ready")
        scale_ready = sem("scale_ready")
        rounded = sem("rounded")
        qb_ready = sem("qb_ready")
        qbt_ready = sem("qbt_ready")
        f_done = sem("f_done")
        x2_ready = sem("x2_ready")
        x2t_ready = sem("x2t_ready")
        q1_ready = sem("q1_ready")
        kv1_ready = sem("kv1_ready")
        shifted = sem("shifted")
        exp1_ready = sem("exp1_ready")
        p1_turned = sem("p1_turned")
        pt1_ready = sem("pt1_ready")
        pv1_done = sem("pv1_done")
        a1_ready = sem("a1_ready")
        a1t_ready = sem("a1t_ready")
        ya_done = sem("ya_done")
        x3_ready = sem("x3_ready")
        x3t_ready = sem("x3t_ready")
        logits_copied = sem("logits_copied")
        logits_ready = sem("logits_ready")
        exps_ready = sem("exps_ready")
        shared_tanh = sem("shared_tanh")
        shared_ready = sem("shared_ready")
        weights_ready = sem("weights_ready")
        gate_tanh = sem("gate_tanh")
        hid_ready = sem("hid_ready")
        hidw_ready = sem("hidw_ready")
        ht_ready = sem("ht_ready")
        ym_done = sem("ym_done")
        y_ready = sem("y_ready")
        block = stack.enter_context(nc.Block())

        def last_read(item):
            n = upto(item)
            if item[0] == "u":
                return (pt_by_act, (n + 1) // 2) if n % 2 else (pt_by_dve, n // 2)
            return {"x0": (lt_ready, 2 * n), "v": (v_ready, n), "q": (q_ready, n), "k": (k_ready, n),
                    "s": (wmean_ready, n), "w": (x1_ready, n), "f1": (xqt_ready, n), "f2": (conv_done, n),
                    "f3": (rounded, n), "f4": (x2_ready, n), "a3": (kv1_ready, n), "a1": (x2t_ready, n),
                    "a2": (q1_ready, n), "a4": (pt1_ready, n), "a6": (x3_ready, n), "m1": (x3t_ready, n),
                    "m3": (shared_ready, n), "m2": (hid_ready, n), "m4": (y_ready, n)}[item[0]]

        def slot(item):
            return slots[NTH[item] % SLOTS]

        def col(name):
            return COL[:, COLS.index(name):COLS.index(name) + 1]

        def walk(first, second, third):
            for i in range(len(STEPS) + 2):
                stages = [(f, STEPS[i - k]) for k, f in enumerate((first, second, third))
                          if 0 <= i - k < len(STEPS) and STEPS[i - k] != ("-",)]
                if i < len(STEPS) and STEPS[i][0] not in EAGER and first is not None:
                    stages.reverse()
                for f, item in stages:
                    f(item)

        @block.sync
        def _(sp):
            xv = x.rearrange("(t p) d -> p t d", p=P)
            for b in range(B):
                sp.dma_start(X[:, b * QT:(b + 1) * QT, :], xv[:, b * QT:(b + 1) * QT, :]).then_inc(ld[f"x{b}"], 16)
            sp.dma_start(WKV[:], wkv).then_inc(ld["wkv"], 16)
            sp.dma_start(W2[:], w2T.rearrange("(c p) d -> p c d", p=P)).then_inc(ld["ffn"], 16)
            sp.dma_start(W1[:], w1T).then_inc(ld["ffn"], 16)
            sp.dma_start(WOUT[:], wout.rearrange("(c p) d -> p c d", p=P)).then_inc(ld["wout"], 16)
            sp.dma_start(L1W[:], l1w.rearrange("p (k d) -> p k d", d=D)).then_inc(ld["l1"], 16)
            sp.dma_start(BO[:], bo).then_inc(ld["l1"], 16)
            sp.dma_start(CTT[:], ctxT.rearrange("p (b c) -> p b c", b=B)).then_inc(ld["l1"], 16)
            sp.dma_start(WGU[:], wgu).then_inc(ld["moe"], 16)
            sp.dma_start(WD[:], wdT.rearrange("(c p) d -> p c d", p=P)).then_inc(ld["moe"], 16)
            ov = out.rearrange("(t p) d -> t p d", p=P)
            for t in range(NT):
                sp.wait_ge(y_ready, t + 1)
                sp.dma_start(ov[t], Y[:, t, :]).then_inc(stored, 16)
            sp.wait_ge(stored, 16 * NT)

        @block.gpsimd
        def _(pool):
            pool.memset(mhalf[:], -0.5).then_inc(pool_const, 1)
            pool.memset(PR[:], 0.0).then_inc(pad_ready, 1)
            pool.wait_ge(pool_const, 1)

            def rstd(n, b):
                r = slice(b * QT, (b + 1) * QT)
                pool.wait_ge(var_ready[n], b + 1)
                pool.tensor_tensor(vex[:, n, r], vex[:, n, r], mhalf[:, r], ALU.pow).then_inc(rstd_ready[n], 1)

            rstd(0, 0)
            pool.wait_ge(varc_ready, 1)
            pool.tensor_tensor(vec[:], vec[:], mhalf[0:C, 0:B], ALU.pow).then_inc(rstdc_ready, 1)
            rstd(0, 1)

            for item in REAL:
                if item[0] == "w" and item[2] == QT - 1:
                    rstd(1, item[1])
                if item[0] == "f4" and item[2] == QT - 1:
                    rstd(2, item[1])
                if item[0] == "a6":
                    rstd(3, item[1])
                if item[0] == "m2":
                    _, b, t = item
                    m = b * QT + t
                    pool.wait_ge(weights_ready, b + 1)
                    pool.wait_ge(hid_ready, m + 1)
                    hm = HMV[:, b, m % QT, 0:MH].rearrange("p (e f) -> p e f", e=E1)
                    pool.tensor_tensor(hm, hm, cwt[:, m, :].unsqueeze(2).broadcast_to([P, E1, F1]),
                                       ALU.mult).then_inc(hidw_ready, 1)

        @block.tensor
        def _(pe):
            def turn(dst, src, p=P):
                return pe.transpose(dst, src, ident[0:p, 0:p])

            def turn_tiles(W, b, n):
                for t in range(QT):
                    pe.wait_ge(xn_ready[n], b * QT + t + 1)
                    mm = turn(W[:, t * P:(t + 1) * P], XN[:, n, b * QT + t, :])
                return mm

            def front(item):
                kind, b = item[0], item[1]
                W = slot(item)
                if NTH[item] >= SLOTS:
                    pe.wait_ge(*last_read(REAL[NTH[item] - SLOTS]))
                if kind == "x0":
                    if b == 0:
                        pe.wait_ge(ld["const"], 16)
                    turn_tiles(W, b, 0)
                    pe.wait_ge(cn_ready, b + 1)
                    mm = turn(W[:, S:S + C], CN[:, b, :], C)
                elif kind == "v":
                    j = item[2]
                    pe.wait_ge(lt_ready, 2 * (b + 1))
                    pe.wait_ge(ld["wkv"], 16)
                    for n, c in enumerate([2 * j, 2 * j + 1] if j < 2 else [4]):
                        w = P if c < 4 else C
                        mm = pe.matmul(W[0:w, n * 512:n * 512 + 512], LT[:, b, c * P:c * P + w], WKV[:, IN0:],
                                       start=True, stop=True)
                elif kind == "q":
                    hp = item[2]
                    pe.wait_ge(ld["wq"], 16)
                    mm = pe.matmul(W[:, 0:S], WQ[:, hp * P:(hp + 1) * P], LT[:, b, 0:S], start=True, stop=True)
                elif kind == "k":
                    hp = item[2]
                    w = WKV[:, hp * P:(hp + 1) * P]
                    pe.matmul(W[:, 0:S], w, LT[:, b, 0:S], start=True, stop=True)
                    mm = pe.matmul(W[:, S:KEYS0], w, LT[:, b, S:KEYS0], start=True, stop=True)
                elif kind == "u":
                    _, b, hp, qt, hh = item
                    g = b * HP + hp
                    r = slice(hh * DH0, (hh + 1) * DH0)
                    pe.wait_ge(q_ready, g + 1)
                    pe.wait_ge(k_ready, g + 1)
                    q = QS[r, g % 2, qt * P:(qt + 1) * P]
                    pe.matmul(W[:, 0:S], q, KS[r, g % 2, 0:S], start=True, stop=True)
                    mm = pe.matmul(W[:, S:KEYS0], q, KS[r, g % 2, S:KEYS0], start=True, stop=True)
                elif kind == "s":
                    pe.wait_ge(wsum_ready, 2)
                    mm = pe.matmul(W[:, 0:2], ones, ws[:, 0, 0:2], start=True, stop=True)
                elif kind == "w":
                    t = b * QT + item[2]
                    pe.wait_ge(o_ready, (b + 1) * HP)
                    for c in range(HC):
                        mm = turn(W[:, c * P:(c + 1) * P], ON[:, t, c * P:(c + 1) * P])
                elif kind == "f1":
                    mm = turn_tiles(W, b, 1)
                elif kind == "f2":
                    c = item[2]
                    pe.wait_ge(xqt_ready, b + 1)
                    pe.wait_ge(w1q_ready, 1)
                    mm = pe.matmul(W[:, 0:S], W1Q[:, c * P:(c + 1) * P], XQT[:, b, :], start=True, stop=True)
                elif kind == "f3":
                    t = item[2]
                    for c in range(HC):
                        pe.wait_ge(silu_ready, upto(("f2", b, c)))
                        mm = turn(W[:, c * P:(c + 1) * P], YC[:, b, c, t * P:(t + 1) * P])
                elif kind == "f4":
                    n = upto(item)
                    pe.wait_ge(qb_ready, n)
                    pe.wait_ge(identb_ready, 1)
                    Wb = W[:, 0:256].bitcast(BF16)
                    for c in range(HC):
                        mm = pe.transpose(Wb[:, c * P:(c + 1) * P], QB[:, (n - 1) % 4, c * P:(c + 1) * P], identb[:])
                elif kind == "a3":
                    pe.wait_ge(ld["l1"], 48)
                    pe.matmul(W[:, 0:C], L1W[:, 2, :], CTT[:, b, :], start=True, stop=True)
                    pe.matmul(W[:, P:P + C], L1W[:, 3, :], CTT[:, b, :], start=True, stop=True)
                    mm = pe.matmul(W[0:C, 512:512 + D], CTT[:, b, :], L1W[:, 4, :], start=True, stop=True)
                elif kind == "a1":
                    mm = turn_tiles(W, b, 2)
                elif kind == "a2":
                    pe.wait_ge(x2t_ready, b + 1)
                    pe.matmul(W[:, 0:S], L1W[:, 0, :], X2T[:, b, :], start=True, stop=True)
                    mm = pe.matmul(W[:, S:2 * S], L1W[:, 1, :], X2T[:, b, :], start=True, stop=True)
                elif kind == "a4":
                    _, b, t, h = item
                    pe.wait_ge(q1_ready, b + 1)
                    pe.wait_ge(kv1_ready, b + 1)
                    for n in range(2):
                        kk = KBD[:, b, h * HH + n * 4:h * HH + n * 4 + 4, :]
                        mm = pe.matmul(W[:, n * 512:n * 512 + 4 * C], Q1[:, b, t * P:(t + 1) * P], kk,
                                       start=True, stop=True)
                elif kind == "a6":
                    for t in range(QT):
                        pe.wait_ge(a1_ready, b * QT + t + 1)
                        mm = turn(W[:, t * P:(t + 1) * P], A1[:, b * QT + t, :])
                elif kind == "m1":
                    mm = turn_tiles(W, b, 3)
                elif kind == "m3":
                    pe.wait_ge(x3t_ready, b + 1)
                    pe.wait_ge(ld["moe"], 32)
                    for t in range(QT):
                        mm = pe.matmul(W[:, t * 256:t * 256 + 2 * F1 + E1], X3T[:, b, t * P:(t + 1) * P],
                                       WGU[:, 2 * MH:], start=True, stop=True)
                elif kind == "m2":
                    t = item[2]
                    xt = X3T[:, b, t * P:(t + 1) * P]
                    pe.matmul(W[:, 0:MH], xt, WGU[:, 0:MH], start=True, stop=True)
                    mm = pe.matmul(W[:, MH:2 * MH], xt, WGU[:, MH:2 * MH], start=True, stop=True)
                elif kind == "m4":
                    m = b * QT + item[2]
                    pe.wait_ge(hidw_ready, m + 1)
                    pe.wait_ge(shared_ready, b + 1)
                    for c in range(HC):
                        turn(W[:, c * P:(c + 1) * P], HMV[:, b, m % QT, c * P:(c + 1) * P])
                    mm = turn(W[0:F1, 512:512 + P], HMV[:, b, m % QT, MH:MT])
                mm.then_inc(front_done, 1)

            def back(item):
                kind, b = item[0], item[1]
                W = slot(item)
                if kind == "u":
                    n = upto(item)
                    pe.wait_ge(prob_ready, n)
                    pe.wait_ge(pad_ready, 1)
                    for c in range(5):
                        mm = turn(W[:, c * P:(c + 1) * P], PR[:, (n - 1) % SLOTS, c * P:(c + 1) * P])
                    mm.then_inc(prob_turned, 1)
                elif kind == "w":
                    n = upto(item)
                    pe.wait_ge(ot_ready, n)
                    pe.wait_ge(ld["wout"], 16)
                    for c in range(HC):
                        mm = pe.matmul(W[:, 512:512 + D], OT[:, (n - 1) % 2, c * P:(c + 1) * P], WOUT[:, c, :],
                                       start=(c == 0), stop=(c == HC - 1))
                    mm.then_inc(y_done, 1)
                elif kind == "f4":
                    n = upto(item)
                    pe.wait_ge(qbt_ready, n)
                    pe.wait_ge(w2q_ready, 1)
                    for c in range(HC):
                        mm = pe.matmul(W[:, 512:512 + D], QBT[:, (n - 1) % 2, c * P:(c + 1) * P],
                                       W2Q[:, c * D:(c + 1) * D], start=(c == 0), stop=(c == HC - 1))
                    mm.then_inc(f_done, 1)
                elif kind == "a4":
                    n = upto(item)
                    pe.wait_ge(exp1_ready, n)
                    for h in range(HH):
                        mm = turn(W[0:C, h * P:(h + 1) * P], S1[:, (n - 1) % 4, h * C:(h + 1) * C])
                    mm.then_inc(p1_turned, 1)
                elif kind == "a6":
                    pe.wait_ge(a1t_ready, b + 1)
                    for t in range(QT):
                        o = W[:, 512 + t * D:512 + (t + 1) * D]
                        pe.matmul(o, A1T[:, b, t * P:(t + 1) * P], L1W[:, 5, :], start=True, stop=False)
                        mm = pe.matmul(o, ones[0:1, :], BO[:], start=False, stop=True)
                    mm.then_inc(ya_done, 1)
                elif kind == "m4":
                    n = upto(item)
                    pe.wait_ge(ht_ready, 2 * n)
                    o = W[:, 640:640 + D]
                    for c in range(HC):
                        pe.matmul(o, HT[:, (n - 1) % 2, c * P:(c + 1) * P], WD[:, c, :], start=(c == 0), stop=False)
                    pe.matmul(o, HT[0:F1, (n - 1) % 2, MH:MH + P], WD[0:F1, 4, :],
                              start=False, stop=True).then_inc(ym_done, 1)

            def tail(item):
                kind, b = item[0], item[1]
                if kind == "u":
                    _, b, hp, qt, hh = item
                    n, g = upto(item), b * HP + hp
                    if (qt, hh) == (0, 0):
                        pe.wait_ge(v_ready, 3 * (b + 1))
                        if g >= 2:
                            pe.wait_ge(o_ready, g - 1)
                    if n % 2:
                        pe.wait_ge(pt_by_act, (n + 1) // 2)
                    else:
                        pe.wait_ge(pt_by_dve, n // 2)
                    o = accs[g % 2][:, (qt * 2 + hh) * DH0:(qt * 2 + hh + 1) * DH0]
                    hcol = (hp * 2 + hh) * DH0
                    for c in range(5):
                        r = P if c < 4 else C
                        mm = pe.matmul(o, PT[0:r, (n - 1) % SLOTS, c * P:(c + 1) * P], V[0:r, b, c, hcol:hcol + DH0],
                                       start=(c == 0), stop=(c == 4))
                    mm.then_inc(pv_done, 1)
                elif kind == "a4":
                    _, b, t, h = item
                    n, m = upto(item), b * QT + t
                    pe.wait_ge(pt1_ready, n)
                    if h == 0 and m >= 2:
                        pe.wait_ge(a1_ready, m - 1)
                    for e in range(HH):
                        he = h * HH + e
                        mm = pe.matmul(accs[m % 2][:, he * (DH1 + 1):(he + 1) * (DH1 + 1)],
                                       PT1[:, (n - 1) % 3, e * P:(e + 1) * P], V1[:, b, he, :], start=True, stop=True)
                    mm.then_inc(pv1_done, 1)

            walk(front, back, tail)

        @block.scalar
        def _(act):
            act.dma_start(K[:], const).then_inc(ld["const"], 16)
            act.dma_start(COL[:], cols).then_inc(ld["cols"], 16)
            act.dma_start(CT[:], ctx.rearrange("(b c) d -> c b d", b=B)).then_inc(ld["ctx"], 16)
            act.dma_start(WQ[:], wq).then_inc(ld["wq"], 16)
            act.wait_ge(ld["cols"], 16)
            act.activation(tg[:], COL[:, COLS.index("gx0"):COLS.index("gx0") + 4], ACT.Tanh).then_inc(gates_ready, 1)

            def first(item):
                kind, b = item[0], item[1]
                W, n = slot(item), upto(item)
                if kind == "u":
                    act.wait_ge(max_ready, n)
                    if n == 1:
                        act.wait_ge(pad_ready, 1)
                    if n > SLOTS:
                        act.wait_ge(prob_turned, n - SLOTS)
                    s, r = (n - 1) % SLOTS, item[3] * 2 + item[4]
                    act.activation(PR[:, s, 0:KEYS0], W[:, 0:KEYS0], ACT.Exp, bias=nm0[:, s:s + 1],
                                   accum_out=sum0[:, b, item[2], r:r + 1]).then_inc(prob_ready, 1)
                    return
                if kind in ("k", "s", "a2", "a3"):
                    return
                act.wait_ge(front_done, NTH[item] + 1)
                if kind == "x0":
                    act.activation(LT[:, b, 0:S], W[:, 0:S], ACT.Identity, bias=col("bl"),
                                   scale=col("gl")).then_inc(lt_ready, 1)
                    act.activation(LT[:, b, S:KEYS0], W[:, S:KEYS0], ACT.Identity, bias=col("bm"),
                                   scale=col("gm")).then_inc(lt_ready, 1)
                elif kind == "v":
                    j = item[2]
                    if j < 2:
                        act.activation(V[:, b, 2 * j:2 * j + 2, :], W[:, :], ACT.Copy).then_inc(v_ready, 1)
                    else:
                        act.activation(V[0:C, b, 4, :], W[0:C, 0:512], ACT.Copy).then_inc(v_ready, 1)
                elif kind == "q":
                    if n > 2:
                        act.wait_ge(prob_turned, 8 * (n - 2))
                    act.activation(QS[:, (n - 1) % 2, :], W[:, 0:S], ACT.Copy,
                                   scale=float(DH0) ** 0.5).then_inc(q_ready, 1)
                elif kind == "w":
                    if n > 2:
                        act.wait_ge(y_done, n - 2)
                    act.activation(OT[:, (n - 1) % 2, 0:IN0], W[:, 0:IN0], ACT.Copy).then_inc(ot_ready, 1)
                elif kind == "f1":
                    act.activation(XQT[:, b, :], W[:, 0:S], ACT.Copy).then_inc(xqt_ready, 1)
                elif kind == "f2":
                    c = item[2]
                    act.wait_ge(conv_scaled, 1)
                    act.activation(YC[:, b, c, :], W[:, 0:S], ACT.Identity,
                                   bias=COL[:, CONV_B + c:CONV_B + c + 1],
                                   scale=cw[:, 3 * c + 1:3 * c + 2]).then_inc(conv_mid, 1)
                elif kind == "f3":
                    m = b * QT + item[2]
                    act.wait_ge(scale_ready, n)
                    if n > 2:
                        act.wait_ge(qb_ready, n - 2)
                    act.activation(QM[:, (n - 1) % 2, :], W[:, 0:HID], ACT.Identity, bias=COL[:, NCOL - 1:NCOL],
                                   scale=aq2[:, m, 2:3]).then_inc(rounded, 1)
                elif kind == "f4":
                    if n > 2:
                        act.wait_ge(f_done, n - 2)
                    act.activation(QBT[:, (n - 1) % 2, :], W[:, 0:256].bitcast(BF16), ACT.Copy).then_inc(qbt_ready, 1)
                elif kind == "a1":
                    act.activation(X2T[:, b, :], W[:, 0:S], ACT.Copy).then_inc(x2t_ready, 1)
                elif kind == "a4":
                    act.wait_ge(shifted, n)
                    s1 = S1[:, (n - 1) % 4, :]
                    act.activation(s1, s1, ACT.Exp, scale=float(DH1) ** -0.5).then_inc(exp1_ready, 1)
                elif kind == "a6":
                    act.activation(A1T[:, b, :], W[:, 0:S], ACT.Identity, bias=col("bv")).then_inc(a1t_ready, 1)
                elif kind == "m1":
                    act.activation(X3T[:, b, :], W[:, 0:S], ACT.Copy).then_inc(x3t_ready, 1)
                elif kind == "m3":
                    act.wait_ge(logits_copied, n)
                    act.activation(SHT[:, b], W[:, :].rearrange("p (t c) -> p t c", t=QT)[:, :, 0:F1], ACT.Tanh,
                                   scale=0.5).then_inc(shared_tanh, 1)
                    act.wait_ge(logits_ready, n)
                    r = slice(b * QT, (b + 1) * QT)
                    act.activation(lg[:, r, :], lg[:, r, :], ACT.Exp).then_inc(exps_ready, 1)
                elif kind == "m2":
                    if n > 2:
                        act.wait_ge(hid_ready, n - 2)
                    act.activation(HB[:, (n - 1) % 2, :], W[:, 0:MH], ACT.Tanh, scale=0.5).then_inc(gate_tanh, 1)
                elif kind == "m4":
                    if n > 2:
                        act.wait_ge(ym_done, n - 2)
                    act.activation(HT[:, (n - 1) % 2, 0:MH], W[:, 0:MH], ACT.Copy).then_inc(ht_ready, 1)
                    act.activation(HT[0:F1, (n - 1) % 2, MH:MH + P], W[0:F1, MH:MH + P],
                                   ACT.Copy).then_inc(ht_ready, 1)

            def second(item):
                kind, b = item[0], item[1]
                W, n = slot(item), upto(item)
                if kind == "u" and n % 2:
                    act.wait_ge(prob_turned, n)
                    if n > SLOTS:
                        act.wait_ge(pv_done, n - SLOTS)
                    act.activation(PT[:, (n - 1) % SLOTS, :], W[:, 0:KP], ACT.Copy).then_inc(pt_by_act, 1)
                elif kind == "f2":
                    c = item[2]
                    act.wait_ge(conv_done, n)
                    if n > 2:
                        act.wait_ge(silu_ready, n - 2)
                    act.activation(TH[:, (n - 1) % 2, :], YC[:, b, c, :], ACT.Tanh, scale=0.5).then_inc(tanh_done, 1)
                elif kind == "a4":
                    act.wait_ge(p1_turned, n)
                    if n > 3:
                        act.wait_ge(pv1_done, n - 3)
                    act.activation(PT1[:, (n - 1) % 3, :], W[0:C, :], ACT.Copy).then_inc(pt1_ready, 1)

            walk(first, second, lambda item: None)

        @block.vector
        def _(dve):
            steps_done = [0]

            def link(ins):
                steps_done[0] += 1
                ins.then_inc(dve_step, 1)
                dve.wait_ge(dve_step, steps_done[0])

            def link_all(instructions):
                for ins in instructions:
                    steps_done[0] += 1
                    ins.then_inc(dve_step, 1)
                dve.wait_ge(dve_step, steps_done[0])

            def stats(n, src, m):
                link(dve.bn_stats(bnx[:, n, m, :], src[:, m, :]))
                return dve.bn_aggr(mvx[:, n, m, :], bnx[:, n, m, :])

            def variance(n, b, twice=False):
                r = slice(b * QT, (b + 1) * QT)
                s1, s2 = (1.0 + EPS, EPS * EPS) if twice else (1.0, EPS)
                dve.tensor_scalar(vex[:, n, r], mvx[:, n, r, 1], s1, s2, ALU.mult, ALU.add).then_inc(var_ready[n], 1)

            def normalise(n, src, m, out, signal):
                return dve.tensor_scalar(out, src[:, m, :], mvx[:, n, m, 0:1], vex[:, n, m:m + 1],
                                         ALU.subtract, ALU.mult).then_inc(signal, 1)

            dve.wait_ge(ld["x0"], 16)
            link_all([dve.bn_stats(bnx[:, 0, m, :], X[:, m, :]) for m in range(QT)])
            link_all([dve.bn_aggr(mvx[:, 0, m, :], bnx[:, 0, m, :]) for m in range(QT)])
            variance(0, 0, twice=True)
            dve.wait_ge(ld["ctx"], 16)
            link_all([dve.bn_stats(bnc[:, b, :], CT[:, b, :]) for b in range(B)])
            link_all([dve.bn_aggr(mvc[:, b, :], bnc[:, b, :]) for b in range(B)])
            dve.tensor_scalar(vec[:], mvc[:, :, 1], EPS, None, ALU.add).then_inc(varc_ready, 1)
            dve.wait_ge(rstd_ready[0], 1)
            for m in range(QT):
                normalise(0, X, m, XN[:, 0, m, :], xn_ready[0])
            dve.wait_ge(rstdc_ready, 1)
            for b in range(B):
                dve.tensor_scalar(CN[:, b, :], CT[:, b, :], mvc[:, b, 0:1], vec[:, b:b + 1],
                                  ALU.subtract, ALU.mult).then_inc(cn_ready, 1)
            dve.wait_ge(ld["x1"], 16)
            link_all([dve.bn_stats(bnx[:, 0, m, :], X[:, m, :]) for m in range(QT, NT)])
            link_all([dve.bn_aggr(mvx[:, 0, m, :], bnx[:, 0, m, :]) for m in range(QT, NT)])
            variance(0, 1, twice=True)

            def first(item):
                kind, b = item[0], item[1]
                W, n = slot(item), upto(item)
                r = slice(b * QT, (b + 1) * QT)
                if kind in ("x0", "v", "q", "w", "f1", "f4", "a1", "a6", "m1", "m4"):
                    return
                dve.wait_ge(front_done, NTH[item] + 1)
                if kind == "k":
                    if n > 2:
                        dve.wait_ge(prob_turned, 8 * (n - 2))
                    dve.tensor_copy(KS[:, (n - 1) % 2, :], W[:, 0:KEYS0]).then_inc(k_ready, 1)
                elif kind == "u":
                    s = (n - 1) % SLOTS
                    if n > SLOTS:
                        dve.wait_ge(prob_ready, n - SLOTS)
                    dve.tensor_reduce(nm0[:, s:s + 1], W[:, 0:KEYS0], AX.X, ALU.max,
                                      negate=True).then_inc(max_ready, 1)
                elif kind == "s":
                    dve.tensor_scalar(ws[:, 1, 0:2], W[:, 0:2], 1.0 / (HID * D), 1e-5,
                                      ALU.mult, ALU.max).then_inc(wmean_ready, 1)
                    dve.wait_ge(wmean_ready, 1)
                    link(dve.reciprocal(ws[:, 1, 2:4], ws[:, 1, 0:2]))
                    w2f = W2[:].rearrange("p c d -> p (c d)")
                    link_all([dve.tensor_scalar(w, w, ws[:, 1, 2 + k:3 + k], MAGIC, ALU.mult, ALU.add)
                              for k, w in enumerate((W1[:], w2f))])
                    link_all([dve.tensor_scalar(w, w, MAGIC, 1.0, ALU.subtract, ALU.min) for w in (W1[:], w2f)])
                    dve.tensor_scalar(W1Q[:], W1[:], -1.0, None, ALU.max).then_inc(w1q_ready, 1)
                    dve.tensor_scalar(W2Q[:], w2f, -1.0, None, ALU.max).then_inc(w2q_ready, 1)
                    dve.tensor_scalar(cw[:], COL[:, CONV_W:CONV_W + 3 * HC], ws[:, 1, 0:1], None,
                                      ALU.mult).then_inc(conv_scaled, 1)
                    dve.wait_ge(gates_ready, 1)
                    link(dve.tensor_tensor(g2[:], tg[:, 2:3], ws[:, 1, 1:2], ALU.mult))
                elif kind == "f2":
                    c = item[2]
                    y = YC[:, b, c, :]
                    dve.wait_ge(conv_mid, n)
                    link(dve.scalar_tensor_tensor(out=y[:, 1:S], in0=W[:, 0:S - 1], scalar=cw[:, 3 * c:3 * c + 1],
                                                  in1=y[:, 1:S], op0=ALU.mult, op1=ALU.add))
                    dve.scalar_tensor_tensor(out=y[:, 0:S - 1], in0=W[:, 1:S], scalar=cw[:, 3 * c + 2:3 * c + 3],
                                             in1=y[:, 0:S - 1], op0=ALU.mult, op1=ALU.add).then_inc(conv_done, 1)
                elif kind == "f3":
                    m = b * QT + item[2]
                    a = aq2[:, m, :]
                    link(dve.tensor_reduce(a[:, 0:1], W[:, 0:HID], AX.X, ALU.max, apply_absolute_value=True))
                    link(dve.tensor_scalar(a[:, 0:1], a[:, 0:1], 0.5, 1e-5, ALU.mult, ALU.max))
                    link(dve.reciprocal(a[:, 1:2], a[:, 0:1]))
                    dve.tensor_scalar(a[:, 2:3], a[:, 1:2], 127.0 / 2, None, ALU.mult).then_inc(scale_ready, 1)
                    link(dve.tensor_scalar(a[:, 3:4], a[:, 0:1], 1.0 / 127, g2[:, 0:1], ALU.mult, ALU.mult))
                elif kind == "a3":
                    link(dve.tensor_copy(V1[:, b, :, 0:DH1],
                                         W[0:C, 512:512 + D].rearrange("p (h d) -> p h d", h=H1)))
                    link(dve.memset(V1[:, b, :, DH1:DH1 + 1], 1.0))
                    link_all([dve.scalar_tensor_tensor(out=RC[:, k, 0:C], in0=W[:, k * P:k * P + C],
                                                       scalar=col(("bk", "bks")[k]), in1=K[:, o:o + C],
                                                       op0=ALU.add, op1=ALU.mult) for k, o in enumerate((K_CK, K_SK))])
                    link(dve.tensor_tensor(K1[:, b, :], RC[:, 0, 0:C], RC[:, 1, 0:C], ALU.add))
                    dve.tensor_tensor(KBD[:, b], K1[:, b, :].unsqueeze(1).broadcast_to([P, H1, C]),
                                      K[:, K_MASK:K_MASK + H1].unsqueeze(2).broadcast_to([P, H1, C]),
                                      ALU.mult).then_inc(kv1_ready, 1)
                elif kind == "a2":
                    link_all([dve.scalar_tensor_tensor(out=RC[:, k, :], in0=W[:, k * S:(k + 1) * S],
                                                       scalar=col(("bq", "bqs")[k]), in1=K[:, o:o + S],
                                                       op0=ALU.add, op1=ALU.mult) for k, o in enumerate((K_CQ, K_SQ))])
                    dve.tensor_tensor(Q1[:, b, :], RC[:, 0, :], RC[:, 1, :], ALU.add).then_inc(q1_ready, 1)
                elif kind == "a4":
                    w = W[:, :].rearrange("p (k c) -> p k c", k=2)[:, :, 0:4 * C].rearrange("p k (h c) -> p k h c", c=C)
                    s = (n - 1) % 4
                    mx = mx1[:, s, :].rearrange("p (k h) -> p k h", k=2)
                    link(dve.tensor_reduce(mx, w, AX.X, ALU.max))
                    if n > 4:
                        dve.wait_ge(p1_turned, n - 4)
                    dve.tensor_tensor(S1[:, s, :].rearrange("p (k h c) -> p k h c", k=2, c=C), w,
                                      mx.unsqueeze(3).broadcast_to([P, 2, 4, C]), ALU.subtract).then_inc(shifted, 1)
                elif kind == "m3":
                    wv = W[:, :].rearrange("p (t c) -> p t c", t=QT)
                    dve.tensor_copy(lg[:, r, :], wv[:, :, 2 * F1:2 * F1 + E1]).then_inc(logits_copied, 1)
                    dve.wait_ge(logits_copied, n)
                    link_all([dve.max(top[:, m, :], lg[:, m, :]) for m in range(b * QT, (b + 1) * QT)])
                    link_all([dve.max_index(idx[:, m, :], top[:, m, :], lg[:, m, :])
                              for m in range(b * QT, (b + 1) * QT)])
                    dve.tensor_tensor(lg[:, r, :], lg[:, r, :], top[:, r, 0:1].broadcast_to([P, QT, E1]),
                                      ALU.subtract).then_inc(logits_ready, 1)
                    link(dve.tensor_copy(idf[:, r, 0:2], idx[:, r, 0:2]))
                    iota = K[:, K_IOTA:K_IOTA + E1].unsqueeze(1).broadcast_to([P, QT, E1])
                    link_all([dve.tensor_tensor(hot[:, r, k, :], iota, idf[:, r, k:k + 1].broadcast_to([P, QT, E1]),
                                                ALU.is_equal) for k in range(2)])
                    link(dve.tensor_tensor(hot[:, r, 0, :], hot[:, r, 0, :], hot[:, r, 1, :], ALU.add))
                    dve.wait_ge(shared_tanh, n)
                    sh = HMV[:, b, :, MH:MT]
                    link(dve.scalar_tensor_tensor(out=sh, in0=SHT[:, b], scalar=1.0, in1=wv[:, :, 0:F1],
                                                  op0=ALU.add, op1=ALU.mult))
                    link(dve.scalar_tensor_tensor(out=sh, in0=sh, scalar=0.5, in1=wv[:, :, F1:2 * F1],
                                                  op0=ALU.mult, op1=ALU.mult))
                    dve.wait_ge(exps_ready, n)
                    link(dve.tensor_reduce(rt[:, r, 0], lg[:, r, :], AX.X, ALU.add))
                    link(dve.reciprocal(rt[:, r, 1], rt[:, r, 0]))
                    link(dve.scalar_tensor_tensor(out=cwt[:, r, :], in0=lg[:, r, :], scalar=0.5, in1=hot[:, r, 0, :],
                                                  op0=ALU.mult, op1=ALU.mult))
                    dve.tensor_tensor(cwt[:, r, :], cwt[:, r, :], rt[:, r, 1:2].broadcast_to([P, QT, E1]),
                                      ALU.mult).then_inc(weights_ready, 1)
                    dve.wait_ge(weights_ready, n)
                    dve.sem_inc(shared_ready, 1)
                elif kind == "m2":
                    m = b * QT + item[2]
                    dve.wait_ge(gate_tanh, n)
                    link(dve.scalar_tensor_tensor(out=HMV[:, b, m % QT, 0:MH], in0=HB[:, (n - 1) % 2, :], scalar=1.0,
                                                  in1=W[:, 0:MH], op0=ALU.add, op1=ALU.mult))
                    dve.tensor_tensor(HMV[:, b, m % QT, 0:MH], HMV[:, b, m % QT, 0:MH], W[:, MH:2 * MH], ALU.mult).then_inc(hid_ready, 1)

            def second(item):
                kind, b = item[0], item[1]
                W, n = slot(item), upto(item)
                if kind == "x0" and b == 0:
                    dve.wait_ge(rstd_ready[0], 2)
                    for m in range(QT, NT):
                        normalise(0, X, m, XN[:, 0, m, :], xn_ready[0])
                    dve.wait_ge(ld["const"], 16)
                    dve.tensor_copy(identb[:], ident).then_inc(identb_ready, 1)
                elif kind == "k" and n == 2:
                    dve.wait_ge(ld["ffn"], 32)
                    dve.tensor_reduce(ws[:, 0, 0:1], W1[:], AX.X, ALU.add,
                                      apply_absolute_value=True).then_inc(wsum_ready, 1)
                    dve.tensor_reduce(ws[:, 0, 1:2], W2[:].rearrange("p c d -> p (c d)"), AX.X, ALU.add,
                                      apply_absolute_value=True).then_inc(wsum_ready, 1)
                elif kind == "u" and n % 2 == 0:
                    dve.wait_ge(prob_turned, n)
                    if n > SLOTS:
                        dve.wait_ge(pv_done, n - SLOTS)
                    dve.tensor_copy(PT[:, (n - 1) % SLOTS, :], W[:, 0:KP]).then_inc(pt_by_dve, 1)
                elif kind == "w":
                    m = b * QT + item[2]
                    dve.wait_ge(y_done, n)
                    dve.wait_ge(gates_ready, 1)
                    dve.scalar_tensor_tensor(out=X1[:, m, :], in0=W[:, 512:512 + D], scalar=tg[:, 0:1],
                                             in1=X[:, m, :], op0=ALU.mult, op1=ALU.add).then_inc(x1_ready, 1)
                    dve.wait_ge(x1_ready, n)
                    link(stats(1, X1, m))
                    if item[2] == QT - 1:
                        variance(1, b)
                elif kind == "f2":
                    c = item[2]
                    dve.wait_ge(tanh_done, n)
                    dve.scalar_tensor_tensor(out=YC[:, b, c, :], in0=TH[:, (n - 1) % 2, :], scalar=1.0,
                                             in1=YC[:, b, c, :], op0=ALU.add, op1=ALU.mult).then_inc(silu_ready, 1)
                elif kind == "f3":
                    dve.wait_ge(rounded, n)
                    if n > 4:
                        dve.wait_ge(qbt_ready, n - 4)
                    dve.tensor_scalar(QB[:, (n - 1) % 4, :], QM[:, (n - 1) % 2, :], MAGIC, None,
                                      ALU.subtract).then_inc(qb_ready, 1)
                elif kind == "f4":
                    m = b * QT + item[2]
                    dve.wait_ge(f_done, n)
                    dve.scalar_tensor_tensor(out=X2[:, m, :], in0=W[:, 512:512 + D], scalar=aq2[:, m, 3:4],
                                             in1=X1[:, m, :], op0=ALU.mult, op1=ALU.add).then_inc(x2_ready, 1)
                    dve.wait_ge(x2_ready, n)
                    link(stats(2, X2, m))
                    if item[2] == QT - 1:
                        variance(2, b)
                elif kind == "a6":
                    r = slice(b * QT, (b + 1) * QT)
                    dve.wait_ge(ya_done, n)
                    dve.scalar_tensor_tensor(out=X3[:, r, :], in0=W[:, 512:1024].rearrange("p (t d) -> p t d", t=QT),
                                             scalar=tg[:, 1:2], in1=X2[:, r, :], op0=ALU.mult,
                                             op1=ALU.add).then_inc(x3_ready, 1)
                    dve.wait_ge(x3_ready, n)
                    link_all([dve.bn_stats(bnx[:, 3, m, :], X3[:, m, :]) for m in range(b * QT, (b + 1) * QT)])
                    link_all([dve.bn_aggr(mvx[:, 3, m, :], bnx[:, 3, m, :]) for m in range(b * QT, (b + 1) * QT)])
                    variance(3, b)
                elif kind == "m4":
                    m = b * QT + item[2]
                    dve.wait_ge(ym_done, n)
                    dve.scalar_tensor_tensor(out=Y[:, m, :], in0=W[:, 640:640 + D], scalar=tg[:, 3:4],
                                             in1=X3[:, m, :], op0=ALU.mult, op1=ALU.add).then_inc(y_ready, 1)

            def third(item):
                kind, b = item[0], item[1]
                n = upto(item)
                tiles = range(b * QT, (b + 1) * QT)
                r = slice(b * QT, (b + 1) * QT)
                if kind == "u" and n % 8 == 0:
                    hp, g = item[2], n // 8
                    dve.wait_ge(prob_ready, n)
                    link(dve.reciprocal(rec0[:, b, hp, :], sum0[:, b, hp, :]))
                    dve.wait_ge(pv_done, n)
                    dve.tensor_tensor(ON[:, r, hp * P:(hp + 1) * P].rearrange("p t (h d) -> p t h d", h=2),
                                      accs[(g - 1) % 2][:, :].rearrange("p (t h d) -> p t h d", t=QT, h=2),
                                      rec0[:, b, hp, :].rearrange("p (t h) -> p t h", h=2).unsqueeze(3)
                                      .broadcast_to([P, QT, 2, DH0]), ALU.mult).then_inc(o_ready, 1)
                elif kind == "w" and item[2] == QT - 1:
                    dve.wait_ge(rstd_ready[1], b + 1)
                    link_all([dve.tensor_scalar(XN[:, 1, m, :], X1[:, m, :], mvx[:, 1, m, 0:1], vex[:, 1, m:m + 1],
                                                ALU.subtract, ALU.mult) for m in tiles])
                    xn = XN[:, 1, r, :]
                    link(dve.tensor_reduce(aq[:, r, 0], xn, AX.X, ALU.max, apply_absolute_value=True))
                    link(dve.tensor_scalar(aq[:, r, 0], aq[:, r, 0], 1e-5, None, ALU.max))
                    link(dve.reciprocal(aq[:, r, 1], aq[:, r, 0]))
                    link_all([dve.tensor_scalar(aq[:, r, 2], aq[:, r, 1], 127.0, None, ALU.mult),
                              dve.tensor_scalar(aq[:, r, 3], aq[:, r, 0], 1.0 / 127, None, ALU.mult)])
                    link_all([dve.tensor_scalar(XN[:, 1, m, :], XN[:, 1, m, :], aq[:, m, 2:3], MAGIC,
                                                ALU.mult, ALU.add) for m in tiles])
                    for m in tiles:
                        dve.tensor_scalar(XN[:, 1, m, :], XN[:, 1, m, :], MAGIC, aq[:, m, 3:4],
                                          ALU.subtract, ALU.mult).then_inc(xn_ready[1], 1)
                elif kind == "f4" and item[2] == QT - 1:
                    dve.wait_ge(rstd_ready[2], b + 1)
                    for m in tiles:
                        normalise(2, X2, m, XN[:, 2, m, :], xn_ready[2])
                elif kind == "a4" and item[3] == 1:
                    m = b * QT + item[2]
                    dve.wait_ge(pv1_done, n)
                    o = accs[m % 2][:, 0:H1 * (DH1 + 1)].rearrange("p (h d) -> p h d", h=H1)
                    link(dve.reciprocal(rec1[:, m, :], o[:, :, DH1]))
                    dve.tensor_tensor(A1[:, m, :].rearrange("p (h d) -> p h d", h=H1), o[:, :, 0:DH1],
                                      rec1[:, m, :].unsqueeze(2).broadcast_to([P, H1, DH1]),
                                      ALU.mult).then_inc(a1_ready, 1)
                elif kind == "a6":
                    dve.wait_ge(rstd_ready[3], b + 1)
                    for m in tiles:
                        normalise(3, X3, m, XN[:, 3, m, :], xn_ready[3])

            walk(first, second, third)


def constants():
    k = np.zeros((P, NCONST), np.float32)
    k[:, K_ID:K_ID + P] = np.eye(P)
    k[:, K_ONE:K_ONE + P] = 1.0
    k[:, K_IOTA:K_IOTA + E1] = np.arange(E1)
    k[:, K_MASK:K_MASK + H1] = np.arange(P)[:, None] // DH1 == np.arange(H1)[None]
    inv_freq = (1.0 / 10000.0 ** (np.arange(0, DH1, 2, dtype=np.float32) / np.float32(DH1))).astype(np.float32)
    half = DH1 // 2
    row = np.arange(P) % DH1
    sign = np.where(row < half, -1.0, 1.0).astype(np.float32)[:, None]
    for n, cos, sin in ((S, K_CQ, K_SQ), (C, K_CK, K_SK)):
        t = np.arange(n, dtype=np.float32) / np.float32(n)
        angle = ((np.float32(10.0) * t)[None, :] * inv_freq[row % half][:, None]).astype(np.float32)
        k[:, cos:cos + n] = np.cos(angle)
        k[:, sin:sin + n] = np.sin(angle) * sign
    return k


def kernel(**inputs):
    import concourse.bacc as bacc
    from concourse.bass_utils import run_bass_kernel_spmd

    a = {n: np.asarray(v) for n, v in inputs.items()}
    swap = np.arange(P) // DH1 * DH1 + (np.arange(P) + DH1 // 2) % DH1
    l1 = {n: a[f"L1_xattn_{n}"] for n in ("Wq", "Wk", "Wv", "Wo", "bq", "bk", "bv", "bo")}
    row = {"gl": a["L0_xattn_gl"], "bl": a["L0_xattn_bl"], "gm": a["L0_xattn_gm"], "bm": a["L0_xattn_bm"],
           "bq": l1["bq"], "bqs": l1["bq"][swap], "bk": l1["bk"], "bks": l1["bk"][swap], "bv": l1["bv"]}
    for n, src, i in (("gx0", "g_xattn", 0), ("gx1", "g_xattn", 1), ("gf0", "g_ffn", 0), ("gf1", "g_ffn", 1)):
        row[n] = np.broadcast_to(a[src][i], (P,))
    cols = np.concatenate([
        np.stack([row[n] for n in COLS], 1),
        a["L0_ffn_conv_w"].reshape(HC, P, 3).transpose(1, 0, 2).reshape(P, 3 * HC),
        a["L0_ffn_conv_b"].reshape(HC, P).T,
        np.full((P, 1), MAGIC, np.float32)], 1)
    ffn = {n: a[f"L1_ffn_{n}"] for n in ("gate_w", "wg", "wu", "wd", "sg", "su", "sd")}
    arrays = {
        "x": a["x"].reshape(NT * P, D), "ctx": a["ctx_1024"].reshape(B * C, D),
        "ctxT": a["ctx_1024"].transpose(2, 0, 1).reshape(D, B * C), "cols": cols,
        "wq": a["L0_xattn_Wq"], "wkv": a["L0_xattn_Wkv"], "wout": a["L0_xattn_Wout"],
        "w1T": a["L0_ffn_w1"].T, "w2T": a["L0_ffn_w2"].T,
        "l1w": np.concatenate([l1["Wq"].T, l1["Wq"][swap].T, l1["Wk"].T, l1["Wk"][swap].T,
                               l1["Wv"].T, l1["Wo"].T], 1),
        "bo": l1["bo"].reshape(1, D),
        "wgu": np.concatenate([ffn["wg"].reshape(MH, D).T, ffn["wu"].reshape(MH, D).T,
                               ffn["sg"].T, ffn["su"].T, ffn["gate_w"].T], 1),
        "wdT": np.concatenate([ffn["wd"].transpose(0, 2, 1).reshape(MH, D), ffn["sd"].T,
                               np.zeros((P - F1, D), np.float32)], 0),
        "const": constants(),
    }
    arrays = {f"in_{n}": np.ascontiguousarray(v) for n, v in arrays.items()}
    nc = bacc.Bacc("TRN2", target_bir_lowering=False, num_devices=1)
    args = [nc.dram_tensor(n, v.shape, mybir.dt.from_np(v.dtype), kind="ExternalInput").ap()
            for n, v in arrays.items()]
    args.append(nc.dram_tensor("out_0", (NT * P, D), F32, kind="ExternalOutput").ap())
    mega_kernel(nc, *args)
    r = run_bass_kernel_spmd(nc, [arrays], core_ids=[0])
    return r.results[0]["out_0"].reshape(B, S, D)
```

```python
from contextlib import ExitStack

import numpy as np

import concourse.bass as bass
from concourse import mybir

F32 = mybir.dt.float32
F32R = mybir.dt.float32r
BF16 = mybir.dt.bfloat16
U32 = mybir.dt.uint32
ALU = mybir.AluOpType
ACT = mybir.ActivationFunctionType
AX = mybir.AxisListType

P = 128
D = 128
B = 2
S = 512
C = 77
QT = S // P
NT = B * QT
H0, DH0 = 8, 64
IN0 = H0 * DH0
KEYS0 = S + C
KP = 5 * P
KEVEN = KEYS0 + 1
KA = 296
K0 = 512 - KA
HID = 512
HC = HID // P
H1, DH1 = 16, 8
HH = H1 // 2
E1, F1 = 8, 64
MH = E1 * F1
MT = MH + F1
EPS = 1e-5
MAGIC = float(1.5 * 2 ** 23)
SLOTS = 3

COLS = ["gl", "bl", "gm", "bm", "bq", "bqs", "bk", "bks", "bv", "gx0", "gx1", "gf0", "gf1"]
CONV_W = len(COLS)
CONV_B = CONV_W + 3 * HC
NCOL = CONV_B + HC + 1
K_ID, K_ONE, K_IOTA, K_MASK = 0, P, 2 * P, 2 * P + E1
K_CQ = K_MASK + H1
K_SQ = K_CQ + S
K_CK = K_SQ + S
K_SK = K_CK + C
NCONST = K_SK + C


def items():
    out = []
    for b in range(B):
        out += [("x0", b), ("q", b, 0), ("k", b, 0)] + [("v", b, j) for j in range(3)]
        for h in range(H0):
            if h + 1 < H0:
                out += [("q", b, (h + 1) // 2)] * (h % 2) + [("k", b, h + 1)]
            out += [("u", b, h, qt) for qt in range(QT)] + [("o", b, h)]
        if b == 0:
            out += [("s", b)]
        out += [("f1", b)] + [("f2", b, c) for c in range(HC)]
        out += [("f3", b, t) for t in range(QT)] + [("f4", b, t) for t in range(QT)]
        out += [("a3", b), ("a1", b), ("a2", b)] + [("a4", b, t, h) for t in range(QT) for h in range(2)]
        out += [("a6", b), ("m1", b), ("m3", b)] + [("m2", b, t) for t in range(QT)]
        out += [("m4", b, t) for t in range(QT)]
    return out


ITEMS = items()
KINDS = {kind: [x for x in ITEMS if x[0] == kind] for kind in dict(x[:1] * 2 for x in ITEMS)}
PLACE = {x: KINDS[x[0]].index(x) + 1 for x in ITEMS}
ENGINE = {"F": "PE", "B": "PE", "T": "PE", "A": "ACT", "D": "DVE", "P": "POOL"}


def upto(item):
    return PLACE[item]


LAST={"x0":"A1","v":"D1","q":"D1","k":"D1","u":"D2","o":"D1","s":"D1","f1":"A1","f2":"D1","f3":"A1","f4":"D2","a3":"D1","a1":"A1","a2":"D1","a4":"D3","a6":"D2","m1":"A1","m3":"D2","m2":"D1","m4":"D2"}


def deps(x):
    k,b=x[0],x[1]; n=PLACE[x]
    def nth(kind,m): return KINDS[kind][m-1]
    S={}
    if k=="x0":
        S["F"]=(1.0,[(("x0",0),"D2")] if b else [])
        S["A1"]=(1.0,["F"])
        if b==0: S["D2"]=(1.6,["F"])
    elif k=="v":
        S["F"]=(1.9 if x[2]<2 else .95,[(("x0",b),"A1")])
        S["A1"]=(1.15 if x[2]<2 else .6,["F"]+([(("u",0,7,3),"T")] if b else []))
        S["D1"]=(1.4 if x[2]<2 else .7,["A1"])
    elif k=="q":
        S["F"]=(.95,[(("x0",b),"A1")])
        S["A1"]=(1.05,["F"]+([(nth("u",8*(n-2)),"B")] if n>2 else []))
        S["D1"]=(1.3,["A1"])
    elif k=="k":
        S["F"]=(1.3,[(("x0",b),"A1")])
        S["A1"]=(.7,["F"]+([(nth("u",4*(n-2)),"B")] if n>2 else []))
        S["D1"]=(.75,["A1"])
        if n==3: S["D2"]=(1.3,[])
    elif k=="u":
        _,b,h,qt=x; g=b*8+h
        S["F"]=(.6,[(("q",b,h//2),"D1"),(("k",b,h),"D1")])
        S["D1"]=(.70,["F"]+([(nth("u",n-3),"A1")] if n>3 else []))
        S["A1"]=(.75,["D1"]+([(nth("u",n-3),"B")] if n>3 else []))
        S["B"]=(.7,["A1"])
        S["A2"]=(.6,["B"]+([(nth("u",2*((n-1)//2-1)),"T")] if n>4 else []))
        S["D2"]=(.75,["A2"])
        if qt%2:
            p=["D2",(("v",b,2),"D1")]
            if qt==1 and g>=2: p.append((nth("u",4*(g-1)),"A3"))
            S["T"]=(1.3,p)
        if qt==3:
            S["A3"]=(.6,["T"]+([(nth("o",n//4-2),"F")] if n//4>2 else []))
    elif k=="o":
        S["F"]=(1.3,[(("u",b,x[2],3),"A3")])
        S["D1"]=(1.6 if x[2]<7 else 3.0,["F"])
        if x[2]==7:
            S["P"]=(1.0,["D1"]); S["D3"]=(4.3,["P"])
    elif k=="s":
        S["F"]=(.3,[(("k",0,2),"D2")]); S["D1"]=(3.2,["F"])
    elif k=="f1":
        S["F"]=(.7,[(("o",b,7),"D3")]); S["A1"]=(.5,["F",(("k",b,7),"F"),(("q",b,3),"F"),(("v",b,2),"F")])
    elif k=="f2":
        S["F"]=(1.1,[(("f1",b),"A1"),(("s",0),"D1")])
        S["A1"]=(.7,["F"]+([(("f3",0,3),"F")] if b else []))
        S["D1"]=(1.5,["A1"]+([(("m2",0,3),"D1")] if b else []))
        S["A2"]=(.55,["D1"]+([(nth("f2",n-2),"D2")] if n>2 else []))
        S["D2"]=(.65,["A2"])
    elif k=="f3":
        S["F"]=(.7,[(("f2",b,3),"D2")]); S["D1"]=(1.4,["F"]); S["A1"]=(.7,["D1"]+([(nth("f3",n-2),"D2")] if n>2 else []))
        S["D2"]=(.4,["A1"]+([(nth("f4",n-4),"A1")] if n>4 else []))
    elif k=="f4":
        S["F"]=(.4,[(("f3",b,x[2]),"D2")]); S["A1"]=(.5,["F"]+([(nth("f4",n-2),"B")] if n>2 else []))
        S["B"]=(.4,["A1"]); S["D2"]=(1.0,["B"])
        if x[2]==3:
            S["P"]=(1.0,["D2"]); S["D3"]=(1.1,["P"])
    elif k=="a3":
        S["F"]=(1.2,[]); S["D1"]=(3.3,["F"]+([(("a4",0,3,1),"F")] if b else []))
    elif k=="a1":
        S["F"]=(.7,[(("f4",b,3),"D3"),(("f2",b,3),"F")]); S["A1"]=(.5,["F"])
    elif k=="a2":
        S["F"]=(2.2,[(("a1",b),"A1")]); S["D1"]=(2.3,["F"]+([(("a4",0,3,1),"F")] if b else []))
    elif k=="a4":
        S["F"]=(1.5,[(("a2",b),"D1"),(("a3",b),"D1")]); S["D1"]=(1.6,["F"]+([(nth("a4",n-3),"B")] if n>3 else []))
        S["A1"]=(.65,["D1"]); S["B"]=(1.1,["A1"]); S["A2"]=(.95,["B"]+([(nth("a4",n-2),"T")] if n>2 else []))
        S["T"]=(2.5,["A2"]); S["D3"]=(.5,["T"]+([(("a6",0),"F")] if b else []))
    elif k=="a6":
        S["F"]=(.7,[(("a4",b,3,1),"D3")]); S["A1"]=(.6,["F"]); S["B"]=(2.2,["A1"]); S["D2"]=(2.2,["B"]); S["P"]=(1.,["D2"]); S["D3"]=(1.1,["P"])
    elif k=="m1":
        S["F"]=(.7,[(("a6",b),"D3")]); S["A1"]=(.5,["F",(("a2",b),"F")])
    elif k=="m3":
        S["F"]=(1.5,[(("m1",b),"A1")]); S["D1"]=(1.3,["F"]); S["A1"]=(.5,["D1"]); S["D2"]=(2.7,["A1"]+([(("m4",0,3),"F")] if b else []))
    elif k=="m2":
        S["F"]=(2.2,[(("m1",b),"A1")]); S["A1"]=(.5,["F"]+([(nth("m2",n-2),"D1")] if n>2 else [])); S["D1"]=(1.35,["A1"]+([(nth("m4",n-4),"F")] if n>4 else []))
        S["P"]=(1.05,["D1",(("m3",b),"D2")])
    elif k=="m4":
        S["F"]=(.7,[(("m2",b,x[2]),"P"),(("m3",b),"D2")]); S["A1"]=(.65+.3,["F"]+([(nth("m4",n-2),"B")] if n>2 else []))
        S["B"]=(1.2,["A1"]); S["D2"]=(.35,["B"])
    return S


def build():
    table, before = {}, {}
    for x in ITEMS:
        for st, (cost, preds) in deps(x).items():
            table[x, st] = [cost, [p if isinstance(p, tuple) else (x, p) for p in preds]]
            if (x[0], st) in before:
                table[x, st][1].append((before[x[0], st], st))
            before[x[0], st] = x
    return table

T=build()
SUCC={t:[] for t in T}
for t,(c,p) in T.items():
    for q in p:
        assert q in T,(t,q)
        SUCC[q].append(t)
def tail_len():
    memo={}
    def f(t):
        if t in memo: return memo[t]
        memo[t]=T[t][0]+.15+max([f(s) for s in SUCC[t]],default=0)
        return memo[t]
    for t in T: f(t)
    return memo
CP=tail_len()
SEM=.15
WIN=.1
def schedule(prio, slots=3, reserve=None):
    left={t:len(p) for t,(c,p) in T.items()}
    ready={e:[] for e in("PE","ACT","DVE","POOL")}
    free={e:0.0 for e in ready}
    slot_free=[0.0]*slots; slot_of={}; occupied=[None]*slots
    fin={}
    rt={t:0.0 for t in T}
    avail={e:set() for e in ready}
    for t in T:
        if left[t]==0: avail[ENGINE[t[1][0]]].add(t)
    order={e:[] for e in ready}
    n=0
    while n<len(T):
        best=None
        for e,av in avail.items():
            if not av: continue
            fs=min([s for i,s in enumerate(slot_free) if occupied[i] is None],default=None)
            cand=[]
            for t in av:
                s=max(free[e],rt[t])
                if t[1]=="F":
                    if fs is None: continue
                    s=max(s,fs)
                cand.append((s,t))
            if not cand: continue
            m=min(s for s,_ in cand)
            s,t=max((c for c in cand if c[0]<=m+WIN),key=lambda c:prio[c[1]])
            if best is None or s<best[0]: best=(s,e,t)
        if best is None: return 1e9,None,None
        s,e,t=best
        x,st=t
        if st=="F":
            i=min((i for i in range(slots) if occupied[i] is None),key=lambda i:slot_free[i])
            occupied[i]=x; slot_of[x]=i
        f=s+T[t][0]; fin[t]=f; free[e]=f; avail[e].discard(t); order[e].append(t); n+=1
        if st==LAST[x[0]]:
            i=slot_of[x]; occupied[i]=None; slot_free[i]=f+SEM
        for q in SUCC[t]:
            left[q]-=1
            r=f+(0.07 if ENGINE[q[1][0]]==e else SEM)
            rt[q]=max(rt[q],r)
            if left[q]==0: avail[ENGINE[q[1][0]]].add(q)
    return max(fin.values()),order,(slot_of,fin)

MAKESPAN, ORDER, (SLOT_OF, _) = schedule(CP)
REAL = [x for x, st in ORDER["PE"] if st == "F"]
NTH = {x: n for n, x in enumerate(REAL)}
HAD = {x: next((y for y in reversed(REAL[:n]) if SLOT_OF[y] == SLOT_OF[x]), None) for n, x in enumerate(REAL)}


def mega_kernel(nc, x, ctx, ctxT, cols, wq, wk, wv, wout, w1T, w2T, l1w, bo, wgu, wdT, const, out):
    stack = ExitStack()
    with stack:
        def sb(name, shape, dt=F32):
            return stack.enter_context(nc.sbuf_tensor(name, shape, dt))

        def sem(name):
            return stack.enter_context(nc.semaphore(name))

        slots = [stack.enter_context(nc.psum_tensor(f"slot{i}", [P, 2 * 512], F32)) for i in range(SLOTS)]
        accs = [stack.enter_context(nc.psum_tensor(f"acc{i}", [P, 512], F32)) for i in range(2)]

        X = sb("X", [P, NT, D])
        CT = sb("CT", [C, B, D])
        CTT = sb("CTT", [P, B, C])
        COL = sb("COL", [P, NCOL])
        WQ = sb("WQ", [P, IN0])
        WK = sb("WK", [P, H0, P])
        WV = sb("WV", [P, IN0])
        WOUT = sb("WOUT", [P, H0, D])
        W1 = sb("W1", [P, HID])
        W2 = sb("W2", [P, HC, D])
        L1W = sb("L1W", [P, 6, D])
        BO = sb("BO", [1, D])
        WGU = sb("WGU", [P, 2 * MT + E1])
        WD = sb("WD", [P, 5, D])
        K = sb("K", [P, NCONST])
        ident, ones = K[:, K_ID:K_ID + P], K[:, K_ONE:K_ONE + P]
        identb = sb("identb", [P, P], BF16)

        bnx = sb("bnx", [P, 4, NT, 6])
        mvx = sb("mvx", [P, 4, NT, 2])
        vex = sb("vex", [P, 4, NT])
        bnc = sb("bnc", [C, B, 6])
        mvc = sb("mvc", [C, B, 2])
        vec = sb("vec", [C, B])
        mhalf = sb("mhalf", [P, NT])
        tg = sb("tg", [P, 4])
        ws = sb("ws", [P, 2, 4])
        cw = sb("cw", [P, 3 * HC])
        g2 = sb("g2", [P, 1])
        aq = sb("aq", [P, NT, 4])
        aq2 = sb("aq2", [P, NT, 4])
        nm0 = sb("nm0", [P, SLOTS])
        sum0 = sb("sum0", [P, B, H0, QT])
        rec0 = sb("rec0", [P, B, H0, QT])
        mx1 = sb("mx1", [P, 4, HH])
        rec1 = sb("rec1", [P, NT, H1])
        lg = sb("lg", [P, NT, E1])
        top = sb("top", [P, NT, 8])
        idx = sb("idx", [P, NT, 8], U32)
        idf = sb("idf", [P, NT, 8])
        rt = sb("rt", [P, NT, 4])
        hot = sb("hot", [P, NT, 2, E1])
        cwt = sb("cwt", [P, NT, E1])

        XN = sb("XN", [P, NT, D])
        CN = sb("CN", [C, B, D])
        LT = sb("LT", [P, B, KEVEN])
        XQT = X2T = X3T = LT[:, :, 0:S]
        Q = sb("Q", [P, 2, 2, S], F32R)
        KH = sb("KH", [P, 2, KEVEN], F32R)
        KL = sb("KL", [P, 2, KEVEN], F32R)
        V = sb("V", [P, 5, H0, 2, DH0], F32R)
        PR = sb("PR", [P, SLOTS, KP])
        PH = sb("PH", [P, 2, 5, 2 * P], F32R)
        PL = sb("PL", [P, 2, 5, 2 * P], F32R)
        OT = sb("OT", [P, 2, S])
        X1 = sb("X1", [P, NT, D])
        X2 = X
        W1Q = sb("W1Q", [P, HID])
        W2Q = sb("W2Q", [P, HC * D], BF16)
        YC = sb("YC", [P, HC, S])
        TH = sb("TH", [P, 2, S])
        QM = sb("QM", [P, 2, HID])
        QB = sb("QB", [P, 4, HID], BF16)
        QBT = sb("QBT", [P, 2, HID], BF16)
        RC = sb("RC", [P, 2, S])
        Q1 = sb("Q1", [P, S])
        K1 = sb("K1", [P, B, C])
        KBD = sb("KBD", [P, H1, C])
        V1 = sb("V1", [C, B, H1, DH1 + 1])
        S1 = sb("S1", [P, 3, HH * C])
        PT1 = sb("PT1", [C, 2, HH * P])
        A1 = sb("A1", [P, QT, D])
        A1T = sb("A1T", [P, S])
        X3 = X1
        HB = TH
        SHT = sb("SHT", [P, QT, F1])
        HM = sb("HM", [P, QT, MT])
        HT = sb("HT", [P, 2, KP])
        Y = X

        names = ["x0", "x1", "ctx", "cols", "wq", "wk", "wv", "const", "wout", "ffn", "l1", "moe"]
        ld = {n: sem(f"ld_{n}") for n in names}
        stored = sem("stored")
        dve_step = sem("dve_step")
        act_step = sem("act_step")
        pool_const = sem("pool_const")
        front_done = sem("front_done")
        var_ready = [sem(f"var_ready{i}") for i in range(4)]
        rstd_ready = [sem(f"rstd_ready{i}") for i in range(4)]
        varc_ready = sem("varc_ready")
        rstdc_ready = sem("rstdc_ready")
        xn_ready = [sem(f"xn_ready{i}") for i in range(4)]
        cn_ready = sem("cn_ready")
        lt_ready = sem("lt_ready")
        v_upper = sem("v_upper")
        v_ready = sem("v_ready")
        q_upper = sem("q_upper")
        q_ready = sem("q_ready")
        k_upper = sem("k_upper")
        k_ready = sem("k_ready")
        max_ready = sem("max_ready")
        prob_ready = sem("prob_ready")
        prob_turned = sem("prob_turned")
        pt_upper = sem("pt_upper")
        pt_ready = sem("pt_ready")
        pv_done = sem("pv_done")
        ot_ready = sem("ot_ready")
        o_added = sem("o_added")
        lt_pad = sem("lt_pad")
        pad_ready = sem("pad_ready")
        identb_ready = sem("identb_ready")
        gates_ready = sem("gates_ready")
        wsum_ready = sem("wsum_ready")
        wmean_ready = sem("wmean_ready")
        w1q_ready = sem("w1q_ready")
        w2q_ready = sem("w2q_ready")
        conv_scaled = sem("conv_scaled")
        xqt_ready = sem("xqt_ready")
        conv_mid = sem("conv_mid")
        conv_done = sem("conv_done")
        tanh_done = sem("tanh_done")
        silu_ready = sem("silu_ready")
        scale_ready = sem("scale_ready")
        rounded = sem("rounded")
        qb_ready = sem("qb_ready")
        qbt_ready = sem("qbt_ready")
        f_done = sem("f_done")
        x2_ready = sem("x2_ready")
        x2t_ready = sem("x2t_ready")
        q1_ready = sem("q1_ready")
        kv1_ready = sem("kv1_ready")
        shifted = sem("shifted")
        exp1_ready = sem("exp1_ready")
        p1_turned = sem("p1_turned")
        pt1_ready = sem("pt1_ready")
        pv1_done = sem("pv1_done")
        a1_ready = sem("a1_ready")
        a1t_ready = sem("a1t_ready")
        ya_done = sem("ya_done")
        x3_ready = sem("x3_ready")
        x3t_ready = sem("x3t_ready")
        logits_copied = sem("logits_copied")
        logits_ready = sem("logits_ready")
        exps_ready = sem("exps_ready")
        shared_tanh = sem("shared_tanh")
        shared_ready = sem("shared_ready")
        weights_ready = sem("weights_ready")
        gate_tanh = sem("gate_tanh")
        hid_ready = sem("hid_ready")
        hidw_ready = sem("hidw_ready")
        ht_ready = sem("ht_ready")
        ym_done = sem("ym_done")
        y_ready = sem("y_ready")
        block = stack.enter_context(nc.Block())

        heads_out = KINDS["o"]

        def value_chunks(j):
            return [(0, 2 * j, P), (1, 2 * j + 1, P)] if j < 2 else [(0, 4, C)]

        def last_read(item):
            n = upto(item)
            return {"u": (pt_ready, n), "x0": (lt_ready, 2 * n), "v": (v_ready, 2 * n - n // 3), "q": (q_ready, 2 * n), "k": (k_ready, n),
                    "s": (wmean_ready, n), "o": (o_added, QT * n), "f1": (xqt_ready, n), "f2": (conv_done, n),
                    "f3": (rounded, n), "f4": (x2_ready, n), "a3": (kv1_ready, n), "a1": (x2t_ready, n),
                    "a2": (q1_ready, n), "a4": (a1_ready, n), "a6": (x3_ready, n), "m1": (x3t_ready, n),
                    "m3": (shared_ready, n), "m2": (hid_ready, n), "m4": (y_ready, n)}[item[0]]

        def slot(item):
            return slots[SLOT_OF[item]]

        def col(name):
            return COL[:, COLS.index(name):COLS.index(name) + 1]

        def walk(engine, stages):
            for item, stage in ORDER[engine]:
                stages[stage](item)

        @block.sync
        def _(sp):
            xv = x.rearrange("(t p) d -> p t d", p=P)
            for b in range(B):
                sp.dma_start(X[:, b * QT:(b + 1) * QT, :], xv[:, b * QT:(b + 1) * QT, :]).then_inc(ld[f"x{b}"], 16)
            sp.dma_start(WV[:], wv).then_inc(ld["wv"], 16)
            sp.dma_start(WK[:], wk.rearrange("p (h c) -> p h c", h=H0)).then_inc(ld["wk"], 16)
            sp.dma_start(W2[:], w2T.rearrange("(c p) d -> p c d", p=P)).then_inc(ld["ffn"], 16)
            sp.dma_start(W1[:], w1T).then_inc(ld["ffn"], 16)
            sp.dma_start(WOUT[:], wout.rearrange("(h p) d -> p h d", p=P)).then_inc(ld["wout"], 16)
            sp.dma_start(L1W[:], l1w.rearrange("p (k d) -> p k d", d=D)).then_inc(ld["l1"], 16)
            sp.dma_start(BO[:], bo).then_inc(ld["l1"], 16)
            sp.dma_start(CTT[:], ctxT.rearrange("p (b c) -> p b c", b=B)).then_inc(ld["l1"], 16)
            sp.dma_start(WGU[:], wgu).then_inc(ld["moe"], 16)
            sp.dma_start(WD[:], wdT.rearrange("(c p) d -> p c d", p=P)).then_inc(ld["moe"], 16)
            ov = out.rearrange("(t p) d -> t p d", p=P)
            for t in range(NT):
                sp.wait_ge(y_ready, t + 1)
                sp.dma_start(ov[t], Y[:, t, :]).then_inc(stored, 16)
            sp.wait_ge(stored, 16 * NT)

        @block.gpsimd
        def _(pool):
            pool.memset(mhalf[:], -0.5).then_inc(pool_const, 1)
            pool.memset(LT[:, :, KEYS0:KEVEN], 0.0).then_inc(lt_pad, 1)
            pool.memset(PR[:], 0.0).then_inc(pad_ready, 1)
            pool.wait_ge(pool_const, 1)

            def rstd(n, b):
                r = slice(b * QT, (b + 1) * QT)
                pool.wait_ge(var_ready[n], b + 1)
                pool.tensor_tensor(vex[:, n, r], vex[:, n, r], mhalf[:, r], ALU.pow).then_inc(rstd_ready[n], 1)

            rstd(0, 0)
            pool.wait_ge(varc_ready, 1)
            pool.tensor_tensor(vec[:], vec[:], mhalf[0:C, 0:B], ALU.pow).then_inc(rstdc_ready, 1)
            rstd(0, 1)

            def stage(item):
                if item[0] in ("o", "f4", "a6"):
                    rstd({"o": 1, "f4": 2, "a6": 3}[item[0]], item[1])
                else:
                    _, b, t = item
                    m = b * QT + t
                    pool.wait_ge(weights_ready, b + 1)
                    pool.wait_ge(hid_ready, m + 1)
                    hm = HM[:, m % QT, 0:MH].rearrange("p (e f) -> p e f", e=E1)
                    pool.tensor_tensor(hm, hm, cwt[:, m, :].unsqueeze(2).broadcast_to([P, E1, F1]),
                                       ALU.mult).then_inc(hidw_ready, 1)

            walk("POOL", {"P": stage})

        @block.tensor
        def _(pe):
            def turn(dst, src, p=P):
                return pe.transpose(dst, src, ident[0:p, 0:p])

            def turn_tiles(W, b, n):
                for t in range(QT):
                    pe.wait_ge(xn_ready[n], b * QT + t + 1)
                    mm = turn(W[:, t * P:(t + 1) * P], XN[:, b * QT + t, :])
                return mm

            def front(item):
                kind, b = item[0], item[1]
                W = slot(item)
                if HAD[item] is not None:
                    pe.wait_ge(*last_read(HAD[item]))
                if kind == "x0":
                    if b == 0:
                        pe.wait_ge(ld["const"], 16)
                    turn_tiles(W, b, 0)
                    pe.wait_ge(cn_ready, b + 1)
                    mm = turn(W[:, S:S + C], CN[:, b, :], C)
                elif kind == "v":
                    j = item[2]
                    pe.wait_ge(lt_ready, 2 * (b + 1))
                    pe.wait_ge(ld["wv"], 16)
                    for n, c, w in value_chunks(j):
                        mm = pe.matmul(W[0:w, n * 512:n * 512 + 512], LT[:, b, c * P:c * P + w], WV[:],
                                       start=True, stop=True)
                elif kind == "q":
                    hp = item[2]
                    pe.wait_ge(lt_ready, 2 * (b + 1))
                    pe.wait_ge(ld["wq"], 16)
                    mm = pe.matmul(W[:, 0:S], WQ[:, hp * P:(hp + 1) * P], LT[:, b, 0:S], start=True, stop=True)
                elif kind == "k":
                    h = item[2]
                    pe.wait_ge(lt_ready, 2 * (b + 1))
                    pe.wait_ge(ld["wk"], 16)
                    pe.wait_ge(lt_pad, 1)
                    pe.matmul(W[:, K0:512], WK[:, h, :], LT[:, b, 0:KA], start=True, stop=True)
                    mm = pe.matmul(W[:, 512:K0 + KEVEN], WK[:, h, :], LT[:, b, KA:KEVEN], start=True, stop=True)
                elif kind == "u":
                    _, b, h, qt = item
                    g = b * H0 + h
                    pe.wait_ge(q_ready, 2 * (g // 2 + 1))
                    pe.wait_ge(k_ready, g + 1)
                    q = Q[:, g // 2 % 2, h % 2, qt * P:(qt + 1) * P]
                    for lo, hi in ((0, KA), (KA, KEVEN)):
                        pe.matmul(W[:, K0 + lo:K0 + hi], q, KH[:, g % 2, lo:hi], start=True, stop=False)
                        mm = pe.matmul(W[:, K0 + lo:K0 + hi], q, KL[:, g % 2, lo:hi], start=False, stop=True)
                elif kind == "o":
                    n = upto(item)
                    pe.wait_ge(ot_ready, n)
                    pe.wait_ge(ld["wout"], 16)
                    for t in range(QT):
                        mm = pe.matmul(W[:, t * D:(t + 1) * D], OT[:, (n - 1) % 2, t * P:(t + 1) * P],
                                       WOUT[:, item[2], :], start=True, stop=True)
                elif kind == "s":
                    pe.wait_ge(wsum_ready, 2)
                    mm = pe.matmul(W[:, 0:2], ones, ws[:, 0, 0:2], start=True, stop=True)
                elif kind == "f1":
                    mm = turn_tiles(W, b, 1)
                elif kind == "f2":
                    c = item[2]
                    pe.wait_ge(xqt_ready, b + 1)
                    pe.wait_ge(w1q_ready, 1)
                    mm = pe.matmul(W[:, 0:S], W1Q[:, c * P:(c + 1) * P], XQT[:, b, :], start=True, stop=True)
                elif kind == "f3":
                    t = item[2]
                    for c in range(HC):
                        pe.wait_ge(silu_ready, upto(("f2", b, c)))
                        mm = turn(W[:, c * P:(c + 1) * P], YC[:, c, t * P:(t + 1) * P])
                elif kind == "f4":
                    n = upto(item)
                    pe.wait_ge(qb_ready, n)
                    pe.wait_ge(identb_ready, 1)
                    Wb = W[:, 0:256].bitcast(BF16)
                    for c in range(HC):
                        mm = pe.transpose(Wb[:, c * P:(c + 1) * P], QB[:, (n - 1) % 4, c * P:(c + 1) * P], identb[:])
                elif kind == "a3":
                    pe.wait_ge(ld["l1"], 48)
                    pe.matmul(W[:, 0:C], L1W[:, 2, :], CTT[:, b, :], start=True, stop=True)
                    pe.matmul(W[:, P:P + C], L1W[:, 3, :], CTT[:, b, :], start=True, stop=True)
                    mm = pe.matmul(W[0:C, 512:512 + D], CTT[:, b, :], L1W[:, 4, :], start=True, stop=True)
                elif kind == "a1":
                    mm = turn_tiles(W, b, 2)
                elif kind == "a2":
                    pe.wait_ge(x2t_ready, b + 1)
                    pe.matmul(W[:, 0:S], L1W[:, 0, :], X2T[:, b, :], start=True, stop=True)
                    mm = pe.matmul(W[:, S:2 * S], L1W[:, 1, :], X2T[:, b, :], start=True, stop=True)
                elif kind == "a4":
                    _, b, t, h = item
                    pe.wait_ge(q1_ready, b + 1)
                    pe.wait_ge(kv1_ready, b + 1)
                    for n in range(2):
                        kk = KBD[:, h * HH + n * 4:h * HH + n * 4 + 4, :]
                        mm = pe.matmul(W[:, n * 512:n * 512 + 4 * C], Q1[:, t * P:(t + 1) * P], kk,
                                       start=True, stop=True)
                elif kind == "a6":
                    for t in range(QT):
                        pe.wait_ge(a1_ready, 2 * (b * QT + t + 1))
                        mm = turn(W[:, t * P:(t + 1) * P], A1[:, t, :])
                elif kind == "m1":
                    mm = turn_tiles(W, b, 3)
                elif kind == "m3":
                    pe.wait_ge(x3t_ready, b + 1)
                    pe.wait_ge(ld["moe"], 32)
                    for t in range(QT):
                        mm = pe.matmul(W[:, t * 256:t * 256 + 2 * F1 + E1], X3T[:, b, t * P:(t + 1) * P],
                                       WGU[:, 2 * MH:], start=True, stop=True)
                elif kind == "m2":
                    t = item[2]
                    pe.wait_ge(x3t_ready, b + 1)
                    pe.wait_ge(ld["moe"], 32)
                    xt = X3T[:, b, t * P:(t + 1) * P]
                    pe.matmul(W[:, 0:MH], xt, WGU[:, 0:MH], start=True, stop=True)
                    mm = pe.matmul(W[:, MH:2 * MH], xt, WGU[:, MH:2 * MH], start=True, stop=True)
                elif kind == "m4":
                    m = b * QT + item[2]
                    pe.wait_ge(hidw_ready, m + 1)
                    pe.wait_ge(shared_ready, b + 1)
                    for c in range(HC):
                        turn(W[:, c * P:(c + 1) * P], HM[:, m % QT, c * P:(c + 1) * P])
                    mm = turn(W[0:F1, 512:512 + P], HM[:, m % QT, MH:MT])
                mm.then_inc(front_done, 1)

            def back(item):
                kind, b = item[0], item[1]
                W = slot(item)
                if kind == "u":
                    n = upto(item)
                    pe.wait_ge(prob_ready, n)
                    pe.wait_ge(pad_ready, 1)
                    for c in range(5):
                        mm = turn(W[:, c * P:(c + 1) * P], PR[:, (n - 1) % SLOTS, c * P:(c + 1) * P])
                    mm.then_inc(prob_turned, 1)
                elif kind == "f4":
                    n = upto(item)
                    pe.wait_ge(qbt_ready, n)
                    pe.wait_ge(w2q_ready, 1)
                    for c in range(HC):
                        mm = pe.matmul(W[:, 512:512 + D], QBT[:, (n - 1) % 2, c * P:(c + 1) * P],
                                       W2Q[:, c * D:(c + 1) * D], start=(c == 0), stop=(c == HC - 1))
                    mm.then_inc(f_done, 1)
                elif kind == "a4":
                    n = upto(item)
                    pe.wait_ge(exp1_ready, n)
                    for h in range(HH):
                        mm = turn(W[0:C, h * P:(h + 1) * P], S1[:, (n - 1) % 3, h * C:(h + 1) * C])
                    mm.then_inc(p1_turned, 1)
                elif kind == "a6":
                    pe.wait_ge(a1t_ready, b + 1)
                    for t in range(QT):
                        o = W[:, 512 + t * D:512 + (t + 1) * D]
                        pe.matmul(o, A1T[:, t * P:(t + 1) * P], L1W[:, 5, :], start=True, stop=False)
                        mm = pe.matmul(o, ones[0:1, :], BO[:], start=False, stop=True)
                    mm.then_inc(ya_done, 1)
                elif kind == "m4":
                    n = upto(item)
                    pe.wait_ge(ht_ready, 2 * n)
                    o = W[:, 640:640 + D]
                    for c in range(HC):
                        pe.matmul(o, HT[:, (n - 1) % 2, c * P:(c + 1) * P], WD[:, c, :], start=(c == 0), stop=False)
                    pe.matmul(o, HT[0:F1, (n - 1) % 2, MH:MH + P], WD[0:F1, 4, :],
                              start=False, stop=True).then_inc(ym_done, 1)

            def tail(item):
                kind, b = item[0], item[1]
                if kind == "u" and item[3] % 2:
                    _, b, h, qt = item
                    n, g = upto(item), b * H0 + h
                    pe.wait_ge(v_ready, 5 * (b + 1))
                    pe.wait_ge(pt_ready, n)
                    if qt == 1 and g >= 2:
                        pe.wait_ge(ot_ready, g - 1)
                    o = accs[g % 2][:, (qt - 1) * P:(qt + 1) * P]
                    s = (n // 2 - 1) % 2
                    for c in range(5):
                        r = P if c < 4 else C
                        v = V[0:r, c, h, :, :].rearrange("p k d -> p (k d)")
                        pe.matmul(o, v, PH[0:r, s, c, :], start=(c == 0), stop=False)
                        mm = pe.matmul(o, v, PL[0:r, s, c, :], start=False, stop=(c == 4))
                    mm.then_inc(pv_done, 1)
                elif kind == "a4":
                    _, b, t, h = item
                    n = upto(item)
                    pe.wait_ge(pt1_ready, n)
                    for e in range(HH):
                        he = h * HH + e
                        mm = pe.matmul(slot(item)[:, e * (DH1 + 1):(e + 1) * (DH1 + 1)],
                                       PT1[:, (n - 1) % 2, e * P:(e + 1) * P], V1[:, b, he, :], start=True, stop=True)
                    mm.then_inc(pv1_done, 1)

            walk("PE", {"F": front, "B": back, "T": tail})

        @block.scalar
        def _(act):
            act.dma_start(K[:], const).then_inc(ld["const"], 16)
            act.dma_start(COL[:], cols).then_inc(ld["cols"], 16)
            act.dma_start(CT[:], ctx.rearrange("(b c) d -> c b d", b=B)).then_inc(ld["ctx"], 16)
            act.dma_start(WQ[:], wq).then_inc(ld["wq"], 16)
            act.wait_ge(ld["cols"], 16)
            act.activation(tg[:], COL[:, COLS.index("gx0"):COLS.index("gx0") + 4], ACT.Tanh).then_inc(gates_ready, 1)

            def first(item):
                kind, b = item[0], item[1]
                W, n = slot(item), upto(item)
                if kind == "u":
                    act.wait_ge(max_ready, n)
                    if n == 1:
                        act.wait_ge(pad_ready, 1)
                    if n > SLOTS:
                        act.wait_ge(prob_turned, n - SLOTS)
                    s, qt = (n - 1) % SLOTS, item[3]
                    act.activation(PR[:, s, 0:KEYS0], W[:, K0:K0 + KEYS0], ACT.Exp, bias=nm0[:, s:s + 1],
                                   accum_out=sum0[:, b, item[2], qt:qt + 1]).then_inc(prob_ready, 1)
                    return
                if kind in ("o", "s", "a2", "a3"):
                    return
                act.wait_ge(front_done, NTH[item] + 1)
                if kind == "x0":
                    act.activation(LT[:, b, 0:S], W[:, 0:S], ACT.Identity, bias=col("bl"),
                                   scale=col("gl")).then_inc(lt_ready, 1)
                    act.activation(LT[:, b, S:KEYS0], W[:, S:KEYS0], ACT.Identity, bias=col("bm"),
                                   scale=col("gm")).then_inc(lt_ready, 1)
                elif kind == "v":
                    if b == 1:
                        act.wait_ge(pv_done, 2 * H0)
                    for n2, c, r in value_chunks(item[2]):
                        act.activation(V[0:r, c, :, 0, :], W[0:r, n2 * 512:n2 * 512 + 512], ACT.Copy).then_inc(v_upper, 1)
                elif kind == "q":
                    if n > 2:
                        act.wait_ge(prob_turned, 8 * (n - 2))
                    for e in range(2):
                        r = slice(e * DH0, (e + 1) * DH0)
                        act.activation(Q[r, (n - 1) % 2, e, :], W[r, 0:S], ACT.Copy,
                                       scale=float(DH0) ** 0.5).then_inc(q_upper, 1)
                elif kind == "k":
                    if n > 2:
                        act.wait_ge(prob_turned, QT * (n - 2))
                    act.activation(KH[:, (n - 1) % 2, :], W[:, K0:K0 + KEVEN], ACT.Copy).then_inc(k_upper, 1)
                elif kind == "f1":
                    act.activation(XQT[:, b, :], W[:, 0:S], ACT.Copy).then_inc(xqt_ready, 1)
                elif kind == "f2":
                    c = item[2]
                    act.wait_ge(conv_scaled, 1)
                    act.activation(YC[:, c, :], W[:, 0:S], ACT.Identity,
                                   bias=COL[:, CONV_B + c:CONV_B + c + 1],
                                   scale=cw[:, 3 * c + 1:3 * c + 2]).then_inc(conv_mid, 1)
                elif kind == "f3":
                    m = b * QT + item[2]
                    act.wait_ge(scale_ready, n)
                    if n > 2:
                        act.wait_ge(qb_ready, n - 2)
                    act.activation(QM[:, (n - 1) % 2, :], W[:, 0:HID], ACT.Identity, bias=COL[:, NCOL - 1:NCOL],
                                   scale=aq2[:, m, 2:3]).then_inc(rounded, 1)
                elif kind == "f4":
                    if n > 2:
                        act.wait_ge(f_done, n - 2)
                    act.activation(QBT[:, (n - 1) % 2, :], W[:, 0:256].bitcast(BF16), ACT.Copy).then_inc(qbt_ready, 1)
                elif kind == "a1":
                    act.activation(X2T[:, b, :], W[:, 0:S], ACT.Copy).then_inc(x2t_ready, 1)
                elif kind == "a4":
                    act.wait_ge(shifted, n)
                    s1 = S1[:, (n - 1) % 3, :]
                    act.activation(s1, s1, ACT.Exp, scale=float(DH1) ** -0.5).then_inc(exp1_ready, 1)
                elif kind == "a6":
                    act.activation(A1T[:, :], W[:, 0:S], ACT.Identity, bias=col("bv")).then_inc(a1t_ready, 1)
                elif kind == "m1":
                    act.activation(X3T[:, b, :], W[:, 0:S], ACT.Copy).then_inc(x3t_ready, 1)
                elif kind == "m3":
                    act.wait_ge(logits_copied, n)
                    act.activation(SHT[:], W[:, :].rearrange("p (t c) -> p t c", t=QT)[:, :, 0:F1], ACT.Tanh,
                                   scale=0.5).then_inc(shared_tanh, 1)
                    act.wait_ge(logits_ready, n)
                    r = slice(b * QT, (b + 1) * QT)
                    act.activation(lg[:, r, :], lg[:, r, :], ACT.Exp).then_inc(exps_ready, 1)
                elif kind == "m2":
                    if n > 2:
                        act.wait_ge(hid_ready, n - 2)
                    act.activation(HB[:, (n - 1) % 2, :], W[:, 0:MH], ACT.Tanh, scale=0.5).then_inc(gate_tanh, 1)
                elif kind == "m4":
                    if n > 2:
                        act.wait_ge(ym_done, n - 2)
                    act.activation(HT[:, (n - 1) % 2, 0:MH], W[:, 0:MH], ACT.Copy).then_inc(ht_ready, 1)
                    act.activation(HT[0:F1, (n - 1) % 2, MH:MH + P], W[0:F1, MH:MH + P],
                                   ACT.Copy).then_inc(ht_ready, 1)

            def second(item):
                kind, b = item[0], item[1]
                W, n = slot(item), upto(item)
                if kind == "u":
                    act.wait_ge(prob_turned, n)
                    if n > 4:
                        act.wait_ge(pv_done, (n - 1) // 2 - 1)
                    qt = item[3]
                    act.activation(PH[:, (n - 1) // 2 % 2, :, qt % 2 * P:(qt % 2 + 1) * P], W[:, 0:KP],
                                   ACT.Copy).then_inc(pt_upper, 1)
                elif kind == "f2":
                    c = item[2]
                    act.wait_ge(conv_done, n)
                    if n > 2:
                        act.wait_ge(silu_ready, n - 2)
                    act.activation(TH[:, (n - 1) % 2, :], YC[:, c, :], ACT.Tanh, scale=0.5).then_inc(tanh_done, 1)
                elif kind == "a4":
                    act.wait_ge(p1_turned, n)
                    if n > 2:
                        act.wait_ge(pv1_done, n - 2)
                    act.activation(PT1[:, (n - 1) % 2, :], W[0:C, :], ACT.Copy).then_inc(pt1_ready, 1)

            def third(item):
                if item[0] == "u" and item[3] == QT - 1:
                    n = upto(item) // QT
                    act.wait_ge(pv_done, 2 * n)
                    if n > 2:
                        act.wait_ge(front_done, NTH[heads_out[n - 3]] + 1)
                    act.activation(OT[:, (n - 1) % 2, :], accs[(n - 1) % 2][:, :], ACT.Copy).then_inc(ot_ready, 1)

            walk("ACT", {"A1": first, "A2": second, "A3": third})

        @block.vector
        def _(dve):
            steps_done = [0]

            def link(ins):
                steps_done[0] += 1
                ins.then_inc(dve_step, 1)
                dve.wait_ge(dve_step, steps_done[0])

            def link_all(instructions):
                for ins in instructions:
                    steps_done[0] += 1
                    ins.then_inc(dve_step, 1)
                dve.wait_ge(dve_step, steps_done[0])

            def stats(n, src, m):
                link(dve.bn_stats(bnx[:, n, m, :], src[:, m, :]))
                return dve.bn_aggr(mvx[:, n, m, :], bnx[:, n, m, :])

            def all_stats(n, src, b):
                tiles = range(b * QT, (b + 1) * QT)
                link_all([dve.bn_stats(bnx[:, n, m, :], src[:, m, :]) for m in tiles])
                link_all([dve.bn_aggr(mvx[:, n, m, :], bnx[:, n, m, :]) for m in tiles])

            def variance(n, b, twice=False):
                r = slice(b * QT, (b + 1) * QT)
                s1, s2 = (1.0 + EPS, EPS * EPS) if twice else (1.0, EPS)
                dve.tensor_scalar(vex[:, n, r], mvx[:, n, r, 1], s1, s2, ALU.mult, ALU.add).then_inc(var_ready[n], 1)

            def normalise(n, src, m, out, signal):
                return dve.tensor_scalar(out, src[:, m, :], mvx[:, n, m, 0:1], vex[:, n, m:m + 1],
                                         ALU.subtract, ALU.mult).then_inc(signal, 1)

            dve.wait_ge(ld["x0"], 16)
            link_all([dve.bn_stats(bnx[:, 0, m, :], X[:, m, :]) for m in range(QT)])
            link_all([dve.bn_aggr(mvx[:, 0, m, :], bnx[:, 0, m, :]) for m in range(QT)])
            variance(0, 0, twice=True)
            dve.wait_ge(ld["ctx"], 16)
            link_all([dve.bn_stats(bnc[:, b, :], CT[:, b, :]) for b in range(B)])
            link_all([dve.bn_aggr(mvc[:, b, :], bnc[:, b, :]) for b in range(B)])
            dve.tensor_scalar(vec[:], mvc[:, :, 1], EPS, None, ALU.add).then_inc(varc_ready, 1)
            dve.wait_ge(rstd_ready[0], 1)
            for m in range(QT):
                normalise(0, X, m, XN[:, m, :], xn_ready[0])
            dve.wait_ge(rstdc_ready, 1)
            for b in range(B):
                dve.tensor_scalar(CN[:, b, :], CT[:, b, :], mvc[:, b, 0:1], vec[:, b:b + 1],
                                  ALU.subtract, ALU.mult).then_inc(cn_ready, 1)
            dve.wait_ge(ld["x1"], 16)
            link_all([dve.bn_stats(bnx[:, 0, m, :], X[:, m, :]) for m in range(QT, NT)])
            link_all([dve.bn_aggr(mvx[:, 0, m, :], bnx[:, 0, m, :]) for m in range(QT, NT)])
            variance(0, 1, twice=True)

            def first(item):
                kind, b = item[0], item[1]
                W, n = slot(item), upto(item)
                r = slice(b * QT, (b + 1) * QT)
                if kind in ("x0", "f1", "f4", "a1", "a6", "m1", "m4"):
                    return
                dve.wait_ge(front_done, NTH[item] + 1)
                if kind == "v":
                    for n2, c, rows in value_chunks(item[2]):
                        dve.wait_ge(v_upper, 5 * b + c + 1)
                        hi = V[0:rows, c, :, 0, :].bitcast(F32)
                        w = W[0:rows, n2 * 512:n2 * 512 + 512].rearrange("p (h d) -> p h d", h=H0)
                        dve.tensor_tensor(V[0:rows, c, :, 1, :], w, hi, ALU.subtract).then_inc(v_ready, 1)
                elif kind == "q":
                    for e in range(2):
                        dve.wait_ge(q_upper, 2 * n - 1 + e)
                        r, o = slice(e * DH0, (e + 1) * DH0), slice((1 - e) * DH0, (2 - e) * DH0)
                        dve.scalar_tensor_tensor(out=Q[o, (n - 1) % 2, e, :], in0=W[r, 0:S], scalar=float(DH0) ** 0.5,
                                                 in1=Q[r, (n - 1) % 2, e, :].bitcast(F32), op0=ALU.mult,
                                                 op1=ALU.subtract).then_inc(q_ready, 1)
                elif kind == "k":
                    dve.wait_ge(k_upper, n)
                    dve.tensor_tensor(KL[:, (n - 1) % 2, :], W[:, K0:K0 + KEVEN], KH[:, (n - 1) % 2, :].bitcast(F32),
                                      ALU.subtract).then_inc(k_ready, 1)
                elif kind == "u":
                    s = (n - 1) % SLOTS
                    if n > SLOTS:
                        dve.wait_ge(prob_ready, n - SLOTS)
                    dve.tensor_reduce(nm0[:, s:s + 1], W[:, K0:K0 + KEYS0], AX.X, ALU.max,
                                      negate=True).then_inc(max_ready, 1)
                elif kind == "o":
                    h = item[2]
                    rec = rec0[:, b, h, :]
                    dve.wait_ge(prob_ready, QT * n)
                    link(dve.reciprocal(rec, sum0[:, b, h, :]))
                    dve.wait_ge(gates_ready, 1)
                    link(dve.tensor_scalar(rec, rec, tg[:, 0:1], None, ALU.mult))
                    if n > 1:
                        dve.wait_ge(o_added, QT * (n - 1))
                    for t in range(QT):
                        m = b * QT + t
                        dve.scalar_tensor_tensor(out=X1[:, m, :], in0=W[:, t * D:(t + 1) * D], scalar=rec[:, t:t + 1],
                                                 in1=(X1 if h else X)[:, m, :], op0=ALU.mult,
                                                 op1=ALU.add).then_inc(o_added, 1)
                    if h == H0 - 1:
                        dve.wait_ge(o_added, QT * n)
                        all_stats(1, X1, b)
                        variance(1, b)
                elif kind == "s":
                    dve.tensor_scalar(ws[:, 1, 0:2], W[:, 0:2], 1.0 / (HID * D), 1e-5,
                                      ALU.mult, ALU.max).then_inc(wmean_ready, 1)
                    dve.wait_ge(wmean_ready, 1)
                    link(dve.reciprocal(ws[:, 1, 2:4], ws[:, 1, 0:2]))
                    w2f = W2[:].rearrange("p c d -> p (c d)")
                    link_all([dve.tensor_scalar(w, w, ws[:, 1, 2 + k:3 + k], MAGIC, ALU.mult, ALU.add)
                              for k, w in enumerate((W1[:], w2f))])
                    link_all([dve.tensor_scalar(w, w, MAGIC, 1.0, ALU.subtract, ALU.min) for w in (W1[:], w2f)])
                    dve.tensor_scalar(W1Q[:], W1[:], -1.0, None, ALU.max).then_inc(w1q_ready, 1)
                    dve.tensor_scalar(W2Q[:], w2f, -1.0, None, ALU.max).then_inc(w2q_ready, 1)
                    dve.tensor_scalar(cw[:], COL[:, CONV_W:CONV_W + 3 * HC], ws[:, 1, 0:1], None,
                                      ALU.mult).then_inc(conv_scaled, 1)
                    dve.wait_ge(gates_ready, 1)
                    link(dve.tensor_tensor(g2[:], tg[:, 2:3], ws[:, 1, 1:2], ALU.mult))
                elif kind == "f2":
                    c = item[2]
                    y = YC[:, c, :]
                    dve.wait_ge(conv_mid, n)
                    link(dve.scalar_tensor_tensor(out=y[:, 1:S], in0=W[:, 0:S - 1], scalar=cw[:, 3 * c:3 * c + 1],
                                                  in1=y[:, 1:S], op0=ALU.mult, op1=ALU.add))
                    dve.scalar_tensor_tensor(out=y[:, 0:S - 1], in0=W[:, 1:S], scalar=cw[:, 3 * c + 2:3 * c + 3],
                                             in1=y[:, 0:S - 1], op0=ALU.mult, op1=ALU.add).then_inc(conv_done, 1)
                elif kind == "f3":
                    m = b * QT + item[2]
                    a = aq2[:, m, :]
                    link(dve.tensor_reduce(a[:, 0:1], W[:, 0:HID], AX.X, ALU.max, apply_absolute_value=True))
                    link(dve.tensor_scalar(a[:, 0:1], a[:, 0:1], 0.5, 1e-5, ALU.mult, ALU.max))
                    link(dve.reciprocal(a[:, 1:2], a[:, 0:1]))
                    dve.tensor_scalar(a[:, 2:3], a[:, 1:2], 127.0 / 2, None, ALU.mult).then_inc(scale_ready, 1)
                    link(dve.tensor_scalar(a[:, 3:4], a[:, 0:1], 1.0 / 127, g2[:, 0:1], ALU.mult, ALU.mult))
                elif kind == "a3":
                    dve.wait_ge(ld["cols"], 16)
                    dve.wait_ge(ld["const"], 16)
                    link(dve.tensor_copy(V1[:, b, :, 0:DH1],
                                         W[0:C, 512:512 + D].rearrange("p (h d) -> p h d", h=H1)))
                    link(dve.memset(V1[:, b, :, DH1:DH1 + 1], 1.0))
                    link_all([dve.scalar_tensor_tensor(out=RC[:, k, 0:C], in0=W[:, k * P:k * P + C],
                                                       scalar=col(("bk", "bks")[k]), in1=K[:, o:o + C],
                                                       op0=ALU.add, op1=ALU.mult) for k, o in enumerate((K_CK, K_SK))])
                    link(dve.tensor_tensor(K1[:, b, :], RC[:, 0, 0:C], RC[:, 1, 0:C], ALU.add))
                    dve.tensor_tensor(KBD[:], K1[:, b, :].unsqueeze(1).broadcast_to([P, H1, C]),
                                      K[:, K_MASK:K_MASK + H1].unsqueeze(2).broadcast_to([P, H1, C]),
                                      ALU.mult).then_inc(kv1_ready, 1)
                elif kind == "a2":
                    link_all([dve.scalar_tensor_tensor(out=RC[:, k, :], in0=W[:, k * S:(k + 1) * S],
                                                       scalar=col(("bq", "bqs")[k]), in1=K[:, o:o + S],
                                                       op0=ALU.add, op1=ALU.mult) for k, o in enumerate((K_CQ, K_SQ))])
                    dve.tensor_tensor(Q1[:, :], RC[:, 0, :], RC[:, 1, :], ALU.add).then_inc(q1_ready, 1)
                elif kind == "a4":
                    w = W[:, :].rearrange("p (k c) -> p k c", k=2)[:, :, 0:4 * C].rearrange("p k (h c) -> p k h c", c=C)
                    s = (n - 1) % 3
                    mx = mx1[:, s, :].rearrange("p (k h) -> p k h", k=2)
                    link(dve.tensor_reduce(mx, w, AX.X, ALU.max))
                    if n > 3:
                        dve.wait_ge(p1_turned, n - 3)
                    dve.tensor_tensor(S1[:, s, :].rearrange("p (k h c) -> p k h c", k=2, c=C), w,
                                      mx.unsqueeze(3).broadcast_to([P, 2, 4, C]), ALU.subtract).then_inc(shifted, 1)
                elif kind == "m3":
                    wv = W[:, :].rearrange("p (t c) -> p t c", t=QT)
                    dve.tensor_copy(lg[:, r, :], wv[:, :, 2 * F1:2 * F1 + E1]).then_inc(logits_copied, 1)
                    dve.wait_ge(logits_copied, n)
                    link_all([dve.max(top[:, m, :], lg[:, m, :]) for m in range(b * QT, (b + 1) * QT)])
                    link_all([dve.max_index(idx[:, m, :], top[:, m, :], lg[:, m, :])
                              for m in range(b * QT, (b + 1) * QT)])
                    dve.tensor_tensor(lg[:, r, :], lg[:, r, :], top[:, r, 0:1].broadcast_to([P, QT, E1]),
                                      ALU.subtract).then_inc(logits_ready, 1)
                elif kind == "m2":
                    m = b * QT + item[2]
                    dve.wait_ge(gate_tanh, n)
                    link(dve.scalar_tensor_tensor(out=HM[:, m % QT, 0:MH], in0=HB[:, (n - 1) % 2, :], scalar=1.0,
                                                  in1=W[:, 0:MH], op0=ALU.add, op1=ALU.mult))
                    dve.tensor_tensor(HM[:, m % QT, 0:MH], HM[:, m % QT, 0:MH], W[:, MH:2 * MH], ALU.mult).then_inc(hid_ready, 1)

            def second(item):
                kind, b = item[0], item[1]
                W, n = slot(item), upto(item)
                if kind == "x0" and b == 0:
                    dve.wait_ge(rstd_ready[0], 2)
                    for m in range(QT, NT):
                        normalise(0, X, m, XN[:, m, :], xn_ready[0])
                    dve.wait_ge(ld["const"], 16)
                    dve.tensor_copy(identb[:], ident).then_inc(identb_ready, 1)
                elif kind == "k" and n == 3:
                    dve.wait_ge(ld["ffn"], 32)
                    dve.tensor_reduce(ws[:, 0, 0:1], W1[:], AX.X, ALU.add,
                                      apply_absolute_value=True).then_inc(wsum_ready, 1)
                    dve.tensor_reduce(ws[:, 0, 1:2], W2[:].rearrange("p c d -> p (c d)"), AX.X, ALU.add,
                                      apply_absolute_value=True).then_inc(wsum_ready, 1)
                elif kind == "u":
                    dve.wait_ge(pt_upper, n)
                    qt, s = item[3], (n - 1) // 2 % 2
                    cols2 = slice(qt % 2 * P, (qt % 2 + 1) * P)
                    dve.tensor_tensor(PL[:, s, :, cols2], W[:, 0:KP].rearrange("p (c q) -> p c q", c=5),
                                      PH[:, s, :, cols2].bitcast(F32), ALU.subtract).then_inc(pt_ready, 1)
                elif kind == "f2":
                    c = item[2]
                    dve.wait_ge(tanh_done, n)
                    dve.scalar_tensor_tensor(out=YC[:, c, :], in0=TH[:, (n - 1) % 2, :], scalar=1.0,
                                             in1=YC[:, c, :], op0=ALU.add, op1=ALU.mult).then_inc(silu_ready, 1)
                elif kind == "f3":
                    dve.wait_ge(rounded, n)
                    if n > 4:
                        dve.wait_ge(qbt_ready, n - 4)
                    dve.tensor_scalar(QB[:, (n - 1) % 4, :], QM[:, (n - 1) % 2, :], MAGIC, None,
                                      ALU.subtract).then_inc(qb_ready, 1)
                elif kind == "f4":
                    m = b * QT + item[2]
                    dve.wait_ge(f_done, n)
                    dve.scalar_tensor_tensor(out=X2[:, m, :], in0=W[:, 512:512 + D], scalar=aq2[:, m, 3:4],
                                             in1=X1[:, m, :], op0=ALU.mult, op1=ALU.add).then_inc(x2_ready, 1)
                    dve.wait_ge(x2_ready, n)
                    link(stats(2, X2, m))
                    if item[2] == QT - 1:
                        variance(2, b)
                elif kind == "m3":
                    r = slice(b * QT, (b + 1) * QT)
                    wv = W[:, :].rearrange("p (t c) -> p t c", t=QT)
                    link(dve.tensor_copy(idf[:, r, 0:2], idx[:, r, 0:2]))
                    iota = K[:, K_IOTA:K_IOTA + E1].unsqueeze(1).broadcast_to([P, QT, E1])
                    link_all([dve.tensor_tensor(hot[:, r, k, :], iota, idf[:, r, k:k + 1].broadcast_to([P, QT, E1]),
                                                ALU.is_equal) for k in range(2)])
                    link(dve.tensor_tensor(hot[:, r, 0, :], hot[:, r, 0, :], hot[:, r, 1, :], ALU.add))
                    dve.wait_ge(shared_tanh, n)
                    sh = HM[:, :, MH:MT]
                    link(dve.scalar_tensor_tensor(out=sh, in0=SHT[:], scalar=1.0, in1=wv[:, :, 0:F1],
                                                  op0=ALU.add, op1=ALU.mult))
                    link(dve.scalar_tensor_tensor(out=sh, in0=sh, scalar=0.5, in1=wv[:, :, F1:2 * F1],
                                                  op0=ALU.mult, op1=ALU.mult))
                    dve.wait_ge(exps_ready, n)
                    link(dve.tensor_reduce(rt[:, r, 0], lg[:, r, :], AX.X, ALU.add))
                    link(dve.reciprocal(rt[:, r, 1], rt[:, r, 0]))
                    link(dve.scalar_tensor_tensor(out=cwt[:, r, :], in0=lg[:, r, :], scalar=0.5, in1=hot[:, r, 0, :],
                                                  op0=ALU.mult, op1=ALU.mult))
                    dve.tensor_tensor(cwt[:, r, :], cwt[:, r, :], rt[:, r, 1:2].broadcast_to([P, QT, E1]),
                                      ALU.mult).then_inc(weights_ready, 1)
                    dve.wait_ge(weights_ready, n)
                    dve.sem_inc(shared_ready, 1)
                elif kind == "a6":
                    r = slice(b * QT, (b + 1) * QT)
                    dve.wait_ge(ya_done, n)
                    dve.scalar_tensor_tensor(out=X3[:, r, :], in0=W[:, 512:1024].rearrange("p (t d) -> p t d", t=QT),
                                             scalar=tg[:, 1:2], in1=X2[:, r, :], op0=ALU.mult,
                                             op1=ALU.add).then_inc(x3_ready, 1)
                    dve.wait_ge(x3_ready, n)
                    all_stats(3, X3, b)
                    variance(3, b)
                elif kind == "m4":
                    m = b * QT + item[2]
                    dve.wait_ge(ym_done, n)
                    dve.scalar_tensor_tensor(out=Y[:, m, :], in0=W[:, 640:640 + D], scalar=tg[:, 3:4],
                                             in1=X3[:, m, :], op0=ALU.mult, op1=ALU.add).then_inc(y_ready, 1)

            def third(item):
                kind, b = item[0], item[1]
                n = upto(item)
                tiles = range(b * QT, (b + 1) * QT)
                r = slice(b * QT, (b + 1) * QT)
                if kind == "o" and item[2] == H0 - 1:
                    dve.wait_ge(rstd_ready[1], b + 1)
                    link_all([dve.tensor_scalar(XN[:, m, :], X1[:, m, :], mvx[:, 1, m, 0:1], vex[:, 1, m:m + 1],
                                                ALU.subtract, ALU.mult) for m in tiles])
                    xn = XN[:, r, :]
                    link(dve.tensor_reduce(aq[:, r, 0], xn, AX.X, ALU.max, apply_absolute_value=True))
                    link(dve.tensor_scalar(aq[:, r, 0], aq[:, r, 0], 1e-5, None, ALU.max))
                    link(dve.reciprocal(aq[:, r, 1], aq[:, r, 0]))
                    link_all([dve.tensor_scalar(aq[:, r, 2], aq[:, r, 1], 127.0, None, ALU.mult),
                              dve.tensor_scalar(aq[:, r, 3], aq[:, r, 0], 1.0 / 127, None, ALU.mult)])
                    link_all([dve.tensor_scalar(XN[:, m, :], XN[:, m, :], aq[:, m, 2:3], MAGIC,
                                                ALU.mult, ALU.add) for m in tiles])
                    for m in tiles:
                        dve.tensor_scalar(XN[:, m, :], XN[:, m, :], MAGIC, aq[:, m, 3:4],
                                          ALU.subtract, ALU.mult).then_inc(xn_ready[1], 1)
                elif kind == "f4" and item[2] == QT - 1:
                    dve.wait_ge(rstd_ready[2], b + 1)
                    for m in tiles:
                        normalise(2, X2, m, XN[:, m, :], xn_ready[2])
                elif kind == "a4":
                    m, h = b * QT + item[2], item[3]
                    dve.wait_ge(pv1_done, n)
                    o = slot(item)[:, 0:HH * (DH1 + 1)].rearrange("p (h d) -> p h d", h=HH)
                    rec = rec1[:, m, h * HH:(h + 1) * HH]
                    link(dve.reciprocal(rec, o[:, :, DH1]))
                    dve.tensor_tensor(A1[:, item[2], h * HH * DH1:(h + 1) * HH * DH1].rearrange("p (h d) -> p h d", h=HH),
                                      o[:, :, 0:DH1], rec.unsqueeze(2).broadcast_to([P, HH, DH1]),
                                      ALU.mult).then_inc(a1_ready, 1)
                elif kind == "a6":
                    dve.wait_ge(rstd_ready[3], b + 1)
                    for m in tiles:
                        normalise(3, X3, m, XN[:, m, :], xn_ready[3])

            walk("DVE", {"D1": first, "D2": second, "D3": third})


def constants():
    k = np.zeros((P, NCONST), np.float32)
    k[:, K_ID:K_ID + P] = np.eye(P)
    k[:, K_ONE:K_ONE + P] = 1.0
    k[:, K_IOTA:K_IOTA + E1] = np.arange(E1)
    k[:, K_MASK:K_MASK + H1] = np.arange(P)[:, None] // DH1 == np.arange(H1)[None]
    inv_freq = (1.0 / 10000.0 ** (np.arange(0, DH1, 2, dtype=np.float32) / np.float32(DH1))).astype(np.float32)
    half = DH1 // 2
    row = np.arange(P) % DH1
    sign = np.where(row < half, -1.0, 1.0).astype(np.float32)[:, None]
    for n, cos, sin in ((S, K_CQ, K_SQ), (C, K_CK, K_SK)):
        t = np.arange(n, dtype=np.float32) / np.float32(n)
        angle = ((np.float32(10.0) * t)[None, :] * inv_freq[row % half][:, None]).astype(np.float32)
        k[:, cos:cos + n] = np.cos(angle)
        k[:, sin:sin + n] = np.sin(angle) * sign
    return k


def kernel(**inputs):
    import concourse.bacc as bacc
    from concourse.bass_utils import run_bass_kernel_spmd

    a = {n: np.asarray(v) for n, v in inputs.items()}
    swap = np.arange(P) // DH1 * DH1 + (np.arange(P) + DH1 // 2) % DH1
    l1 = {n: a[f"L1_xattn_{n}"] for n in ("Wq", "Wk", "Wv", "Wo", "bq", "bk", "bv", "bo")}
    row = {"gl": a["L0_xattn_gl"], "bl": a["L0_xattn_bl"], "gm": a["L0_xattn_gm"], "bm": a["L0_xattn_bm"],
           "bq": l1["bq"], "bqs": l1["bq"][swap], "bk": l1["bk"], "bks": l1["bk"][swap], "bv": l1["bv"]}
    for n, src, i in (("gx0", "g_xattn", 0), ("gx1", "g_xattn", 1), ("gf0", "g_ffn", 0), ("gf1", "g_ffn", 1)):
        row[n] = np.broadcast_to(a[src][i], (P,))
    cols = np.concatenate([
        np.stack([row[n] for n in COLS], 1),
        a["L0_ffn_conv_w"].reshape(HC, P, 3).transpose(1, 0, 2).reshape(P, 3 * HC),
        a["L0_ffn_conv_b"].reshape(HC, P).T,
        np.full((P, 1), MAGIC, np.float32)], 1)
    ffn = {n: a[f"L1_ffn_{n}"] for n in ("gate_w", "wg", "wu", "wd", "sg", "su", "sd")}
    arrays = {
        "x": a["x"].reshape(NT * P, D), "ctx": a["ctx_1024"].reshape(B * C, D),
        "ctxT": a["ctx_1024"].transpose(2, 0, 1).reshape(D, B * C), "cols": cols,
        "wq": a["L0_xattn_Wq"],
        "wk": np.repeat(a["L0_xattn_Wkv"][:, :IN0].reshape(D, H0, 1, DH0), 2, 2).reshape(D, H0 * P),
        "wv": a["L0_xattn_Wkv"][:, IN0:],
        "wout": np.repeat(a["L0_xattn_Wout"].reshape(H0, 1, DH0, D), 2, 1).reshape(H0 * P, D),
        "w1T": a["L0_ffn_w1"].T, "w2T": a["L0_ffn_w2"].T,
        "l1w": np.concatenate([l1["Wq"].T, l1["Wq"][swap].T, l1["Wk"].T, l1["Wk"][swap].T,
                               l1["Wv"].T, l1["Wo"].T], 1),
        "bo": l1["bo"].reshape(1, D),
        "wgu": np.concatenate([ffn["wg"].reshape(MH, D).T, ffn["wu"].reshape(MH, D).T,
                               ffn["sg"].T, ffn["su"].T, ffn["gate_w"].T], 1),
        "wdT": np.concatenate([ffn["wd"].transpose(0, 2, 1).reshape(MH, D), ffn["sd"].T,
                               np.zeros((P - F1, D), np.float32)], 0),
        "const": constants(),
    }
    arrays = {f"in_{n}": np.ascontiguousarray(v) for n, v in arrays.items()}
    nc = bacc.Bacc("TRN2", target_bir_lowering=False, num_devices=1)
    args = [nc.dram_tensor(n, v.shape, mybir.dt.from_np(v.dtype), kind="ExternalInput").ap()
            for n, v in arrays.items()]
    args.append(nc.dram_tensor("out_0", (NT * P, D), F32, kind="ExternalOutput").ap())
    mega_kernel(nc, *args)
    r = run_bass_kernel_spmd(nc, [arrays], core_ids=[0])
    return r.results[0]["out_0"].reshape(B, S, D)
```

```python
from contextlib import ExitStack

import numpy as np

import concourse.bass as bass
from concourse import mybir

F32 = mybir.dt.float32
F32R = mybir.dt.float32r
BF16 = mybir.dt.bfloat16
U32 = mybir.dt.uint32
ALU = mybir.AluOpType
ACT = mybir.ActivationFunctionType
AX = mybir.AxisListType

P = 128
D = 128
B = 2
S = 512
C = 77
QT = S // P
NT = B * QT
H0, DH0 = 8, 64
IN0 = H0 * DH0
KEYS0 = S + C
KP = 5 * P
KEVEN = KEYS0 + 1
KA = 296
K0 = 512 - KA
HID = 512
HC = HID // P
H1, DH1 = 16, 8
HH = H1 // 2
KC1 = -(-HH * C // P)
KP1 = KC1 * P
E1, F1 = 8, 64
MH = E1 * F1
MT = MH + F1
EPS = 1e-5
MAGIC = float(1.5 * 2 ** 23)
PAIRS, SINGLES = 3, 2
RING = 3
PARTS = 2
TP = QT // PARTS
N = TP * P

COLS = ["gl", "bl", "gm", "bm", "bq", "bqs", "bk", "bks", "bv", "gx0", "gx1", "gf0", "gf1"]
CONV_W = len(COLS)
CONV_B = CONV_W + 3 * HC
NCOL = CONV_B + HC + 1
K_ID, K_ONE, K_IOTA, K_MASK = 0, P, 2 * P, 2 * P + E1
K_BLOCK = K_MASK + H1
K_CQ = K_BLOCK + KC1 * HH
K_SQ = K_CQ + S
K_CK = K_SQ + S
K_SK = K_CK + C
NCONST = K_SK + C


def items():
    out = []
    for b in range(B):
        out += [("x0", b), ("q", b, 0), ("k", b, 0)] + [("v", b, j) for j in range(3)]
        for h in range(H0):
            if h + 1 < H0:
                out += [("q", b, (h + 1) // 2)] * (h % 2) + [("k", b, h + 1)]
            out += [("u", b, h, qt) for qt in range(QT)] + [("w", b, h, j) for j in range(2)] + [("o", b, h)]
        if b == 0:
            out += [("s", b)]
        out += [("f1", b)] + [("f2", b, c) for c in range(HC)]
        out += [("f3", b, t) for t in range(QT)] + [("f4", b, t) for t in range(QT)]
        out += [("a3", b)] + [("a4", b, t, h) for t in range(QT) for h in range(2)]
        out += [(kind, b, p) for kind in ("a1", "a2", "a6", "m1", "m3") for p in range(PARTS)]
        out += [("m2", b, t) for t in range(QT)]
        out += [("m4", b, t) for t in range(QT)]
    return out


ITEMS = items()
KINDS = {kind: [x for x in ITEMS if x[0] == kind] for kind in dict(x[:1] * 2 for x in ITEMS)}
PLACE = {x: KINDS[x[0]].index(x) + 1 for x in ITEMS}


def upto(item):
    return PLACE[item]


PLAN = """
x0:F0 x0:A1 v:F0 v:F1 v:A1 x0:D2 v:F2 v:A1 v:D1 q:F3 v:A1 q:F4 q:A1 v:D1 k:F0 q:A1 v:D1 k:F1 k:A1 q:D1
x0:F2 k:A1 k:D1 x0:A1 k:D1 u:F0 u:F2 u:D1 u:F1 u:D1 u:A1 u:D1 u:A1 u:B q:D1 u:A1 u:B u:A2 u:B k:D2 u:A2
u:A2 u:D2 s:F3 u:D2 u:F0 u:D1 w:F4 u:D2 u:A1 u:F2 s:D1 w:A1 u:F1 u:B u:A2 u:D2 u:D1 w:F3 u:D1 u:A1 u:F0
o:D1 u:A1 u:B u:D1 w:A1 u:B u:A1 o:F3 u:A2 u:B u:A2 u:D2 u:A2 u:D2 u:F2 o:A1 u:D1 k:F1 u:D2 u:A1 o:P1
w:F3 k:A1 o:D1 u:B w:A1 k:D1 k:F0 u:A2 u:D2 u:F1 k:A1 q:F3 u:D1 u:F2 q:A1 k:D1 w:F4 u:D1 u:A1 u:F0 q:D1
u:A1 u:B w:A1 u:B u:D1 u:A2 o:F3 u:A2 u:D2 u:A1 u:D2 u:F1 o:A1 u:B u:D1 w:F4 u:A1 o:P1 u:F2 u:A2 o:D1
u:B u:D1 w:A1 u:A2 u:D2 u:A1 u:D2 u:F0 u:B u:D1 k:F1 u:A2 u:A1 u:D2 w:F3 k:A1 u:F2 w:A1 k:D1 u:B u:D1
o:F3 u:A2 u:A1 u:F1 u:D2 o:A1 u:B u:D1 w:F4 u:A1 o:P1 u:F0 u:A2 o:D1 u:B u:D1 w:A1 q:F3 u:A2 u:D2 u:A1
u:D2 u:F2 q:A1 u:B u:D1 w:F4 u:A2 q:D1 u:A1 u:F1 w:A1 u:D2 u:B o:F3 u:D1 u:A2 u:F0 u:D2 u:A1 u:D1 o:A1
w:F4 u:B u:A1 o:P1 k:F2 u:A2 o:D1 w:A1 u:D2 u:B k:A1 k:F1 u:A2 k:D1 u:D2 u:F2 k:A1 u:D1 u:F0 w:F3 u:D1
u:A1 k:D1 u:A1 u:B u:F1 u:A2 u:B u:D1 w:A1 u:A2 o:F3 u:D2 u:A1 u:D2 u:F2 o:A1 u:B u:D1 w:F4 u:A1 o:P1
u:F0 u:A2 o:D1 u:B w:A1 u:D1 q:F3 u:A2 u:D2 u:A1 u:D2 u:F1 q:A1 u:B u:D1 k:F2 u:A2 q:D1 u:A1 w:F4 k:A1
u:D2 u:B w:A1 k:D1 u:F0 u:A2 o:F3 u:D1 u:D2 u:F2 u:A1 u:D1 w:F4 o:A1 u:F1 u:A1 o:P1 u:B u:D1 w:A1 u:B
u:A2 o:D1 u:A2 u:D2 u:A1 u:D2 u:F0 u:B u:D1 w:F3 u:A2 u:A1 u:D2 u:F2 w:A1 u:F1 u:D1 o:F3 u:D1 u:A1 u:B
u:A1 u:B u:A2 o:D1 u:B u:A2 u:D2 q:F4 u:A2 u:D2 k:F0 q:A1 u:D2 k:F2 k:A1 q:D1 o:A1 w:F1 k:D1 k:A1 w:F4
o:P1 w:A1 k:D1 u:F0 w:A1 u:F1 u:D1 o:F3 u:D1 u:A1 a3:F2 o:D2 u:A1 u:B u:B u:A2 a3:D1 o:P2 u:A2 u:D2 v:F2
a3:P1 u:D2 o:D3 v:F0 v:A1 v:F1 v:A1 v:A1 v:D1 f1:F3 f1:A1 v:D1 u:F2 f2:F3 u:D1 u:F0 f2:A1 v:D1 f2:F4
u:A1 u:D1 w:F1 f2:A1 f2:D1 u:A1 u:B w:A1 u:B o:D1 u:A2 f2:D1 u:F1 u:A2 f2:F3 f2:A2 u:D2 f2:A2 f2:F4
f2:A1 u:D2 u:F2 f2:A1 u:D1 w:F0 u:D1 u:A1 f2:D1 w:A1 u:B u:A1 u:F0 u:A2 u:B u:D1 o:F3 u:A2 u:D2 u:A1
u:D2 u:F1 o:A1 u:B u:D1 w:F2 f2:D1 u:A1 o:P1 u:A2 u:B o:D1 w:A1 q:F3 u:D2 u:A2 k:F2 f2:D2 q:A1 u:D2 k:F0
k:A1 q:D1 f2:A2 w:F4 k:A1 k:D1 w:A1 k:D1 u:F1 u:F2 u:D1 u:F0 u:D1 u:A1 o:F3 u:D1 u:A1 u:B f2:D2 u:A1 u:B
f2:D2 u:A2 u:B u:A2 u:D2 u:A2 u:D2 u:F1 o:A1 u:D2 w:F4 u:D1 f2:A2 o:P1 u:F0 w:A1 f2:D2 u:A1 u:F2 u:D1
f3:F3 u:D1 u:A1 u:B o:D1 f3:F4 u:A1 f3:D1 u:B u:A2 u:B f3:A1 u:D2 u:A2 f3:D2 k:F1 f3:D1 u:A2 f4:F3 k:A1
u:D2 f4:A1 u:D2 f3:A1 w:F0 k:D1 u:F2 w:A1 f3:D2 u:F1 u:D1 f4:F4 u:D1 f4:B u:A1 o:F0 f4:D2 f4:A1 u:A1 u:B
f4:B u:A2 o:D1 u:B f4:D2 o:A1 q:F3 u:D2 w:F4 f4:P2 u:A2 q:A1 u:D2 o:P1 u:F0 f4:D3 u:F2 w:A1 k:F1 u:D1
u:D1 u:A1 w:F4 q:D1 u:A1 u:B w:A1 u:B u:A2 o:F3 u:A2 u:D2 k:A1 a1:F4 u:D2 u:F0 a1:A1 o:A1 u:D1 u:F2
a2:F4 u:D1 u:A1 o:P1 k:D1 f3:F3 u:A1 a2:D1 u:B u:B u:A2 o:D1 k:F1 u:A2 u:D2 f3:F4 u:D2 k:A1 a4:F0 f3:D1
a4:F2 k:D1 f3:A1 a4:D1 a4:F1 w:F3 a4:D1 a4:A1 a4:B w:A1 a4:D1 a4:A1 w:F3 a4:A2 a4:B w:A1 f3:D2 a4:A1
a4:T f3:D1 a4:A2 f4:F3 f3:A1 a4:D3 a4:B f4:A1 f3:D2 u:F0 a4:A2 f4:B u:D1 f4:F4 a4:T f4:D2 f4:A1 u:A1
f4:B a4:D3 u:B f4:D2 u:F2 u:A2 a4:T u:D1 f4:P2 u:D2 u:A1 o:F3 f4:D3 u:F0 a4:D3 o:A1 u:B u:D1 u:F1 u:A2
o:P1 a1:F3 u:D1 u:A1 u:D2 a1:A1 u:B u:A1 a2:F3 u:A2 o:D1 u:D2 u:B a4:F2 u:A2 a2:D1 k:F0 u:D2 w:F3 a4:D1
k:A1 a4:F1 w:A1 k:D1 a4:A1 w:F3 a4:D1 a4:F0 w:A1 a4:A1 a4:B a4:D1 a4:B a4:A2 o:F3 a4:A2 a4:T a4:A1 o:A1
a4:T a4:D3 o:P1 u:F2 a4:D3 a6:F3 u:D1 u:F1 a6:A1 a4:B u:A1 u:D1 a6:B a4:A2 u:A1 u:B a6:D2 a4:T u:A2 u:D2
a6:P2 u:B a4:D3 u:F2 u:A2 a6:D3 u:F0 u:D2 m1:F3 m1:A1 u:D1 a4:F1 u:D1 u:A1 m3:F3 a4:D1 u:A1 u:B u:B u:A2
o:D1 w:F4 a4:A1 u:D2 u:A2 m3:D1 a4:F2 w:A1 u:D2 m3:A1 a4:B a4:D1 u:F0 a4:A2 w:F4 u:D1 a4:A1 a4:T m3:D2
u:A1 a4:B w:A1 u:B a4:A2 a4:D3 o:F4 u:A2 u:F1 o:A1 u:D2 a4:T u:D1 o:P1 u:A1 u:F0 a4:D3 u:D1 a6:F3 u:F2
a6:A1 u:B u:A1 u:D1 a6:B u:A2 u:A1 u:D2 u:B u:B o:D1 u:A2 a6:D2 w:F4 u:A2 u:D2 m2:F1 a6:P2 w:A1 u:D2
a6:D3 m1:F3 m2:A1 w:F4 m1:A1 m2:D1 m3:F3 w:A1 o:F4 m2:P1 m3:D1 m2:F0 o:D2 m3:A1 m2:F1 m2:A1 m3:D2 o:P2
m2:F2 m2:A1 o:D3 m2:D1 f1:F3 f1:A1 m2:D1 a3:F0 m2:A1 m2:P1 m2:D1 m2:P1 m4:F1 a3:D1 m2:P1 f2:F3 m4:A1
f2:F4 f2:A1 m4:B f2:D1 f2:A1 a3:P1 f2:F0 f2:D1 f2:A2 f2:F3 f2:A1 f2:D2 m4:F2 f2:A1 f2:D1 f2:A2 m4:A1
f2:D2 m4:F0 f2:A2 f2:D1 m4:B m4:A1 m4:B f2:D2 f2:A2 m4:D2 f2:D2 m4:F1 m4:D2 f3:F3 m4:A1 m4:D2 f3:F4
f3:D1 f3:F0 f3:D1 f3:A1 f3:F2 m4:B f3:D2 f3:A1 f3:D1 f4:F3 f4:A1 f3:D2 f3:A1 f3:D1 f4:F4 f4:B f4:A1
f4:D2 f4:B f3:A1 f4:D2 f3:D2 f4:P2 f3:D2 f4:F3 m4:D2 f4:F4 f4:A1 f4:D3 f4:A1 f4:B a1:F0 f4:D2 f4:B a1:A1
a2:F0 f4:D2 a2:D1 f4:P2 f4:D3 a4:F0 a4:F1 a4:D1 a4:F2 a4:D1 a4:A1 a1:F3 a4:B a1:A1 a4:D1 a2:F3 a4:A1
a4:A2 a4:B a2:D1 a4:A1 a4:T a4:A2 a4:B a4:D3 a4:T a4:A2 a4:F0 a4:D3 a4:T a4:D1 a4:F1 a4:D3 a4:A1 a4:F2
a4:D1 a4:B a4:D1 a4:A1 a4:A2 a4:B a4:T a4:A1 a4:A2 a4:B a4:D3 a4:T a4:A2 a4:F0 a4:D3 a4:F1 a4:D1 a4:T
a4:D1 a4:A1 a6:F3 a4:B a6:A1 a4:D3 a4:A1 a6:B a4:A2 a4:B a6:D2 a4:T a4:A2 a6:P2 a4:T a4:D3 a6:D3 a4:D3
m1:F3 m1:A1 a6:F4 m3:F3 a6:A1 a6:B m3:D1 m2:F0 a6:D2 m3:A1 m3:D2 a6:P2 m2:F1 m2:A1 a6:D3 m2:D1 m1:F3
m2:A1 m1:A1 m3:F3 m2:D1 m2:P1 m2:F0 m3:D1 m2:P1 m3:A1 m2:F1 m2:A1 m3:D2 m2:D1 m4:F2 m2:A1 m4:A1 m2:D1
m4:F0 m2:P1 m4:B m4:A1 m2:P1 m4:B m4:D2 m4:F1 m4:D2 m4:F0 m4:A1 m4:A1 m4:B m4:B m4:D2 m4:D2
"""
ENGINE = {"F": "PE", "B": "PE", "T": "PE", "A": "ACT", "D": "DVE", "P": "POOL"}


def takes(item, stage):
    kind, n = item[0], item[-1]
    return {"x0 D2": n == 0, "k D2": item == ("k", 0, 2),
            "o A1": n < H0 - 1, "o P1": n < H0 - 1, "o D2": n == H0 - 1, "o P2": n == H0 - 1,
            "o D3": n == H0 - 1, "f4 P2": n % TP == TP - 1, "f4 D3": n % TP == TP - 1}.get(f"{kind} {stage}", True)


def orders():
    order = {engine: [] for engine in ("PE", "ACT", "DVE", "POOL")}
    slot_of, had, latest, passed = {}, {}, {}, {}
    for word in PLAN.split():
        kind, stage = word.split(":")
        if stage[0] == "F":
            stage, slot = "F", int(stage[1:])
        n = passed[kind, stage] = passed.get((kind, stage), 0) + 1
        item = [x for x in KINDS[kind] if takes(x, stage)][n - 1]
        order[ENGINE[stage[0]]].append((item, stage))
        if stage == "F":
            slot_of[item], had[item], latest[slot] = slot, latest.get(slot), item
    return order, slot_of, had


ORDER, SLOT_OF, HAD = orders()
NTH = {x: n for n, x in enumerate(x for x, stage in ORDER["PE"] if stage == "F")}


def mega_kernel(nc, x, ctx, ctxT, cols, wq, wk, wv, wout, w1T, w2T, l1w, bo, wgu, wdT, const, out):
    stack = ExitStack()
    with stack:
        def sb(name, shape, dt=F32):
            return stack.enter_context(nc.sbuf_tensor(name, shape, dt))

        def sem(name):
            return stack.enter_context(nc.semaphore(name))

        slots = [stack.enter_context(nc.psum_tensor(f"slot{i}", [P, 512 * (1 + (i < PAIRS))], F32))
                 for i in range(PAIRS + SINGLES)]

        X = sb("X", [P, NT, D])
        CT = sb("CT", [C, B, D])
        CTT = sb("CTT", [P, B, KP1])
        COL = sb("COL", [P, NCOL])
        WQ = sb("WQ", [P, IN0])
        WK = sb("WK", [P, H0, P])
        WV = sb("WV", [P, IN0])
        WOUT = sb("WOUT", [P, H0, D])
        W1 = sb("W1", [P, HID])
        W2 = sb("W2", [P, HC, D])
        L1W = sb("L1W", [P, 6, D])
        BO = sb("BO", [1, D])
        WGU = sb("WGU", [P, 2 * MT + E1])
        WD = sb("WD", [P, 5, D])
        K = sb("K", [P, NCONST])
        ident, ones = K[:, K_ID:K_ID + P], K[:, K_ONE:K_ONE + P]
        identb = sb("identb", [P, P], BF16)

        bnx = sb("bnx", [P, 4, NT, 6])
        mvx = sb("mvx", [P, 4, NT, 2])
        vex = sb("vex", [P, 4, NT])
        bnc = sb("bnc", [C, B, 6])
        mvc = sb("mvc", [C, B, 2])
        vec = sb("vec", [C, B])
        mhalf = sb("mhalf", [P, NT])
        tg = sb("tg", [P, 4])
        ws = sb("ws", [P, 2, 4])
        cw = sb("cw", [P, 3 * HC])
        g2 = sb("g2", [P, 1])
        aq = sb("aq", [P, NT, 4])
        aq2 = sb("aq2", [P, NT, 4])
        nm0 = sb("nm0", [P, RING])
        sum0 = sb("sum0", [P, B, H0, QT])
        rec0 = sb("rec0", [P, B, H0, QT])
        mx1 = sb("mx1", [P, 4, HH])
        rec1 = sb("rec1", [P, NT, H1])
        lg = sb("lg", [P, NT, E1])
        top = sb("top", [P, NT, 8])
        idx = sb("idx", [P, NT, 8], U32)
        idf = sb("idf", [P, NT, 8])
        rt = sb("rt", [P, NT, 4])
        hot = sb("hot", [P, NT, 2, E1])
        cwt = sb("cwt", [P, NT, E1])

        XN = sb("XN", [P, NT, D])
        CN = sb("CN", [C, B, D])
        LT = sb("LT", [P, B, KEVEN])
        XQT = X2T = X3T = LT[:, :, 0:S]
        Q = sb("Q", [P, 2, 2, S], F32R)
        KH = sb("KH", [P, 2, KEVEN], F32R)
        KL = sb("KL", [P, 2, KEVEN], F32R)
        V = sb("V", [P, 5, H0, 2, DH0], F32R)
        PR = sb("PR", [P, RING, KP])
        PH = sb("PH", [P, 2, 5, 2 * P], F32R)
        PL = sb("PL", [P, 2, 5, 2 * P], F32R)
        OT = sb("OT", [P, 2, S])
        X1 = sb("X1", [P, NT, D])
        X2 = X
        W1Q = sb("W1Q", [P, HID])
        W2Q = sb("W2Q", [P, HC * D], BF16)
        YC = sb("YC", [P, HC, S])
        TH = sb("TH", [P, 2, S])
        QM = sb("QM", [P, 2, HID])
        QB = sb("QB", [P, 4, HID], BF16)
        QBT = sb("QBT", [P, 2, HID], BF16)
        RC = sb("RC", [P, 2, S])
        RK = sb("RK", [P, 2, C])
        Q1 = sb("Q1", [P, S])
        OB = sb("OB", [P, 2, QT * D])
        K1 = sb("K1", [P, B, C])
        KBD = sb("KBD", [P, H1, C])
        V1 = sb("V1", [P, KC1, 2, HH, DH1 + 1])
        S1 = sb("S1", [P, 3, KP1])
        PT1 = sb("PT1", [P, 2, KP1])
        A1 = sb("A1", [P, QT, D])
        A1T = sb("A1T", [P, S])
        X3 = X1
        HB = TH
        SHT = sb("SHT", [P, QT, F1])
        HM = sb("HM", [P, QT, MT])
        HT = sb("HT", [P, 2, KP])
        Y = X

        names = ["x0", "x1", "ctx", "cols", "wq", "wk", "wv", "const", "wout", "ffn", "l1", "moe"]
        ld = {n: sem(f"ld_{n}") for n in names}
        stored = sem("stored")
        dve_step = sem("dve_step")
        act_step = sem("act_step")
        pool_const = sem("pool_const")
        front_done = sem("front_done")
        var_ready = [sem(f"var_ready{i}") for i in range(4)]
        rstd_ready = [sem(f"rstd_ready{i}") for i in range(4)]
        varc_ready = sem("varc_ready")
        rstdc_ready = sem("rstdc_ready")
        xn_ready = [sem(f"xn_ready{i}") for i in range(4)]
        cn_ready = sem("cn_ready")
        lt_ready = sem("lt_ready")
        v_upper = sem("v_upper")
        v_ready = sem("v_ready")
        q_upper = sem("q_upper")
        q_ready = sem("q_ready")
        k_upper = sem("k_upper")
        k_ready = sem("k_ready")
        max_ready = sem("max_ready")
        prob_ready = sem("prob_ready")
        prob_turned = sem("prob_turned")
        pt_upper = sem("pt_upper")
        pt_ready = sem("pt_ready")
        ot_ready = sem("ot_ready")
        rec_ready = sem("rec_ready")
        o_scaled = sem("o_scaled")
        o_added = sem("o_added")
        x1_ready = sem("x1_ready")
        lt_pad = sem("lt_pad")
        pad_ready = sem("pad_ready")
        s1_pad = sem("s1_pad")
        identb_ready = sem("identb_ready")
        gates_ready = sem("gates_ready")
        wsum_ready = sem("wsum_ready")
        wmean_ready = sem("wmean_ready")
        w1q_ready = sem("w1q_ready")
        w2q_ready = sem("w2q_ready")
        conv_scaled = sem("conv_scaled")
        xqt_ready = sem("xqt_ready")
        conv_mid = sem("conv_mid")
        conv_done = sem("conv_done")
        tanh_done = sem("tanh_done")
        silu_ready = sem("silu_ready")
        scale_ready = sem("scale_ready")
        rounded = sem("rounded")
        qb_ready = sem("qb_ready")
        qbt_ready = sem("qbt_ready")
        f_done = sem("f_done")
        x2_ready = sem("x2_ready")
        x2t_ready = sem("x2t_ready")
        q1_ready = sem("q1_ready")
        k1_ready = sem("k1_ready")
        kbd_ready = sem("kbd_ready")
        shifted = sem("shifted")
        exp1_ready = sem("exp1_ready")
        p1_turned = sem("p1_turned")
        pt1_ready = sem("pt1_ready")
        pv1_done = sem("pv1_done")
        a1_ready = sem("a1_ready")
        a1t_ready = sem("a1t_ready")
        ya_done = sem("ya_done")
        x3_ready = sem("x3_ready")
        x3t_ready = sem("x3t_ready")
        logits_copied = sem("logits_copied")
        logits_ready = sem("logits_ready")
        exps_ready = sem("exps_ready")
        shared_tanh = sem("shared_tanh")
        shared_ready = sem("shared_ready")
        weights_ready = sem("weights_ready")
        gate_tanh = sem("gate_tanh")
        hid_ready = sem("hid_ready")
        hidw_ready = sem("hidw_ready")
        ht_ready = sem("ht_ready")
        ym_done = sem("ym_done")
        y_ready = sem("y_ready")
        block = stack.enter_context(nc.Block())

        def value_chunks(j):
            return [(0, 2 * j, P), (1, 2 * j + 1, P)] if j < 2 else [(0, 4, C)]

        def last_read(item):
            n = upto(item)
            return {"u": (pt_ready, n), "w": (ot_ready, n), "x0": (lt_ready, 2 * n), "v": (v_ready, 2 * n - n // 3), "q": (q_ready, 2 * n), "k": (k_ready, n),
                    "s": (wmean_ready, n), "o": (x1_ready, QT * (n // H0)) if n % H0 == 0 else (o_scaled, QT * (n - n // H0)), "f1": (xqt_ready, n), "f2": (conv_done, n),
                    "f3": (rounded, n), "f4": (x2_ready, n), "a3": (k1_ready, n), "a1": (x2t_ready, n),
                    "a2": (q1_ready, n), "a4": (a1_ready, n), "a6": (x3_ready, n), "m1": (x3t_ready, n),
                    "m3": (shared_ready, n), "m2": (hid_ready, n), "m4": (y_ready, n)}[item[0]]

        def part_tiles(item):
            m = item[1] * QT + item[2] * TP
            return slice(m, m + TP)

        def slot(item):
            return slots[SLOT_OF[item]]

        def col(name):
            return COL[:, COLS.index(name):COLS.index(name) + 1]

        def walk(engine, stages):
            for item, stage in ORDER[engine]:
                stages[stage](item)

        @block.sync
        def _(sp):
            xv = x.rearrange("(t p) d -> p t d", p=P)
            for b in range(B):
                sp.dma_start(X[:, b * QT:(b + 1) * QT, :], xv[:, b * QT:(b + 1) * QT, :]).then_inc(ld[f"x{b}"], 16)
            sp.dma_start(WV[:], wv).then_inc(ld["wv"], 16)
            sp.dma_start(WK[:], wk.rearrange("p (h c) -> p h c", h=H0)).then_inc(ld["wk"], 16)
            sp.dma_start(W2[:], w2T.rearrange("(c p) d -> p c d", p=P)).then_inc(ld["ffn"], 16)
            sp.dma_start(W1[:], w1T).then_inc(ld["ffn"], 16)
            sp.dma_start(WOUT[:], wout.rearrange("(h p) d -> p h d", p=P)).then_inc(ld["wout"], 16)
            sp.dma_start(L1W[:], l1w.rearrange("p (k d) -> p k d", d=D)).then_inc(ld["l1"], 16)
            sp.dma_start(BO[:], bo).then_inc(ld["l1"], 16)
            sp.dma_start(CTT[:], ctxT.rearrange("p (b c) -> p b c", b=B)).then_inc(ld["l1"], 16)
            sp.dma_start(WGU[:], wgu).then_inc(ld["moe"], 16)
            sp.dma_start(WD[:], wdT.rearrange("(c p) d -> p c d", p=P)).then_inc(ld["moe"], 16)
            ov = out.rearrange("(t p) d -> t p d", p=P)
            for t in range(NT):
                sp.wait_ge(y_ready, t + 1)
                sp.dma_start(ov[t], Y[:, t, :]).then_inc(stored, 16)
            sp.wait_ge(stored, 16 * NT)

        @block.gpsimd
        def _(pool):
            pool.memset(mhalf[:], -0.5).then_inc(pool_const, 1)
            pool.memset(LT[:, :, KEYS0:KEVEN], 0.0).then_inc(lt_pad, 1)
            pool.memset(PR[:], 0.0).then_inc(pad_ready, 1)
            pool.memset(S1[:, :, HH * C:KP1], 0.0).then_inc(s1_pad, 1)
            pool.wait_ge(pool_const, 1)

            def rstd(n, part, parts=1):
                r = slice(part * QT // parts, (part + 1) * QT // parts)
                pool.wait_ge(var_ready[n], part + 1)
                pool.tensor_tensor(vex[:, n, r], vex[:, n, r], mhalf[:, r], ALU.pow).then_inc(rstd_ready[n], 1)

            rstd(0, 0)
            pool.wait_ge(varc_ready, 1)
            pool.tensor_tensor(vec[:], vec[:], mhalf[0:C, 0:B], ALU.pow).then_inc(rstdc_ready, 1)
            rstd(0, 1)

            def work(item):
                kind, b = item[0], item[1]
                n = upto(item)
                if kind == "o":
                    h, e, r = item[2], n - n // H0, slice(b * QT, (b + 1) * QT)
                    pool.wait_ge(o_scaled, QT * e)
                    if h == 0:
                        pool.wait_ge(ld[f"x{b}"], 16)
                    if e > 1:
                        pool.wait_ge(o_added, e - 1)
                    pool.tensor_tensor(X1[:, r, :], OB[:, e % 2, :].rearrange("p (t d) -> p t d", t=QT),
                                       (X1 if h else X)[:, r, :], ALU.add).then_inc(o_added, 1)
                elif kind == "a3":
                    pool.wait_ge(k1_ready, n)
                    pool.wait_ge(ld["const"], 16)
                    if n > 1:
                        pool.wait_ge(p1_turned, 2 * QT * (n - 1))
                    pool.tensor_tensor(KBD[:], K1[:, b, :].unsqueeze(1).broadcast_to([P, H1, C]),
                                       K[:, K_MASK:K_MASK + H1].unsqueeze(2).broadcast_to([P, H1, C]),
                                       ALU.mult).then_inc(kbd_ready, 1)
                else:
                    m = n - 1
                    pool.wait_ge(weights_ready, m // TP + 1)
                    pool.wait_ge(hid_ready, m + 1)
                    hm = HM[:, m % QT, 0:MH].rearrange("p (e f) -> p e f", e=E1)
                    pool.tensor_tensor(hm, hm, cwt[:, m, :].unsqueeze(2).broadcast_to([P, E1, F1]),
                                       ALU.mult).then_inc(hidw_ready, 1)

            def power(item):
                if item[0] == "o":
                    rstd(1, item[1])
                elif item[0] == "f4":
                    rstd(2, upto(item) // TP - 1, PARTS)
                else:
                    rstd(3, upto(item) - 1, PARTS)

            walk("POOL", {"P1": work, "P2": power})

        @block.tensor
        def _(pe):
            def turn(dst, src, p=P):
                return pe.transpose(dst, src, ident[0:p, 0:p])

            def turn_tiles(W, part, n, tiles=QT):
                for t in range(tiles):
                    pe.wait_ge(xn_ready[n], part * tiles + t + 1)
                    mm = turn(W[:, t * P:(t + 1) * P], XN[:, part * tiles + t, :])
                return mm

            def front(item):
                kind, b = item[0], item[1]
                W = slot(item)
                if HAD[item] is not None:
                    pe.wait_ge(*last_read(HAD[item]))
                if kind == "x0":
                    if b == 0:
                        pe.wait_ge(ld["const"], 16)
                    turn_tiles(W, b, 0)
                    pe.wait_ge(cn_ready, b + 1)
                    mm = turn(W[:, S:S + C], CN[:, b, :], C)
                elif kind == "v":
                    j = item[2]
                    pe.wait_ge(lt_ready, 2 * (b + 1))
                    pe.wait_ge(ld["wv"], 16)
                    for n, c, w in value_chunks(j):
                        mm = pe.matmul(W[0:w, n * 512:n * 512 + 512], LT[:, b, c * P:c * P + w], WV[:],
                                       start=True, stop=True)
                elif kind == "q":
                    hp = item[2]
                    pe.wait_ge(lt_ready, 2 * (b + 1))
                    pe.wait_ge(ld["wq"], 16)
                    mm = pe.matmul(W[:, 0:S], WQ[:, hp * P:(hp + 1) * P], LT[:, b, 0:S], start=True, stop=True)
                elif kind == "k":
                    h = item[2]
                    pe.wait_ge(lt_ready, 2 * (b + 1))
                    pe.wait_ge(ld["wk"], 16)
                    pe.wait_ge(lt_pad, 1)
                    pe.matmul(W[:, K0:512], WK[:, h, :], LT[:, b, 0:KA], start=True, stop=True)
                    mm = pe.matmul(W[:, 512:K0 + KEVEN], WK[:, h, :], LT[:, b, KA:KEVEN], start=True, stop=True)
                elif kind == "u":
                    _, b, h, qt = item
                    g = b * H0 + h
                    pe.wait_ge(q_ready, 2 * (g // 2 + 1))
                    pe.wait_ge(k_ready, g + 1)
                    q = Q[:, g // 2 % 2, h % 2, qt * P:(qt + 1) * P]
                    for lo, hi in ((0, KA), (KA, KEVEN)):
                        pe.matmul(W[:, K0 + lo:K0 + hi], q, KH[:, g % 2, lo:hi], start=True, stop=False)
                        mm = pe.matmul(W[:, K0 + lo:K0 + hi], q, KL[:, g % 2, lo:hi], start=False, stop=True)
                elif kind == "w":
                    h = item[2]
                    pe.wait_ge(v_ready, 5 * (b + 1))
                    pe.wait_ge(pt_ready, 2 * upto(item))
                    s = (upto(item) - 1) % 2
                    for c in range(5):
                        r = P if c < 4 else C
                        v = V[0:r, c, h, :, :].rearrange("p k d -> p (k d)")
                        pe.matmul(W[:, 0:2 * P], v, PH[0:r, s, c, :], start=(c == 0), stop=False)
                        mm = pe.matmul(W[:, 0:2 * P], v, PL[0:r, s, c, :], start=False, stop=(c == 4))
                elif kind == "o":
                    n = upto(item)
                    pe.wait_ge(ot_ready, 2 * n)
                    pe.wait_ge(ld["wout"], 16)
                    for t in range(QT):
                        mm = pe.matmul(W[:, t * D:(t + 1) * D], OT[:, (n - 1) % 2, t * P:(t + 1) * P],
                                       WOUT[:, item[2], :], start=True, stop=True)
                elif kind == "s":
                    pe.wait_ge(wsum_ready, 2)
                    mm = pe.matmul(W[:, 0:2], ones, ws[:, 0, 0:2], start=True, stop=True)
                elif kind == "f1":
                    mm = turn_tiles(W, b, 1)
                elif kind == "f2":
                    c = item[2]
                    pe.wait_ge(xqt_ready, b + 1)
                    pe.wait_ge(w1q_ready, 1)
                    mm = pe.matmul(W[:, 0:S], W1Q[:, c * P:(c + 1) * P], XQT[:, b, :], start=True, stop=True)
                elif kind == "f3":
                    t = item[2]
                    for c in range(HC):
                        pe.wait_ge(silu_ready, upto(("f2", b, c)))
                        mm = turn(W[:, c * P:(c + 1) * P], YC[:, c, t * P:(t + 1) * P])
                elif kind == "f4":
                    n = upto(item)
                    pe.wait_ge(qb_ready, n)
                    pe.wait_ge(identb_ready, 1)
                    Wb = W[:, 0:256].bitcast(BF16)
                    for c in range(HC):
                        mm = pe.transpose(Wb[:, c * P:(c + 1) * P], QB[:, (n - 1) % 4, c * P:(c + 1) * P], identb[:])
                elif kind == "a3":
                    pe.wait_ge(ld["l1"], 48)
                    pe.matmul(W[:, 0:C], L1W[:, 2, :], CTT[:, b, 0:C], start=True, stop=True)
                    pe.matmul(W[:, P:P + C], L1W[:, 3, :], CTT[:, b, 0:C], start=True, stop=True)
                    for c in range(KC1):
                        mm = pe.matmul(W[:, (c + 2) * P:(c + 3) * P], CTT[:, b, c * P:(c + 1) * P], L1W[:, 4, :],
                                       start=True, stop=True)
                elif kind == "a1":
                    mm = turn_tiles(W, upto(item) - 1, 2, TP)
                elif kind == "a2":
                    pe.wait_ge(x2t_ready, upto(item))
                    pe.wait_ge(ld["l1"], 48)
                    xt = X2T[:, b, item[2] * N:(item[2] + 1) * N]
                    for k in range(2):
                        mm = pe.matmul(W[:, k * N:(k + 1) * N], L1W[:, k, :], xt, start=True, stop=True)
                elif kind == "a4":
                    _, b, t, h = item
                    pe.wait_ge(q1_ready, (b * QT + t) // TP + 1)
                    pe.wait_ge(kbd_ready, b + 1)
                    for n in range(2):
                        kk = KBD[:, h * HH + n * 4:h * HH + n * 4 + 4, :]
                        mm = pe.matmul(W[:, n * 512:n * 512 + 4 * C], Q1[:, t * P:(t + 1) * P], kk,
                                       start=True, stop=True)
                elif kind == "a6":
                    for j in range(TP):
                        t = item[2] * TP + j
                        pe.wait_ge(a1_ready, 2 * (b * QT + t + 1))
                        mm = turn(W[:, j * P:(j + 1) * P], A1[:, t, :])
                elif kind == "m1":
                    mm = turn_tiles(W, upto(item) - 1, 3, TP)
                elif kind == "m3":
                    pe.wait_ge(x3t_ready, upto(item))
                    pe.wait_ge(ld["moe"], 32)
                    for j in range(TP):
                        t = item[2] * TP + j
                        mm = pe.matmul(W[:, j * 256:j * 256 + 2 * F1 + E1], X3T[:, b, t * P:(t + 1) * P],
                                       WGU[:, 2 * MH:], start=True, stop=True)
                elif kind == "m2":
                    t = item[2]
                    pe.wait_ge(x3t_ready, (b * QT + t) // TP + 1)
                    pe.wait_ge(ld["moe"], 32)
                    xt = X3T[:, b, t * P:(t + 1) * P]
                    pe.matmul(W[:, 0:MH], xt, WGU[:, 0:MH], start=True, stop=True)
                    mm = pe.matmul(W[:, MH:2 * MH], xt, WGU[:, MH:2 * MH], start=True, stop=True)
                elif kind == "m4":
                    m = b * QT + item[2]
                    pe.wait_ge(hidw_ready, m + 1)
                    pe.wait_ge(shared_ready, m // TP + 1)
                    for c in range(HC):
                        turn(W[:, c * P:(c + 1) * P], HM[:, m % QT, c * P:(c + 1) * P])
                    mm = turn(W[0:F1, 512:512 + P], HM[:, m % QT, MH:MT])
                mm.then_inc(front_done, 1)

            def back(item):
                kind, b = item[0], item[1]
                W = slot(item)
                if kind == "u":
                    n = upto(item)
                    pe.wait_ge(prob_ready, n)
                    pe.wait_ge(pad_ready, 1)
                    for c in range(5):
                        mm = turn(W[:, c * P:(c + 1) * P], PR[:, (n - 1) % RING, c * P:(c + 1) * P])
                    mm.then_inc(prob_turned, 1)
                elif kind == "f4":
                    n = upto(item)
                    pe.wait_ge(qbt_ready, n)
                    pe.wait_ge(w2q_ready, 1)
                    for c in range(HC):
                        mm = pe.matmul(W[:, 2 * P:2 * P + D], QBT[:, (n - 1) % 2, c * P:(c + 1) * P],
                                       W2Q[:, c * D:(c + 1) * D], start=(c == 0), stop=(c == HC - 1))
                    mm.then_inc(f_done, 1)
                elif kind == "a4":
                    n = upto(item)
                    pe.wait_ge(exp1_ready, n)
                    pe.wait_ge(s1_pad, 1)
                    for c in range(KC1):
                        mm = turn(W[:, c * P:(c + 1) * P], S1[:, (n - 1) % 3, c * P:(c + 1) * P])
                    mm.then_inc(p1_turned, 1)
                elif kind == "a6":
                    pe.wait_ge(a1t_ready, upto(item))
                    for j in range(TP):
                        t = item[2] * TP + j
                        o = W[:, N + j * D:N + (j + 1) * D]
                        pe.matmul(o, A1T[:, t * P:(t + 1) * P], L1W[:, 5, :], start=True, stop=False)
                        mm = pe.matmul(o, ones[0:1, :], BO[:], start=False, stop=True)
                    mm.then_inc(ya_done, 1)
                elif kind == "m4":
                    n = upto(item)
                    pe.wait_ge(ht_ready, 2 * n)
                    o = W[:, 640:640 + D]
                    for c in range(HC):
                        pe.matmul(o, HT[:, (n - 1) % 2, c * P:(c + 1) * P], WD[:, c, :], start=(c == 0), stop=False)
                    pe.matmul(o, HT[0:F1, (n - 1) % 2, MH:MH + P], WD[0:F1, 4, :],
                              start=False, stop=True).then_inc(ym_done, 1)

            def tail(item):
                kind, b = item[0], item[1]
                if kind == "a4":
                    _, b, t, h = item
                    n = upto(item)
                    pe.wait_ge(pt1_ready, n)
                    for c in range(KC1):
                        mm = pe.matmul(slot(item)[:, KP1:KP1 + HH * (DH1 + 1)], PT1[:, (n - 1) % 2, c * P:(c + 1) * P],
                                       V1[:, c, h, :, :].rearrange("p h d -> p (h d)"),
                                       start=(c == 0), stop=(c == KC1 - 1))
                    mm.then_inc(pv1_done, 1)

            walk("PE", {"F": front, "B": back, "T": tail})

        @block.scalar
        def _(act):
            act.dma_start(K[:], const).then_inc(ld["const"], 16)
            act.dma_start(COL[:], cols).then_inc(ld["cols"], 16)
            act.dma_start(CT[:], ctx.rearrange("(b c) d -> c b d", b=B)).then_inc(ld["ctx"], 16)
            act.dma_start(WQ[:], wq).then_inc(ld["wq"], 16)
            act.wait_ge(ld["cols"], 16)
            act.activation(tg[:], COL[:, COLS.index("gx0"):COLS.index("gx0") + 4], ACT.Tanh).then_inc(gates_ready, 1)

            def first(item):
                kind, b = item[0], item[1]
                W, n = slot(item), upto(item)
                if kind == "u":
                    act.wait_ge(max_ready, n)
                    if n == 1:
                        act.wait_ge(pad_ready, 1)
                    if n > RING:
                        act.wait_ge(prob_turned, n - RING)
                    s, qt = (n - 1) % RING, item[3]
                    act.activation(PR[:, s, 0:KEYS0], W[:, K0:K0 + KEYS0], ACT.Exp, bias=nm0[:, s:s + 1],
                                   accum_out=sum0[:, b, item[2], qt:qt + 1]).then_inc(prob_ready, 1)
                    return
                act.wait_ge(front_done, NTH[item] + 1)
                if kind == "x0":
                    act.activation(LT[:, b, 0:S], W[:, 0:S], ACT.Identity, bias=col("bl"),
                                   scale=col("gl")).then_inc(lt_ready, 1)
                    act.activation(LT[:, b, S:KEYS0], W[:, S:KEYS0], ACT.Identity, bias=col("bm"),
                                   scale=col("gm")).then_inc(lt_ready, 1)
                elif kind == "w":
                    g, j = b * H0 + item[2], item[3]
                    if g >= 2:
                        act.wait_ge(front_done, NTH[KINDS["o"][g - 2]] + 1)
                    act.activation(OT[:, g % 2, 2 * j * P:(2 * j + 2) * P], W[:, 0:2 * P], ACT.Copy).then_inc(ot_ready, 1)
                elif kind == "o":
                    e = n - n // H0
                    act.wait_ge(rec_ready, n)
                    if e > 2:
                        act.wait_ge(o_added, e - 2)
                    for t in range(QT):
                        act.activation(OB[:, e % 2, t * D:(t + 1) * D], W[:, t * D:(t + 1) * D], ACT.Copy,
                                       scale=rec0[:, b, item[2], t:t + 1]).then_inc(o_scaled, 1)
                elif kind == "v":
                    if b == 1:
                        act.wait_ge(front_done, NTH["w", 0, H0 - 1, 1] + 1)
                    for n2, c, r in value_chunks(item[2]):
                        act.activation(V[0:r, c, :, 0, :], W[0:r, n2 * 512:n2 * 512 + 512], ACT.Copy).then_inc(v_upper, 1)
                elif kind == "q":
                    if n > 2:
                        act.wait_ge(prob_turned, 8 * (n - 2))
                    for e in range(2):
                        r = slice(e * DH0, (e + 1) * DH0)
                        act.activation(Q[r, (n - 1) % 2, e, :], W[r, 0:S], ACT.Copy,
                                       scale=float(DH0) ** 0.5).then_inc(q_upper, 1)
                elif kind == "k":
                    if n > 2:
                        act.wait_ge(prob_turned, QT * (n - 2))
                    act.activation(KH[:, (n - 1) % 2, :], W[:, K0:K0 + KEVEN], ACT.Copy).then_inc(k_upper, 1)
                elif kind == "f1":
                    act.activation(XQT[:, b, :], W[:, 0:S], ACT.Copy).then_inc(xqt_ready, 1)
                elif kind == "f2":
                    c = item[2]
                    act.wait_ge(conv_scaled, 1)
                    act.activation(YC[:, c, :], W[:, 0:S], ACT.Identity,
                                   bias=COL[:, CONV_B + c:CONV_B + c + 1],
                                   scale=cw[:, 3 * c + 1:3 * c + 2]).then_inc(conv_mid, 1)
                elif kind == "f3":
                    m = b * QT + item[2]
                    act.wait_ge(scale_ready, n)
                    if n > 2:
                        act.wait_ge(qb_ready, n - 2)
                    act.activation(QM[:, (n - 1) % 2, :], W[:, 0:HID], ACT.Identity, bias=COL[:, NCOL - 1:NCOL],
                                   scale=aq2[:, m, 2:3]).then_inc(rounded, 1)
                elif kind == "f4":
                    if n > 2:
                        act.wait_ge(f_done, n - 2)
                    act.activation(QBT[:, (n - 1) % 2, :], W[:, 0:256].bitcast(BF16), ACT.Copy).then_inc(qbt_ready, 1)
                elif kind == "a1":
                    act.activation(X2T[:, b, item[2] * N:(item[2] + 1) * N], W[:, 0:N], ACT.Copy).then_inc(x2t_ready, 1)
                elif kind == "a4":
                    act.wait_ge(shifted, n)
                    s1 = S1[:, (n - 1) % 3, 0:HH * C]
                    act.activation(s1, s1, ACT.Exp, scale=float(DH1) ** -0.5).then_inc(exp1_ready, 1)
                elif kind == "a6":
                    act.activation(A1T[:, item[2] * N:(item[2] + 1) * N], W[:, 0:N], ACT.Identity,
                                   bias=col("bv")).then_inc(a1t_ready, 1)
                elif kind == "m1":
                    act.activation(X3T[:, b, item[2] * N:(item[2] + 1) * N], W[:, 0:N], ACT.Copy).then_inc(x3t_ready, 1)
                elif kind == "m3":
                    act.wait_ge(logits_copied, n)
                    act.activation(SHT[:, item[2] * TP:(item[2] + 1) * TP, :],
                                   W[:, 0:TP * 256].rearrange("p (t c) -> p t c", t=TP)[:, :, 0:F1], ACT.Tanh,
                                   scale=0.5).then_inc(shared_tanh, 1)
                    act.wait_ge(logits_ready, n)
                    r = part_tiles(item)
                    act.activation(lg[:, r, :], lg[:, r, :], ACT.Exp).then_inc(exps_ready, 1)
                elif kind == "m2":
                    if n > 2:
                        act.wait_ge(hid_ready, n - 2)
                    act.activation(HB[:, (n - 1) % 2, :], W[:, 0:MH], ACT.Tanh, scale=0.5).then_inc(gate_tanh, 1)
                elif kind == "m4":
                    if n > 2:
                        act.wait_ge(ym_done, n - 2)
                    act.activation(HT[:, (n - 1) % 2, 0:MH], W[:, 0:MH], ACT.Copy).then_inc(ht_ready, 1)
                    act.activation(HT[0:F1, (n - 1) % 2, MH:MH + P], W[0:F1, MH:MH + P],
                                   ACT.Copy).then_inc(ht_ready, 1)

            def second(item):
                kind, b = item[0], item[1]
                W, n = slot(item), upto(item)
                if kind == "u":
                    act.wait_ge(prob_turned, n)
                    if n > 4:
                        act.wait_ge(front_done, NTH[KINDS["w"][(n - 1) // 2 - 2]] + 1)
                    qt = item[3]
                    act.activation(PH[:, (n - 1) // 2 % 2, :, qt % 2 * P:(qt % 2 + 1) * P], W[:, 0:KP],
                                   ACT.Copy).then_inc(pt_upper, 1)
                elif kind == "f2":
                    c = item[2]
                    act.wait_ge(conv_done, n)
                    if n > 2:
                        act.wait_ge(silu_ready, n - 2)
                    act.activation(TH[:, (n - 1) % 2, :], YC[:, c, :], ACT.Tanh, scale=0.5).then_inc(tanh_done, 1)
                elif kind == "a4":
                    act.wait_ge(p1_turned, n)
                    if n > 2:
                        act.wait_ge(pv1_done, n - 2)
                    act.activation(PT1[:, (n - 1) % 2, :], W[:, 0:KP1], ACT.Copy).then_inc(pt1_ready, 1)

            walk("ACT", {"A1": first, "A2": second})

        @block.vector
        def _(dve):
            steps_done = [0]

            def link(ins):
                steps_done[0] += 1
                ins.then_inc(dve_step, 1)
                dve.wait_ge(dve_step, steps_done[0])

            def link_all(instructions):
                for ins in instructions:
                    steps_done[0] += 1
                    ins.then_inc(dve_step, 1)
                dve.wait_ge(dve_step, steps_done[0])

            def stats(n, src, m):
                link(dve.bn_stats(bnx[:, n, m, :], src[:, m, :]))
                return dve.bn_aggr(mvx[:, n, m, :], bnx[:, n, m, :])

            def all_stats(n, src, r):
                tiles = range(r.start, r.stop)
                link_all([dve.bn_stats(bnx[:, n, m, :], src[:, m, :]) for m in tiles])
                link_all([dve.bn_aggr(mvx[:, n, m, :], bnx[:, n, m, :]) for m in tiles])

            def variance(n, r, twice=False):
                s1, s2 = (1.0 + EPS, EPS * EPS) if twice else (1.0, EPS)
                dve.tensor_scalar(vex[:, n, r], mvx[:, n, r, 1], s1, s2, ALU.mult, ALU.add).then_inc(var_ready[n], 1)

            def normalise(n, src, m, out, signal):
                return dve.tensor_scalar(out, src[:, m, :], mvx[:, n, m, 0:1], vex[:, n, m:m + 1],
                                         ALU.subtract, ALU.mult).then_inc(signal, 1)

            dve.wait_ge(ld["x0"], 16)
            link_all([dve.bn_stats(bnx[:, 0, m, :], X[:, m, :]) for m in range(QT)])
            link_all([dve.bn_aggr(mvx[:, 0, m, :], bnx[:, 0, m, :]) for m in range(QT)])
            variance(0, slice(0, QT), twice=True)
            dve.wait_ge(ld["ctx"], 16)
            link_all([dve.bn_stats(bnc[:, b, :], CT[:, b, :]) for b in range(B)])
            link_all([dve.bn_aggr(mvc[:, b, :], bnc[:, b, :]) for b in range(B)])
            dve.tensor_scalar(vec[:], mvc[:, :, 1], EPS, None, ALU.add).then_inc(varc_ready, 1)
            dve.wait_ge(rstd_ready[0], 1)
            for m in range(QT):
                normalise(0, X, m, XN[:, m, :], xn_ready[0])
            dve.wait_ge(rstdc_ready, 1)
            for b in range(B):
                dve.tensor_scalar(CN[:, b, :], CT[:, b, :], mvc[:, b, 0:1], vec[:, b:b + 1],
                                  ALU.subtract, ALU.mult).then_inc(cn_ready, 1)
            dve.wait_ge(ld["x1"], 16)
            link_all([dve.bn_stats(bnx[:, 0, m, :], X[:, m, :]) for m in range(QT, NT)])
            link_all([dve.bn_aggr(mvx[:, 0, m, :], bnx[:, 0, m, :]) for m in range(QT, NT)])
            variance(0, slice(QT, NT), twice=True)

            def first(item):
                kind, b = item[0], item[1]
                W, n = slot(item), upto(item)
                r = slice(b * QT, (b + 1) * QT)
                if kind != "o":
                    dve.wait_ge(front_done, NTH[item] + 1)
                if kind == "v":
                    for n2, c, rows in value_chunks(item[2]):
                        dve.wait_ge(v_upper, 5 * b + c + 1)
                        hi = V[0:rows, c, :, 0, :].bitcast(F32)
                        w = W[0:rows, n2 * 512:n2 * 512 + 512].rearrange("p (h d) -> p h d", h=H0)
                        dve.tensor_tensor(V[0:rows, c, :, 1, :], w, hi, ALU.subtract).then_inc(v_ready, 1)
                elif kind == "q":
                    for e in range(2):
                        dve.wait_ge(q_upper, 2 * n - 1 + e)
                        r, o = slice(e * DH0, (e + 1) * DH0), slice((1 - e) * DH0, (2 - e) * DH0)
                        dve.scalar_tensor_tensor(out=Q[o, (n - 1) % 2, e, :], in0=W[r, 0:S], scalar=float(DH0) ** 0.5,
                                                 in1=Q[r, (n - 1) % 2, e, :].bitcast(F32), op0=ALU.mult,
                                                 op1=ALU.subtract).then_inc(q_ready, 1)
                elif kind == "k":
                    dve.wait_ge(k_upper, n)
                    dve.tensor_tensor(KL[:, (n - 1) % 2, :], W[:, K0:K0 + KEVEN], KH[:, (n - 1) % 2, :].bitcast(F32),
                                      ALU.subtract).then_inc(k_ready, 1)
                elif kind == "u":
                    s = (n - 1) % RING
                    if n > RING:
                        dve.wait_ge(prob_ready, n - RING)
                    dve.tensor_reduce(nm0[:, s:s + 1], W[:, K0:K0 + KEYS0], AX.X, ALU.max,
                                      negate=True).then_inc(max_ready, 1)
                elif kind == "o":
                    rec = rec0[:, b, item[2], :]
                    dve.wait_ge(prob_ready, QT * n)
                    link(dve.reciprocal(rec, sum0[:, b, item[2], :]))
                    dve.wait_ge(gates_ready, 1)
                    dve.tensor_scalar(rec, rec, tg[:, 0:1], None, ALU.mult).then_inc(rec_ready, 1)
                elif kind == "s":
                    dve.tensor_scalar(ws[:, 1, 0:2], W[:, 0:2], 1.0 / (HID * D), 1e-5,
                                      ALU.mult, ALU.max).then_inc(wmean_ready, 1)
                    dve.wait_ge(wmean_ready, 1)
                    link(dve.reciprocal(ws[:, 1, 2:4], ws[:, 1, 0:2]))
                    w2f = W2[:].rearrange("p c d -> p (c d)")
                    link_all([dve.tensor_scalar(w, w, ws[:, 1, 2 + k:3 + k], MAGIC, ALU.mult, ALU.add)
                              for k, w in enumerate((W1[:], w2f))])
                    link_all([dve.tensor_scalar(w, w, MAGIC, 1.0, ALU.subtract, ALU.min) for w in (W1[:], w2f)])
                    dve.tensor_scalar(W1Q[:], W1[:], -1.0, None, ALU.max).then_inc(w1q_ready, 1)
                    dve.tensor_scalar(W2Q[:], w2f, -1.0, None, ALU.max).then_inc(w2q_ready, 1)
                    dve.tensor_scalar(cw[:], COL[:, CONV_W:CONV_W + 3 * HC], ws[:, 1, 0:1], None,
                                      ALU.mult).then_inc(conv_scaled, 1)
                    dve.wait_ge(gates_ready, 1)
                    link(dve.tensor_tensor(g2[:], tg[:, 2:3], ws[:, 1, 1:2], ALU.mult))
                elif kind == "f2":
                    c = item[2]
                    y = YC[:, c, :]
                    dve.wait_ge(conv_mid, n)
                    link(dve.scalar_tensor_tensor(out=y[:, 1:S], in0=W[:, 0:S - 1], scalar=cw[:, 3 * c:3 * c + 1],
                                                  in1=y[:, 1:S], op0=ALU.mult, op1=ALU.add))
                    dve.scalar_tensor_tensor(out=y[:, 0:S - 1], in0=W[:, 1:S], scalar=cw[:, 3 * c + 2:3 * c + 3],
                                             in1=y[:, 0:S - 1], op0=ALU.mult, op1=ALU.add).then_inc(conv_done, 1)
                elif kind == "f3":
                    m = b * QT + item[2]
                    a = aq2[:, m, :]
                    link(dve.tensor_reduce(a[:, 0:1], W[:, 0:HID], AX.X, ALU.max, apply_absolute_value=True))
                    link(dve.tensor_scalar(a[:, 1:2], a[:, 0:1], 2e-5, 1.0 / 127, ALU.max, ALU.mult))
                    dve.reciprocal(a[:, 2:3], a[:, 1:2]).then_inc(scale_ready, 1)
                    link(dve.tensor_scalar(a[:, 3:4], a[:, 1:2], 0.5, g2[:, 0:1], ALU.mult, ALU.mult))
                elif kind == "a3":
                    dve.wait_ge(ld["cols"], 16)
                    dve.wait_ge(ld["const"], 16)
                    block = K[:, K_BLOCK:K_BLOCK + KC1 * HH].rearrange("p (c h) -> p c h", c=KC1)
                    w = W[:, 2 * P:2 * P + KC1 * D].rearrange("p (c k h d) -> p c k h d", c=KC1, k=2, h=HH)
                    link_all([dve.tensor_tensor(V1[:, :, k, :, 0:DH1], w[:, :, k, :, :],
                                                block.unsqueeze(3).broadcast_to([P, KC1, HH, DH1]), ALU.mult)
                              for k in range(2)])
                    link_all([dve.tensor_copy(V1[:, :, k, :, DH1], block) for k in range(2)])
                    link_all([dve.scalar_tensor_tensor(out=RK[:, k, :], in0=W[:, k * P:k * P + C],
                                                       scalar=col(("bk", "bks")[k]), in1=K[:, o:o + C],
                                                       op0=ALU.add, op1=ALU.mult) for k, o in enumerate((K_CK, K_SK))])
                    dve.tensor_tensor(K1[:, b, :], RK[:, 0, :], RK[:, 1, :], ALU.add).then_inc(k1_ready, 1)
                elif kind == "a2":
                    if n > 1:
                        dve.wait_ge(q1_ready, n - 1)
                    at = item[2] * N
                    link_all([dve.scalar_tensor_tensor(out=RC[:, k, 0:N], in0=W[:, k * N:(k + 1) * N],
                                                       scalar=col(("bq", "bqs")[k]), in1=K[:, o + at:o + at + N],
                                                       op0=ALU.add, op1=ALU.mult) for k, o in enumerate((K_CQ, K_SQ))])
                    dve.tensor_tensor(Q1[:, at:at + N], RC[:, 0, 0:N], RC[:, 1, 0:N], ALU.add).then_inc(q1_ready, 1)
                elif kind == "a4":
                    w = W[:, :].rearrange("p (k c) -> p k c", k=2)[:, :, 0:4 * C].rearrange("p k (h c) -> p k h c", c=C)
                    s = (n - 1) % 3
                    mx = mx1[:, s, :].rearrange("p (k h) -> p k h", k=2)
                    link(dve.tensor_reduce(mx, w, AX.X, ALU.max))
                    if n > 3:
                        dve.wait_ge(p1_turned, n - 3)
                    dve.tensor_tensor(S1[:, s, 0:HH * C].rearrange("p (k h c) -> p k h c", k=2, c=C), w,
                                      mx.unsqueeze(3).broadcast_to([P, 2, 4, C]), ALU.subtract).then_inc(shifted, 1)
                elif kind == "m3":
                    r, tiles = part_tiles(item), range(part_tiles(item).start, part_tiles(item).stop)
                    wv = W[:, 0:TP * 256].rearrange("p (t c) -> p t c", t=TP)
                    dve.tensor_copy(lg[:, r, :], wv[:, :, 2 * F1:2 * F1 + E1]).then_inc(logits_copied, 1)
                    dve.wait_ge(logits_copied, n)
                    link_all([dve.max(top[:, m, :], lg[:, m, :]) for m in tiles])
                    link_all([dve.max_index(idx[:, m, :], top[:, m, :], lg[:, m, :])
                              for m in tiles])
                    dve.tensor_tensor(lg[:, r, :], lg[:, r, :], top[:, r, 0:1].broadcast_to([P, TP, E1]),
                                      ALU.subtract).then_inc(logits_ready, 1)
                elif kind == "m2":
                    m = b * QT + item[2]
                    dve.wait_ge(gate_tanh, n)
                    link(dve.scalar_tensor_tensor(out=HM[:, m % QT, 0:MH], in0=HB[:, (n - 1) % 2, :], scalar=1.0,
                                                  in1=W[:, 0:MH], op0=ALU.add, op1=ALU.mult))
                    dve.tensor_tensor(HM[:, m % QT, 0:MH], HM[:, m % QT, 0:MH], W[:, MH:2 * MH], ALU.mult).then_inc(hid_ready, 1)

            def second(item):
                kind, b = item[0], item[1]
                W, n = slot(item), upto(item)
                if kind == "x0" and b == 0:
                    dve.wait_ge(rstd_ready[0], 2)
                    for m in range(QT, NT):
                        normalise(0, X, m, XN[:, m, :], xn_ready[0])
                    dve.wait_ge(ld["const"], 16)
                    dve.tensor_copy(identb[:], ident).then_inc(identb_ready, 1)
                elif kind == "o":
                    dve.wait_ge(front_done, NTH[item] + 1)
                    dve.wait_ge(rec_ready, n)
                    dve.wait_ge(o_added, n - n // H0)
                    for t in range(QT):
                        m = b * QT + t
                        dve.scalar_tensor_tensor(out=X1[:, m, :], in0=W[:, t * D:(t + 1) * D],
                                                 scalar=rec0[:, b, item[2], t:t + 1], in1=X1[:, m, :],
                                                 op0=ALU.mult, op1=ALU.add).then_inc(x1_ready, 1)
                    dve.wait_ge(x1_ready, QT * (b + 1))
                    r = slice(b * QT, (b + 1) * QT)
                    all_stats(1, X1, r)
                    variance(1, r)
                elif kind == "k" and n == 3:
                    dve.wait_ge(ld["ffn"], 32)
                    dve.tensor_reduce(ws[:, 0, 0:1], W1[:], AX.X, ALU.add,
                                      apply_absolute_value=True).then_inc(wsum_ready, 1)
                    dve.tensor_reduce(ws[:, 0, 1:2], W2[:].rearrange("p c d -> p (c d)"), AX.X, ALU.add,
                                      apply_absolute_value=True).then_inc(wsum_ready, 1)
                elif kind == "u":
                    dve.wait_ge(pt_upper, n)
                    qt, s = item[3], (n - 1) // 2 % 2
                    cols2 = slice(qt % 2 * P, (qt % 2 + 1) * P)
                    dve.tensor_tensor(PL[:, s, :, cols2], W[:, 0:KP].rearrange("p (c q) -> p c q", c=5),
                                      PH[:, s, :, cols2].bitcast(F32), ALU.subtract).then_inc(pt_ready, 1)
                elif kind == "f2":
                    c = item[2]
                    dve.wait_ge(tanh_done, n)
                    dve.scalar_tensor_tensor(out=YC[:, c, :], in0=TH[:, (n - 1) % 2, :], scalar=1.0,
                                             in1=YC[:, c, :], op0=ALU.add, op1=ALU.mult).then_inc(silu_ready, 1)
                elif kind == "f3":
                    dve.wait_ge(rounded, n)
                    if n > 4:
                        dve.wait_ge(qbt_ready, n - 4)
                    dve.tensor_scalar(QB[:, (n - 1) % 4, :], QM[:, (n - 1) % 2, :], MAGIC, None,
                                      ALU.subtract).then_inc(qb_ready, 1)
                elif kind == "f4":
                    m = b * QT + item[2]
                    dve.wait_ge(f_done, n)
                    dve.scalar_tensor_tensor(out=X2[:, m, :], in0=W[:, 2 * P:2 * P + D], scalar=aq2[:, m, 3:4],
                                             in1=X1[:, m, :], op0=ALU.mult, op1=ALU.add).then_inc(x2_ready, 1)
                    dve.wait_ge(x2_ready, n)
                    link(stats(2, X2, m))
                    if item[2] % TP == TP - 1:
                        variance(2, slice(m + 1 - TP, m + 1))
                elif kind == "m3":
                    r, local = part_tiles(item), slice(item[2] * TP, (item[2] + 1) * TP)
                    wv = W[:, 0:TP * 256].rearrange("p (t c) -> p t c", t=TP)
                    link(dve.tensor_copy(idf[:, r, 0:2], idx[:, r, 0:2]))
                    iota = K[:, K_IOTA:K_IOTA + E1].unsqueeze(1).broadcast_to([P, TP, E1])
                    link_all([dve.tensor_tensor(hot[:, r, k, :], iota, idf[:, r, k:k + 1].broadcast_to([P, TP, E1]),
                                                ALU.is_equal) for k in range(2)])
                    link(dve.tensor_tensor(hot[:, r, 0, :], hot[:, r, 0, :], hot[:, r, 1, :], ALU.add))
                    dve.wait_ge(shared_tanh, n)
                    sh = HM[:, local, MH:MT]
                    link(dve.scalar_tensor_tensor(out=sh, in0=SHT[:, local, :], scalar=1.0, in1=wv[:, :, 0:F1],
                                                  op0=ALU.add, op1=ALU.mult))
                    link(dve.scalar_tensor_tensor(out=sh, in0=sh, scalar=0.5, in1=wv[:, :, F1:2 * F1],
                                                  op0=ALU.mult, op1=ALU.mult))
                    dve.wait_ge(exps_ready, n)
                    link(dve.tensor_reduce(rt[:, r, 0], lg[:, r, :], AX.X, ALU.add))
                    link(dve.reciprocal(rt[:, r, 1], rt[:, r, 0]))
                    link(dve.scalar_tensor_tensor(out=cwt[:, r, :], in0=lg[:, r, :], scalar=0.5, in1=hot[:, r, 0, :],
                                                  op0=ALU.mult, op1=ALU.mult))
                    dve.tensor_tensor(cwt[:, r, :], cwt[:, r, :], rt[:, r, 1:2].broadcast_to([P, TP, E1]),
                                      ALU.mult).then_inc(weights_ready, 1)
                    dve.wait_ge(weights_ready, n)
                    dve.sem_inc(shared_ready, 1)
                elif kind == "a6":
                    r = part_tiles(item)
                    dve.wait_ge(ya_done, n)
                    dve.scalar_tensor_tensor(out=X3[:, r, :], in0=W[:, N:N + TP * D].rearrange("p (t d) -> p t d", t=TP),
                                             scalar=tg[:, 1:2], in1=X2[:, r, :], op0=ALU.mult,
                                             op1=ALU.add).then_inc(x3_ready, 1)
                    dve.wait_ge(x3_ready, n)
                    all_stats(3, X3, r)
                    variance(3, r)
                elif kind == "m4":
                    m = b * QT + item[2]
                    dve.wait_ge(ym_done, n)
                    dve.scalar_tensor_tensor(out=Y[:, m, :], in0=W[:, 640:640 + D], scalar=tg[:, 3:4],
                                             in1=X3[:, m, :], op0=ALU.mult, op1=ALU.add).then_inc(y_ready, 1)

            def third(item):
                kind, b = item[0], item[1]
                n = upto(item)
                tiles = range(b * QT, (b + 1) * QT)
                r = slice(b * QT, (b + 1) * QT)
                if kind == "o" and item[2] == H0 - 1:
                    dve.wait_ge(rstd_ready[1], b + 1)
                    link_all([dve.tensor_scalar(XN[:, m, :], X1[:, m, :], mvx[:, 1, m, 0:1], vex[:, 1, m:m + 1],
                                                ALU.subtract, ALU.mult) for m in tiles])
                    xn = XN[:, r, :]
                    link(dve.tensor_reduce(aq[:, r, 0], xn, AX.X, ALU.max, apply_absolute_value=True))
                    link(dve.tensor_scalar(aq[:, r, 3], aq[:, r, 0], 1e-5, 1.0 / 127, ALU.max, ALU.mult))
                    link(dve.reciprocal(aq[:, r, 2], aq[:, r, 3]))
                    link_all([dve.tensor_scalar(XN[:, m, :], XN[:, m, :], aq[:, m, 2:3], MAGIC,
                                                ALU.mult, ALU.add) for m in tiles])
                    for m in tiles:
                        dve.tensor_scalar(XN[:, m, :], XN[:, m, :], MAGIC, aq[:, m, 3:4],
                                          ALU.subtract, ALU.mult).then_inc(xn_ready[1], 1)
                elif kind == "f4":
                    dve.wait_ge(rstd_ready[2], n // TP)
                    for m in range(n - TP, n):
                        normalise(2, X2, m, XN[:, m, :], xn_ready[2])
                elif kind == "a4":
                    m, h = b * QT + item[2], item[3]
                    dve.wait_ge(pv1_done, n)
                    o = slot(item)[:, KP1:KP1 + HH * (DH1 + 1)].rearrange("p (h d) -> p h d", h=HH)
                    rec = rec1[:, m, h * HH:(h + 1) * HH]
                    link(dve.reciprocal(rec, o[:, :, DH1]))
                    dve.tensor_tensor(A1[:, item[2], h * HH * DH1:(h + 1) * HH * DH1].rearrange("p (h d) -> p h d", h=HH),
                                      o[:, :, 0:DH1], rec.unsqueeze(2).broadcast_to([P, HH, DH1]),
                                      ALU.mult).then_inc(a1_ready, 1)
                elif kind == "a6":
                    dve.wait_ge(rstd_ready[3], n)
                    for m in range(part_tiles(item).start, part_tiles(item).stop):
                        normalise(3, X3, m, XN[:, m, :], xn_ready[3])

            walk("DVE", {"D1": first, "D2": second, "D3": third})


def constants():
    k = np.zeros((P, NCONST), np.float32)
    k[:, K_ID:K_ID + P] = np.eye(P)
    k[:, K_ONE:K_ONE + P] = 1.0
    k[:, K_IOTA:K_IOTA + E1] = np.arange(E1)
    key = np.arange(KP1).reshape(KC1, P).T[:, :, None]
    k[:, K_BLOCK:K_BLOCK + KC1 * HH] = (key // C == np.arange(HH)).reshape(P, KC1 * HH)
    k[:, K_MASK:K_MASK + H1] = np.arange(P)[:, None] // DH1 == np.arange(H1)[None]
    inv_freq = (1.0 / 10000.0 ** (np.arange(0, DH1, 2, dtype=np.float32) / np.float32(DH1))).astype(np.float32)
    half = DH1 // 2
    row = np.arange(P) % DH1
    sign = np.where(row < half, -1.0, 1.0).astype(np.float32)[:, None]
    for n, cos, sin in ((S, K_CQ, K_SQ), (C, K_CK, K_SK)):
        t = np.arange(n, dtype=np.float32) / np.float32(n)
        angle = ((np.float32(10.0) * t)[None, :] * inv_freq[row % half][:, None]).astype(np.float32)
        k[:, cos:cos + n] = np.cos(angle)
        k[:, sin:sin + n] = np.sin(angle) * sign
    return k


def kernel(**inputs):
    import concourse.bacc as bacc
    from concourse.bass_utils import run_bass_kernel_spmd

    a = {n: np.asarray(v) for n, v in inputs.items()}
    swap = np.arange(P) // DH1 * DH1 + (np.arange(P) + DH1 // 2) % DH1
    l1 = {n: a[f"L1_xattn_{n}"] for n in ("Wq", "Wk", "Wv", "Wo", "bq", "bk", "bv", "bo")}
    row = {"gl": a["L0_xattn_gl"], "bl": a["L0_xattn_bl"], "gm": a["L0_xattn_gm"], "bm": a["L0_xattn_bm"],
           "bq": l1["bq"], "bqs": l1["bq"][swap], "bk": l1["bk"], "bks": l1["bk"][swap], "bv": l1["bv"]}
    for n, src, i in (("gx0", "g_xattn", 0), ("gx1", "g_xattn", 1), ("gf0", "g_ffn", 0), ("gf1", "g_ffn", 1)):
        row[n] = np.broadcast_to(a[src][i], (P,))
    cols = np.concatenate([
        np.stack([row[n] for n in COLS], 1),
        a["L0_ffn_conv_w"].reshape(HC, P, 3).transpose(1, 0, 2).reshape(P, 3 * HC),
        a["L0_ffn_conv_b"].reshape(HC, P).T,
        np.full((P, 1), MAGIC, np.float32)], 1)
    ffn = {n: a[f"L1_ffn_{n}"] for n in ("gate_w", "wg", "wu", "wd", "sg", "su", "sd")}
    arrays = {
        "x": a["x"].reshape(NT * P, D), "ctx": a["ctx_1024"].reshape(B * C, D),
        "ctxT": np.tile(a["ctx_1024"].transpose(2, 0, 1), (1, 1, HH + 1))[:, :, :KP1].reshape(D, B * KP1), "cols": cols,
        "wq": a["L0_xattn_Wq"],
        "wk": np.repeat(a["L0_xattn_Wkv"][:, :IN0].reshape(D, H0, 1, DH0), 2, 2).reshape(D, H0 * P),
        "wv": a["L0_xattn_Wkv"][:, IN0:],
        "wout": np.repeat(a["L0_xattn_Wout"].reshape(H0, 1, DH0, D), 2, 1).reshape(H0 * P, D),
        "w1T": a["L0_ffn_w1"].T, "w2T": a["L0_ffn_w2"].T,
        "l1w": np.concatenate([l1["Wq"].T, l1["Wq"][swap].T, l1["Wk"].T, l1["Wk"][swap].T,
                               l1["Wv"].T, l1["Wo"].T], 1),
        "bo": l1["bo"].reshape(1, D),
        "wgu": np.concatenate([ffn["wg"].reshape(MH, D).T, ffn["wu"].reshape(MH, D).T,
                               ffn["sg"].T, ffn["su"].T, ffn["gate_w"].T], 1),
        "wdT": np.concatenate([ffn["wd"].transpose(0, 2, 1).reshape(MH, D), ffn["sd"].T,
                               np.zeros((P - F1, D), np.float32)], 0),
        "const": constants(),
    }
    arrays = {f"in_{n}": np.ascontiguousarray(v) for n, v in arrays.items()}
    nc = bacc.Bacc("TRN2", target_bir_lowering=False, num_devices=1)
    args = [nc.dram_tensor(n, v.shape, mybir.dt.from_np(v.dtype), kind="ExternalInput").ap()
            for n, v in arrays.items()]
    args.append(nc.dram_tensor("out_0", (NT * P, D), F32, kind="ExternalOutput").ap())
    mega_kernel(nc, *args)
    r = run_bass_kernel_spmd(nc, [arrays], core_ids=[0])
    return r.results[0]["out_0"].reshape(B, S, D)
```
